# Optimizing a Trainium2 kernel written in Bass

```python
import numpy as np
import jax
import jax.numpy as jnp

def _softmax(x, axis=-1):
    return jax.nn.softmax(x, axis=axis)

def _gelu(x):
    return jax.nn.gelu(x, approximate=True)

def _silu(x):
    return jax.nn.silu(x)

def _sigmoid(x):
    return jax.nn.sigmoid(x)

def _layernorm(x, axis=-1, eps=1e-05):
    m = jnp.mean(x, axis=axis, keepdims=True)
    v = jnp.var(x, axis=axis, keepdims=True)
    return (x - m) / jnp.sqrt(v + eps)

def _scatter_add(tgt, idx, src, axis=0):
    return tgt.at[idx].add(src)

def _segment_sum(src, seg, n):
    return jax.ops.segment_sum(src, seg, n)
kernel_name = 'mk_gnn_resnorm_d4_gnn_r32_4066aa'

def setup_inputs(seed: int=0):
    np.random.seed(seed)
    _w = jnp.asarray

    def _rec_inputs():
        import jax
        import jax.numpy as jnp
        _gk = jax.random.key(seed)
        x = -0.0003713 + 1 * jax.random.normal(jax.random.fold_in(_gk, 1), (3125, 128), jnp.float32)
        _s = jax.random.randint(jax.random.fold_in(_gk, 2), (50000,), 0, 3125, jnp.int32)
        _d = jax.random.randint(jax.random.fold_in(_gk, 3), (50000,), 0, 3125, jnp.int32)
        _loop = jnp.arange(3125, dtype=jnp.int32)
        src = jnp.concatenate([_s, _d, _loop])
        dst = jnp.concatenate([_d, _s, _loop])
        _o = jnp.argsort(dst, stable=True)
        src = src[_o]
        dst = dst[_o]
        edge_attr_10 = jax.random.uniform(jax.random.fold_in(_gk, 12), (103125, 10), jnp.float32, 0.0, 1)
        edge_attr_4 = 0.00121237 + 1.00026 * jax.random.normal(jax.random.fold_in(_gk, 13), (103125, 4), jnp.float32)
        edge_weight = jax.random.uniform(jax.random.fold_in(_gk, 15), (103125,), jnp.float32, 0.0, 1)
        node_vec1 = jax.random.uniform(jax.random.fold_in(_gk, 16), (3125, 1), jnp.float32, 0.0, 1)
        return (x, src, dst, edge_attr_10, edge_attr_4, edge_weight, node_vec1)
    x, src, dst, edge_attr_10, edge_attr_4, edge_weight, node_vec1 = _rec_inputs()

    def _L0_gnn_setup():
        import jax, jax.numpy as jnp
        import numpy as np
        N = 3125
        E = 50000
        D_IN = 128
        D_H = 128
        D_OUT = 128
        key = jax.random.key(seed)
        ks = jax.random.split(key, 11)
        x = jax.random.normal(ks[0], (N, D_IN), dtype=jnp.float32)
        edge_index = jax.random.randint(ks[1], (2, E), 0, N, dtype=jnp.int32)
        s_in = 1.0 / np.sqrt(D_IN)
        s_h = 1.0 / np.sqrt(D_H)
        return {'x': x, 'edge_index': edge_index, 'W_neigh1': jax.random.uniform(ks[2], (D_H, D_IN), jnp.float32, -s_in, s_in), 'b_neigh1': jax.random.uniform(ks[3], (D_H,), jnp.float32, -s_in, s_in), 'W_self1': jax.random.uniform(ks[4], (D_H, D_IN), jnp.float32, -s_in, s_in), 'b_self1': jax.random.uniform(ks[5], (D_H,), jnp.float32, -s_in, s_in), 'W_neigh2': jax.random.uniform(ks[6], (D_OUT, D_H), jnp.float32, -s_h, s_h), 'b_neigh2': jax.random.uniform(ks[7], (D_OUT,), jnp.float32, -s_h, s_h), 'W_self2': jax.random.uniform(ks[8], (D_OUT, D_H), jnp.float32, -s_h, s_h), 'b_self2': jax.random.uniform(ks[9], (D_OUT,), jnp.float32, -s_h, s_h)}
    _L0_gnn_all = _L0_gnn_setup()
    _L0_gnn_in = {k: v for k, v in _L0_gnn_all.items() if k in ('W_neigh1', 'b_neigh1', 'W_self1', 'b_self1', 'W_neigh2', 'b_neigh2', 'W_self2', 'b_self2')}
    del _L0_gnn_all

    def _L1_gnn_setup():
        import jax, jax.numpy as jnp
        import numpy as np
        N, E, D_IN, H1, H2 = (50000, 25000, 128, 128, 64)

        def _gcn_conv(x, W, b, src, dst, dinv):
            h = x @ W
            coef = dinv[src] * dinv[dst]
            agg = jax.ops.segment_sum(h[src] * coef[:, None], dst, num_segments=x.shape[0])
            agg = agg + h * (dinv * dinv)[:, None]
            return agg + b
        key = jax.random.key(seed)
        ks = jax.random.split(key, 10)
        x = jax.random.normal(ks[0], (N, D_IN), dtype=jnp.float32)
        edge_index = jax.random.randint(ks[1], (2, E), 0, N, dtype=jnp.int64)

        def lin(k, fan_in, fan_out):
            return jax.random.normal(k, (fan_in, fan_out), dtype=jnp.float32) / np.sqrt(fan_in).astype(np.float32)
        return {'x': x, 'W1': lin(ks[2], D_IN, H1), 'b1': jnp.zeros((H1,), jnp.float32), 'W2': lin(ks[3], H1, H2), 'b2': jnp.zeros((H2,), jnp.float32), 'W3': lin(ks[4], H2, H1), 'b3': jnp.zeros((H1,), jnp.float32), 'W4': lin(ks[5], H1, D_IN), 'b4': jnp.zeros((D_IN,), jnp.float32), 'edge_index': edge_index}
    _L1_gnn_all = _L1_gnn_setup()
    _L1_gnn_in = {k: v for k, v in _L1_gnn_all.items() if k in ('W1', 'b1', 'W2', 'b2', 'W3', 'b3', 'W4', 'b4')}
    del _L1_gnn_all

    def _L2_gnn_setup():
        import jax, jax.numpy as jnp
        import numpy as np
        N, E, MUL = (50000, 12500, 32)
        SQ3 = float(np.sqrt(3.0))
        key = jax.random.key(seed)
        ks = jax.random.split(key, 16)
        rn = lambda k, s: jax.random.normal(k, s, dtype=jnp.float32)
        return {'x': rn(ks[0], (N, 4 * MUL)), 'node_attr': jnp.ones((N, 1), jnp.float32), 'edge_src': jax.random.randint(ks[1], (E,), 0, N), 'edge_dst': jax.random.randint(ks[2], (E,), 0, N), 'edge_sh': rn(ks[3], (E, 4)), 'edge_scalars': jax.random.uniform(ks[4], (E, 10), dtype=jnp.float32), 'W_fc1': rn(ks[5], (10, 100)), 'W_fc2': rn(ks[6], (100, 4 * MUL)), 'W_sc0': rn(ks[7], (MUL, MUL)), 'W_sc1': rn(ks[8], (MUL, MUL)), 'W_l1_0': rn(ks[9], (MUL, MUL)), 'W_l1_1': rn(ks[10], (MUL, MUL)), 'W_l2_0': rn(ks[11], (2 * MUL, MUL)), 'W_l2_1': rn(ks[12], (2 * MUL, MUL)), 'W_alpha': rn(ks[13], (2 * MUL, 1))}
    _L2_gnn_all = _L2_gnn_setup()
    _L2_gnn_in = {k: v for k, v in _L2_gnn_all.items() if k in ('W_fc1', 'W_fc2', 'W_sc0', 'W_sc1', 'W_l1_0', 'W_l1_1', 'W_l2_0', 'W_l2_1', 'W_alpha')}
    del _L2_gnn_all

    def _L3_gnn_setup():
        import jax, jax.numpy as jnp
        import numpy as np
        N, F_IN, H, HEADS = (50000, 128, 128, 4)
        C = H // HEADS
        E = 25000

        def layer_norm(x, w, b, eps=1e-05):
            mu = x.mean(-1, keepdims=True)
            var = ((x - mu) ** 2).mean(-1, keepdims=True)
            return (x - mu) * jax.lax.rsqrt(var + eps) * w + b

        def gat_conv(x, src, dst, edge_attr, W, att_src, att_dst, W_edge, att_edge, bias):
            n = x.shape[0]
            ones = jnp.ones((src.shape[0],), dtype=edge_attr.dtype)
            deg = jax.ops.segment_sum(ones, dst, n)
            loop_attr = jax.ops.segment_sum(edge_attr, dst, n) / jnp.maximum(deg, 1.0)[:, None]
            loop = jnp.arange(n, dtype=src.dtype)
            src = jnp.concatenate([src, loop])
            dst = jnp.concatenate([dst, loop])
            ea = jnp.concatenate([edge_attr, loop_attr], axis=0)
            h = (x @ W).reshape(n, HEADS, C)
            a_src = (h * att_src).sum(-1)
            a_dst = (h * att_dst).sum(-1)
            e = (ea @ W_edge).reshape(-1, HEADS, C)
            a_edge = (e * att_edge).sum(-1)
            alpha = jax.nn.leaky_relu(a_src[src] + a_dst[dst] + a_edge, 0.2)
            m = jax.lax.stop_gradient(jax.ops.segment_max(alpha, dst, n))
            alpha = jnp.exp(alpha - m[dst])
            s = jax.ops.segment_sum(alpha, dst, n)
            alpha = alpha / (s[dst] + 1e-16)
            out = jax.ops.segment_sum(alpha[:, :, None] * h[src], dst, n)
            return out.reshape(n, H) + bias
        key = jax.random.key(seed)
        ks = iter(jax.random.split(key, 40))

        def lin(k, i, o, s=0.05):
            return jax.random.normal(k, (i, o), jnp.float32) * s
        d = {}
        d['x'] = jax.random.normal(next(ks), (N, F_IN), jnp.float32)
        d['edge_time'] = jax.random.uniform(next(ks), (E,), jnp.float32)
        d['ip_w1'] = lin(next(ks), F_IN, 2 * H)
        d['ip_b1'] = jnp.zeros((2 * H,), jnp.float32)
        d['ip_ln_w'] = jnp.ones((2 * H,), jnp.float32)
        d['ip_ln_b'] = jnp.zeros((2 * H,), jnp.float32)
        d['ip_w2'] = lin(next(ks), 2 * H, H)
        d['ip_b2'] = jnp.zeros((H,), jnp.float32)
        d['pn_w'] = jnp.ones((H,), jnp.float32)
        d['pn_b'] = jnp.zeros((H,), jnp.float32)
        d['ta_w1'] = lin(next(ks), 1, H)
        d['ta_b1'] = jnp.zeros((H,), jnp.float32)
        d['ta_ln_w'] = jnp.ones((H,), jnp.float32)
        d['ta_ln_b'] = jnp.zeros((H,), jnp.float32)
        d['ta_w2'] = lin(next(ks), H, H)
        d['ta_b2'] = jnp.zeros((H,), jnp.float32)
        for p in ('g1', 'g2'):
            d[p + '_w'] = lin(next(ks), H, H)
            d[p + '_att_src'] = jax.random.normal(next(ks), (HEADS, C), jnp.float32) * 0.05
            d[p + '_att_dst'] = jax.random.normal(next(ks), (HEADS, C), jnp.float32) * 0.05
            d[p + '_ew'] = lin(next(ks), H, H)
            d[p + '_att_edge'] = jax.random.normal(next(ks), (HEADS, C), jnp.float32) * 0.05
            d[p + '_b'] = jnp.zeros((H,), jnp.float32)
        d['n1_w'] = jnp.ones((H,), jnp.float32)
        d['n1_b'] = jnp.zeros((H,), jnp.float32)
        d['n2_w'] = jnp.ones((H,), jnp.float32)
        d['n2_b'] = jnp.zeros((H,), jnp.float32)
        d['edge_index'] = jax.random.randint(next(ks), (2, E), 0, N, jnp.int32)
        return d
    _L3_gnn_all = _L3_gnn_setup()
    _L3_gnn_in = {k: v for k, v in _L3_gnn_all.items() if k in ('ip_w1', 'ip_b1', 'ip_ln_w', 'ip_ln_b', 'ip_w2', 'ip_b2', 'pn_w', 'pn_b', 'ta_w1', 'ta_b1', 'ta_ln_w', 'ta_ln_b', 'ta_w2', 'ta_b2', 'g1_w', 'g1_att_src', 'g1_att_dst', 'g1_ew', 'g1_att_edge', 'g1_b', 'g2_w', 'g2_att_src', 'g2_att_dst', 'g2_ew', 'g2_att_edge', 'g2_b', 'n1_w', 'n1_b', 'n2_w', 'n2_b')}
    del _L3_gnn_all
    return {'x': x, 'src': src, 'dst': dst, 'edge_attr_10': edge_attr_10, 'edge_attr_4': edge_attr_4, 'edge_weight': edge_weight, 'node_vec1': node_vec1, 'L0_gnn_W_neigh1': _L0_gnn_in['W_neigh1'], 'L0_gnn_b_neigh1': _L0_gnn_in['b_neigh1'], 'L0_gnn_W_self1': _L0_gnn_in['W_self1'], 'L0_gnn_b_self1': _L0_gnn_in['b_self1'], 'L0_gnn_W_neigh2': _L0_gnn_in['W_neigh2'], 'L0_gnn_b_neigh2': _L0_gnn_in['b_neigh2'], 'L0_gnn_W_self2': _L0_gnn_in['W_self2'], 'L0_gnn_b_self2': _L0_gnn_in['b_self2'], 'L1_gnn_W1': _L1_gnn_in['W1'], 'L1_gnn_b1': _L1_gnn_in['b1'], 'L1_gnn_W2': _L1_gnn_in['W2'], 'L1_gnn_b2': _L1_gnn_in['b2'], 'L1_gnn_W3': _L1_gnn_in['W3'], 'L1_gnn_b3': _L1_gnn_in['b3'], 'L1_gnn_W4': _L1_gnn_in['W4'], 'L1_gnn_b4': _L1_gnn_in['b4'], 'L2_gnn_W_fc1': _L2_gnn_in['W_fc1'], 'L2_gnn_W_fc2': _L2_gnn_in['W_fc2'], 'L2_gnn_W_sc0': _L2_gnn_in['W_sc0'], 'L2_gnn_W_sc1': _L2_gnn_in['W_sc1'], 'L2_gnn_W_l1_0': _L2_gnn_in['W_l1_0'], 'L2_gnn_W_l1_1': _L2_gnn_in['W_l1_1'], 'L2_gnn_W_l2_0': _L2_gnn_in['W_l2_0'], 'L2_gnn_W_l2_1': _L2_gnn_in['W_l2_1'], 'L2_gnn_W_alpha': _L2_gnn_in['W_alpha'], 'L3_gnn_ip_w1': _L3_gnn_in['ip_w1'], 'L3_gnn_ip_b1': _L3_gnn_in['ip_b1'], 'L3_gnn_ip_ln_w': _L3_gnn_in['ip_ln_w'], 'L3_gnn_ip_ln_b': _L3_gnn_in['ip_ln_b'], 'L3_gnn_ip_w2': _L3_gnn_in['ip_w2'], 'L3_gnn_ip_b2': _L3_gnn_in['ip_b2'], 'L3_gnn_pn_w': _L3_gnn_in['pn_w'], 'L3_gnn_pn_b': _L3_gnn_in['pn_b'], 'L3_gnn_ta_w1': _L3_gnn_in['ta_w1'], 'L3_gnn_ta_b1': _L3_gnn_in['ta_b1'], 'L3_gnn_ta_ln_w': _L3_gnn_in['ta_ln_w'], 'L3_gnn_ta_ln_b': _L3_gnn_in['ta_ln_b'], 'L3_gnn_ta_w2': _L3_gnn_in['ta_w2'], 'L3_gnn_ta_b2': _L3_gnn_in['ta_b2'], 'L3_gnn_g1_w': _L3_gnn_in['g1_w'], 'L3_gnn_g1_att_src': _L3_gnn_in['g1_att_src'], 'L3_gnn_g1_att_dst': _L3_gnn_in['g1_att_dst'], 'L3_gnn_g1_ew': _L3_gnn_in['g1_ew'], 'L3_gnn_g1_att_edge': _L3_gnn_in['g1_att_edge'], 'L3_gnn_g1_b': _L3_gnn_in['g1_b'], 'L3_gnn_g2_w': _L3_gnn_in['g2_w'], 'L3_gnn_g2_att_src': _L3_gnn_in['g2_att_src'], 'L3_gnn_g2_att_dst': _L3_gnn_in['g2_att_dst'], 'L3_gnn_g2_ew': _L3_gnn_in['g2_ew'], 'L3_gnn_g2_att_edge': _L3_gnn_in['g2_att_edge'], 'L3_gnn_g2_b': _L3_gnn_in['g2_b'], 'L3_gnn_n1_w': _L3_gnn_in['n1_w'], 'L3_gnn_n1_b': _L3_gnn_in['n1_b'], 'L3_gnn_n2_w': _L3_gnn_in['n2_w'], 'L3_gnn_n2_b': _L3_gnn_in['n2_b']}

def reference(x, src, dst, edge_attr_10, edge_attr_4, edge_weight, node_vec1, L0_gnn_W_neigh1, L0_gnn_b_neigh1, L0_gnn_W_self1, L0_gnn_b_self1, L0_gnn_W_neigh2, L0_gnn_b_neigh2, L0_gnn_W_self2, L0_gnn_b_self2, L1_gnn_W1, L1_gnn_b1, L1_gnn_W2, L1_gnn_b2, L1_gnn_W3, L1_gnn_b3, L1_gnn_W4, L1_gnn_b4, L2_gnn_W_fc1, L2_gnn_W_fc2, L2_gnn_W_sc0, L2_gnn_W_sc1, L2_gnn_W_l1_0, L2_gnn_W_l1_1, L2_gnn_W_l2_0, L2_gnn_W_l2_1, L2_gnn_W_alpha, L3_gnn_ip_w1, L3_gnn_ip_b1, L3_gnn_ip_ln_w, L3_gnn_ip_ln_b, L3_gnn_ip_w2, L3_gnn_ip_b2, L3_gnn_pn_w, L3_gnn_pn_b, L3_gnn_ta_w1, L3_gnn_ta_b1, L3_gnn_ta_ln_w, L3_gnn_ta_ln_b, L3_gnn_ta_w2, L3_gnn_ta_b2, L3_gnn_g1_w, L3_gnn_g1_att_src, L3_gnn_g1_att_dst, L3_gnn_g1_ew, L3_gnn_g1_att_edge, L3_gnn_g1_b, L3_gnn_g2_w, L3_gnn_g2_att_src, L3_gnn_g2_att_dst, L3_gnn_g2_ew, L3_gnn_g2_att_edge, L3_gnn_g2_b, L3_gnn_n1_w, L3_gnn_n1_b, L3_gnn_n2_w, L3_gnn_n2_b):
    import jax
    import jax.numpy as jnp

    def _L0_gnn_ref(x, edge_index, W_neigh1, b_neigh1, W_self1, b_self1, W_neigh2, b_neigh2, W_self2, b_self2):
        import jax, jax.numpy as jnp
        import numpy as np
        N = 3125
        E = 50000
        D_IN = 128
        D_H = 128
        D_OUT = 128
        src, dst = (edge_index[0], edge_index[1])
        n = x.shape[0]
        deg = jax.ops.segment_sum(jnp.ones(src.shape[0], x.dtype), dst, num_segments=n)
        inv_deg = 1.0 / jnp.maximum(deg, 1.0)

        def agg(h):
            return jax.ops.segment_sum(h[src], dst, num_segments=n) * inv_deg[:, None]
        h1 = agg(x) @ W_neigh1.T + b_neigh1 + x @ W_self1.T + b_self1
        h1 = jax.nn.relu(h1)
        h2 = agg(h1) @ W_neigh2.T + b_neigh2 + h1 @ W_self2.T + b_self2
        return h2

    def _L1_gnn_ref(x, W1, b1, W2, b2, W3, b3, W4, b4, edge_index):
        import jax, jax.numpy as jnp
        import numpy as np
        N, E, D_IN, H1, H2 = (50000, 25000, 128, 128, 64)

        def _gcn_conv(x, W, b, src, dst, dinv):
            h = x @ W
            coef = dinv[src] * dinv[dst]
            agg = jax.ops.segment_sum(h[src] * coef[:, None], dst, num_segments=x.shape[0])
            agg = agg + h * (dinv * dinv)[:, None]
            return agg + b
        src, dst = (edge_index[0], edge_index[1])
        n = x.shape[0]
        deg = jax.ops.segment_sum(jnp.ones(src.shape, x.dtype), dst, num_segments=n) + 1.0
        dinv = jax.lax.rsqrt(deg)
        h = jax.nn.relu(_gcn_conv(x, W1, b1, src, dst, dinv))
        h = _gcn_conv(h, W2, b2, src, dst, dinv)
        h = jax.nn.relu(_gcn_conv(h, W3, b3, src, dst, dinv))
        h = _gcn_conv(h, W4, b4, src, dst, dinv)
        return h

    def _L2_gnn_ref(x, node_attr, edge_src, edge_dst, edge_sh, edge_scalars, W_fc1, W_fc2, W_sc0, W_sc1, W_l1_0, W_l1_1, W_l2_0, W_l2_1, W_alpha):
        import jax, jax.numpy as jnp
        import numpy as np
        N, E, MUL = (50000, 12500, 32)
        SQ3 = float(np.sqrt(3.0))
        n = x.shape[0]
        x0 = x[:, :MUL]
        x1 = x[:, MUL:].reshape(n, MUL, 3)
        a = node_attr
        inv = 1.0 / np.sqrt(MUL)
        inv2 = 1.0 / np.sqrt(2 * MUL)
        sc0 = x0 @ W_sc0 * inv * a
        sc1 = jnp.einsum('nuc,uv->nvc', x1, W_sc1) * inv * a[:, :, None]
        sc = jnp.concatenate([sc0, sc1.reshape(n, 3 * MUL)], axis=1)
        y0 = x0 @ W_l1_0 * inv * a
        y1 = jnp.einsum('nuc,uv->nvc', x1, W_l1_1) * inv * a[:, :, None]
        h = jax.nn.silu(edge_scalars @ W_fc1 / np.sqrt(10.0))
        w = h @ W_fc2 / np.sqrt(100.0)
        w00, w11 = (w[:, :MUL], w[:, MUL:2 * MUL])
        w01, w10 = (w[:, 2 * MUL:3 * MUL], w[:, 3 * MUL:])
        x0e = y0[edge_src]
        x1e = y1[edge_src]
        sh0 = edge_sh[:, :1]
        sh1 = edge_sh[:, 1:4]
        m00 = w00 * x0e * sh0
        m11 = w11 * jnp.einsum('euc,ec->eu', x1e, sh1) / SQ3
        m01 = w01[:, :, None] * x0e[:, :, None] * sh1[:, None, :]
        m10 = w10[:, :, None] * x1e * sh0[:, :, None]
        edge_feat = jnp.concatenate([m00, m11, m01.reshape(-1, 3 * MUL), m10.reshape(-1, 3 * MUL)], axis=1)
        sums = jax.ops.segment_sum(edge_feat, edge_dst, num_segments=n)
        cnt = jax.ops.segment_sum(jnp.ones((edge_feat.shape[0],), x.dtype), edge_dst, num_segments=n)
        mean = sums / jnp.maximum(cnt, 1.0)[:, None]
        mid0 = mean[:, :2 * MUL]
        mid1 = mean[:, 2 * MUL:].reshape(n, 2 * MUL, 3)
        alpha = mid0 @ W_alpha * inv2 * a
        c0 = mid0 @ W_l2_0 * inv2 * a
        c1 = jnp.einsum('nuc,uv->nvc', mid1, W_l2_1) * inv2 * a[:, :, None]
        conv = jnp.concatenate([c0, c1.reshape(n, 3 * MUL)], axis=1)
        return sc + alpha * conv

    def _L3_gnn_ref(x, edge_time, ip_w1, ip_b1, ip_ln_w, ip_ln_b, ip_w2, ip_b2, pn_w, pn_b, ta_w1, ta_b1, ta_ln_w, ta_ln_b, ta_w2, ta_b2, g1_w, g1_att_src, g1_att_dst, g1_ew, g1_att_edge, g1_b, g2_w, g2_att_src, g2_att_dst, g2_ew, g2_att_edge, g2_b, n1_w, n1_b, n2_w, n2_b, edge_index):
        import jax, jax.numpy as jnp
        import numpy as np
        N, F_IN, H, HEADS = (50000, 128, 128, 4)
        C = H // HEADS
        E = 25000

        def layer_norm(x, w, b, eps=1e-05):
            mu = x.mean(-1, keepdims=True)
            var = ((x - mu) ** 2).mean(-1, keepdims=True)
            return (x - mu) * jax.lax.rsqrt(var + eps) * w + b

        def gat_conv(x, src, dst, edge_attr, W, att_src, att_dst, W_edge, att_edge, bias):
            n = x.shape[0]
            ones = jnp.ones((src.shape[0],), dtype=edge_attr.dtype)
            deg = jax.ops.segment_sum(ones, dst, n)
            loop_attr = jax.ops.segment_sum(edge_attr, dst, n) / jnp.maximum(deg, 1.0)[:, None]
            loop = jnp.arange(n, dtype=src.dtype)
            src = jnp.concatenate([src, loop])
            dst = jnp.concatenate([dst, loop])
            ea = jnp.concatenate([edge_attr, loop_attr], axis=0)
            h = (x @ W).reshape(n, HEADS, C)
            a_src = (h * att_src).sum(-1)
            a_dst = (h * att_dst).sum(-1)
            e = (ea @ W_edge).reshape(-1, HEADS, C)
            a_edge = (e * att_edge).sum(-1)
            alpha = jax.nn.leaky_relu(a_src[src] + a_dst[dst] + a_edge, 0.2)
            m = jax.lax.stop_gradient(jax.ops.segment_max(alpha, dst, n))
            alpha = jnp.exp(alpha - m[dst])
            s = jax.ops.segment_sum(alpha, dst, n)
            alpha = alpha / (s[dst] + 1e-16)
            out = jax.ops.segment_sum(alpha[:, :, None] * h[src], dst, n)
            return out.reshape(n, H) + bias
        src, dst = (edge_index[0], edge_index[1])
        h = jax.nn.relu(x @ ip_w1 + ip_b1)
        h = layer_norm(h, ip_ln_w, ip_ln_b)
        h = h @ ip_w2 + ip_b2
        h = jnp.clip(jax.nn.relu(layer_norm(h, pn_w, pn_b)), -10.0, 10.0)
        tw = edge_time[:, None] @ ta_w1 + ta_b1
        tw = jax.nn.relu(layer_norm(tw, ta_ln_w, ta_ln_b))
        tw = jnp.clip(jnp.tanh(tw @ ta_w2 + ta_b2), -3.0, 3.0)
        g = gat_conv(h, src, dst, tw, g1_w, g1_att_src, g1_att_dst, g1_ew, g1_att_edge, g1_b) + h
        g = jax.nn.elu(layer_norm(jnp.clip(g, -10.0, 10.0), n1_w, n1_b))
        g2 = gat_conv(g, src, dst, tw, g2_w, g2_att_src, g2_att_dst, g2_ew, g2_att_edge, g2_b) + g
        return jax.nn.elu(layer_norm(jnp.clip(g2, -10.0, 10.0), n2_w, n2_b))
    edge_index = jnp.stack([src, dst])
    x = _layernorm(x + _L0_gnn_ref(x, edge_index, L0_gnn_W_neigh1, L0_gnn_b_neigh1, L0_gnn_W_self1, L0_gnn_b_self1, L0_gnn_W_neigh2, L0_gnn_b_neigh2, L0_gnn_W_self2, L0_gnn_b_self2), axis=-1)
    x = _layernorm(x + _L1_gnn_ref(x, L1_gnn_W1, L1_gnn_b1, L1_gnn_W2, L1_gnn_b2, L1_gnn_W3, L1_gnn_b3, L1_gnn_W4, L1_gnn_b4, edge_index), axis=-1)
    x = _layernorm(x + _L2_gnn_ref(x, node_vec1, src, dst, edge_attr_4, edge_attr_10, L2_gnn_W_fc1, L2_gnn_W_fc2, L2_gnn_W_sc0, L2_gnn_W_sc1, L2_gnn_W_l1_0, L2_gnn_W_l1_1, L2_gnn_W_l2_0, L2_gnn_W_l2_1, L2_gnn_W_alpha), axis=-1)
    x = _layernorm(x + _L3_gnn_ref(x, edge_weight, L3_gnn_ip_w1, L3_gnn_ip_b1, L3_gnn_ip_ln_w, L3_gnn_ip_ln_b, L3_gnn_ip_w2, L3_gnn_ip_b2, L3_gnn_pn_w, L3_gnn_pn_b, L3_gnn_ta_w1, L3_gnn_ta_b1, L3_gnn_ta_ln_w, L3_gnn_ta_ln_b, L3_gnn_ta_w2, L3_gnn_ta_b2, L3_gnn_g1_w, L3_gnn_g1_att_src, L3_gnn_g1_att_dst, L3_gnn_g1_ew, L3_gnn_g1_att_edge, L3_gnn_g1_b, L3_gnn_g2_w, L3_gnn_g2_att_src, L3_gnn_g2_att_dst, L3_gnn_g2_ew, L3_gnn_g2_att_edge, L3_gnn_g2_b, L3_gnn_n1_w, L3_gnn_n1_b, L3_gnn_n2_w, L3_gnn_n2_b, edge_index), axis=-1)
    return x

_drawn_inputs = setup_inputs


def setup_inputs(seed=0):
    import zlib

    import numpy as np

    out = dict(_drawn_inputs(seed))
    spreads = {'L1_gnn_b1': (0.0, 0.1),
     'L1_gnn_b2': (0.0, 0.1),
     'L1_gnn_b3': (0.0, 0.1),
     'L1_gnn_b4': (0.0, 0.1),
     'L3_gnn_ip_b1': (0.0, 0.1),
     'L3_gnn_ip_ln_w': (1.0, 0.2),
     'L3_gnn_ip_ln_b': (0.0, 0.1),
     'L3_gnn_ip_b2': (0.0, 0.1),
     'L3_gnn_pn_w': (1.0, 0.2),
     'L3_gnn_pn_b': (0.0, 0.1),
     'L3_gnn_ta_b1': (0.0, 0.8),
     'L3_gnn_ta_ln_w': (1.0, 0.6),
     'L3_gnn_ta_ln_b': (0.0, 0.8),
     'L3_gnn_ta_b2': (0.0, 0.8),
     'L3_gnn_g1_b': (0.0, 0.1),
     'L3_gnn_g2_b': (0.0, 0.1),
     'L3_gnn_n1_w': (1.0, 0.2),
     'L3_gnn_n1_b': (0.0, 0.1),
     'L3_gnn_n2_w': (1.0, 0.2),
     'L3_gnn_n2_b': (0.0, 0.1)}
    factors = {'edge_attr_10': 8.0,
     'edge_attr_4': 8.0,
     'edge_weight': 8.0,
     'L2_gnn_W_fc1': 8.0,
     'L2_gnn_W_fc2': 8.0,
     'L2_gnn_W_l1_0': 8.0,
     'L2_gnn_W_l1_1': 8.0,
     'L2_gnn_W_l2_0': 8.0,
     'L2_gnn_W_l2_1': 8.0,
     'L2_gnn_W_alpha': 8.0,
     'L3_gnn_ta_w1': 8.0,
     'L3_gnn_ta_w2': 8.0,
     'L3_gnn_g1_att_src': 8.0,
     'L3_gnn_g1_att_dst': 40.273,
     'L3_gnn_g1_ew': 8.0,
     'L3_gnn_g1_att_edge': 8.0,
     'L3_gnn_g2_att_src': 7.799,
     'L3_gnn_g2_att_dst': 64.0,
     'L3_gnn_g2_ew': 8.0,
     'L3_gnn_g2_att_edge': 8.0,
     'L2_gnn_W_sc0': 8.0,
     'L2_gnn_W_sc1': 8.0}
    for name, (base, spread) in spreads.items():
        noise = np.random.default_rng([zlib.crc32(name.encode()), seed]).standard_normal(out[name].shape)
        drawn = base * np.exp(spread * noise) if base else spread * noise
        out[name] = jnp.asarray(drawn.astype(out[name].dtype))
    for name, factor in factors.items():
        out[name] = (out[name] * factor).astype(out[name].dtype)
    return out
```

```python
from contextlib import ExitStack

import numpy as np
import concourse.bass as bass
from concourse import mybir

F32 = mybir.dt.float32
I32 = mybir.dt.int32
ALU = mybir.AluOpType
ACT = mybir.ActivationFunctionType
AX = mybir.AxisListType.X

P = 128
N = 3125
E = 103125
D = 128
MUL = 32
HEADS = 4
C = D // HEADS
BUCKETS = -(-N // P)
NP = BUCKETS * P
TILES = -(-E // P)
EP = TILES * P
RUN = TILES
ITEMS = TILES + BUCKETS - 1
RING = 16
TURNS = -(-ITEMS // RING)
ITEMS_RUN = TURNS * RING
IBLK = -(-ITEMS_RUN // P)
IPAD = IBLK * P
ZR = 13
ZTURNS = RUN // ZR
assert ZTURNS * ZR == RUN
BIG = 1e30
FAR = float(1 << 20)
LN_EPS = 1e-5
CHUNKS = [(c, min(c + 512, NP)) for c in range(0, NP, 512)]
TW_COLS = 416
TW_STEPS = ZR * P // TW_COLS
SLOT = 3232

WEIGHTS = ["wn1", "ws1", "wn2", "ws2", "gcn0", "gcn1", "gcn2", "gcn3", "wy", "wsc", "wl2a", "wl2b",
           "walpha", "wfc2", "ipw1a", "ipw1b", "ipw2a", "ipw2b", "taw2", "gw0", "gw1", "ident"]
VECS = ["bn1", "bs1", "bn2", "bs2", "gb0", "gb1", "gb2", "gb3", "ipb1a", "ipb1b", "lnwa", "lnwb", "lnba",
        "lnbb", "ipb2", "pnw", "pnb", "tab2", "g1b", "g2b", "n1w", "n1b", "n2w", "n2b"]


def gnn_kernel(nc, io, out):
    with ExitStack() as ctx:
        def sb(name, shape, dt=F32):
            return ctx.enter_context(nc.sbuf_tensor(name, shape, dt))

        sems = {}

        def S(name):
            if name not in sems:
                sems[name] = ctx.enter_context(nc.semaphore(name))
            return sems[name]

        def dram(name, shape, dt=F32):
            return nc.dram_tensor(name, shape, dt).ap()

        ps = ctx.enter_context(nc.psum_tensor("ps", [P, 8 * 512], F32))
        acc = ps[:, 0:NP]
        side = ps[:, 7 * 512:8 * 512]
        W = sb("weights", [P, len(WEIGHTS) * P])
        V = sb("vectors", [P, len(VECS)])
        w = {n: W[:, i * P:(i + 1) * P] for i, n in enumerate(WEIGHTS)}
        v = {n: V[:, i:i + 1] for i, n in enumerate(VECS)}
        ident = w["ident"]
        wfc1 = sb("wfc1", [10, 100])
        att = sb("att", [P, 16])
        attw = sb("attw", [P, 8])
        ones = sb("ones", [P, 2 * P])
        zeros = sb("zeros", [1, P])
        iota = sb("iota", [P, P])
        eps = sb("eps", [P, 1])
        big = sb("big", [P, 7 * SLOT])
        G = [big[:, i * SLOT:i * SLOT + NP] for i in range(7)]
        edge = sb("edge", [P, 20 * RUN])
        fillw = edge[:, 0:8 * RUN]
        ae = edge[:, 8 * RUN:16 * RUN]
        z = edge[:, 16 * RUN:20 * RUN]
        dloc = sb("dloc", [P, IPAD])
        srcI = sb("srcI", [P, IPAD], I32)
        src_scan = sb("src_scan", [P, RUN], I32)
        keep = sb("keep", [P, RUN])
        still = sb("still", [P, RUN])
        bk_row = sb("bk_row", [1, IPAD], I32)
        rows = sb("rows", [P, RING * P])
        hot = sb("hot", [P, RING * P])
        idx_ring = sb("idx_ring", [P, 2 * ZR], I32)
        node = sb("node", [P, 24 * BUCKETS])

        def nd(i, k=1):
            return node[:, i * BUCKETS:(i + k) * BUCKETS]

        nodeid, cnt, rowptr, nextptr, deg, invdeg, has, dinv = (nd(i) for i in range(8))
        a8, aeloop8 = nd(8, 8), nd(16, 8)
        nodei = sb("nodei", [P, 3 * BUCKETS], I32)
        rowsel, end_i, start_i = (nodei[:, i * BUCKETS:(i + 1) * BUCKETS] for i in range(3))
        gat = sb("gat", [P, 24 * BUCKETS])
        zmax, sseg, ploop, rs = (gat[:, 4 * i * BUCKETS:4 * (i + 1) * BUCKETS] for i in range(4))
        am = gat[:, 16 * BUCKETS:24 * BUCKETS]
        small = sb("small", [P, 48])
        item_f, thresh = rows[:, 0:8 * IBLK], rows[:, P:P + BUCKETS]
        item_i = sb("item_i", [P, 2 * IBLK], I32)
        thresh_i = sb("thresh_i", [P, BUCKETS - 1], I32)
        keepT = sb("keepT", [8, 2 * P])
        carry = hot[0:8, 0:P + 1]
        carry_in = sb("carry_in", [P, 8])

        rp_d = dram("rp_d", [NP + P])
        item_d = dram("item_d", [2, IPAD], I32)
        nodevec_d = dram("nodevec_d", [2, NP])
        tabs = [io["x_rows"]] + [dram(f"tab{i}", [NP, D]) for i in range(1, 9)]
        seg_d = dram("seg_d", [EP, 8])
        run8_d = dram("run8_d", [EP, 8])
        run4_d = [dram(f"run4_{i}", [EP, 4]) for i in range(4)]
        p_d = [dram(f"p_{i}", [EP, 4]) for i in range(2)]
        asrc_d = [dram(f"asrc_{i}", [NP, 4]) for i in range(2)]
        tw_d = dram("tw_d", [3, EP])

        invdeg_bc, dinv_bc, attr_bc = G[0], G[1], G[1]
        tw_ring = big[0:3, 0:2 * ZR * P]
        tw_act, tw_th = G[2][:, 0:ZR * P], G[3][:, 0:ZR * P]
        run = big[:, 5 * SLOT:5 * SLOT + 4 * RUN]
        pen_keep = big[:, 6 * SLOT:6 * SLOT + RUN]
        pen_still = big[:, 6 * SLOT + RUN:6 * SLOT + 2 * RUN]
        prob_rows = big[:, 5 * SLOT:5 * SLOT + IBLK * 512]
        ea_ring = big[0:10, 6 * SLOT:6 * SLOT + RING * P]
        accAB, scT = edge[:, 0:2 * NP], edge[:, 2 * NP:3 * NP]
        accA, accB = edge[:, 0:NP], edge[:, NP:2 * NP]
        sh_rows = edge[:, 0:IBLK * 512]
        shT = edge[:, 3 * NP:3 * NP + 4 * IPAD]
        after = 3 * NP + 4 * IPAD
        msg_ring = edge[:, after:after + 4 * 256]
        hid_ring = edge[0:100, after + 1024:after + 1024 + 4 * P]
        mul_tmp = edge[:, after + 1536:after + 1536 + 2 * 160]
        pT = edge[:, 0:4 * IPAD]
        zring = rows[:, 0:2 * ZR * 4]
        taln = rows[0:3, 4 * D:5 * D]
        edgew = rows[:, 0:4 * D]
        z_v, run_v = (a.rearrange("p (j h) -> p j h", h=4) for a in (z, run))
        fill_v, ae_v = (a.rearrange("p (j h) -> p j h", h=8) for a in (fillw, ae))
        t_time, t_tr, t_r, t_one, t_std, t_var = (fillw[:, i * RUN:(i + 1) * RUN] for i in range(6))
        LOADS = 7
        HALF = RING // 2
        INV, INV2 = float(1 / np.sqrt(MUL)), float(1 / np.sqrt(2 * MUL))

        def hold(eng, sem, val):
            eng.wait_ge(sem, val)
            eng.sem_inc(S("holds"), 1)

        ctx.enter_context(nc.allow_non_contiguous_dma(reason="small node-major arrays"))
        block = ctx.enter_context(nc.Block())

        @block.sync
        def _(sp):
            def load(dst, src, sem="loads"):
                sp.dma_start(dst, src).then_inc(S(sem), 16)

            load(big[:, 0:RUN].bitcast(I32), io["dst_ext"][0:EP].rearrange("(p j) -> p j", p=P), "scan_loads")
            load(big[:, RUN:2 * RUN].bitcast(I32), io["dst_ext"][1:EP + 1].rearrange("(p j) -> p j", p=P), "scan_loads")
            load(big[:, 2 * RUN:3 * RUN].bitcast(I32), io["dst_first"].unsqueeze(0).to_broadcast([P, TILES]), "scan_loads")
            load(W[:], io["weights"])
            load(V[:], io["vectors"])
            load(src_scan[:], io["src_rows"].rearrange("t e -> (t e)").rearrange("(p j) -> p j", p=P))
            load(wfc1[:], io["wfc1"])
            load(att[:], io["att"])
            load(G[5], io["xT"])
            load(small[:, 16:20], io["ta_cols"])
            sp.wait_ge(S("rowptr_ready"), 1)
            sp.dma_start(rp_d[0:NP].rearrange("(b p) -> p b", p=P), rowptr).then_inc(S("rp_out"), 16)
            sp.dma_start(rp_d[NP:NP + P].rearrange("(p b) -> p b", p=P), small[:, 0:1]).then_inc(S("rp_out"), 16)
            sp.wait_ge(S("rp_out"), 32)
            load(nextptr, rp_d[1:NP + 1].rearrange("(b p) -> p b", p=P), "rp_in")
            load(thresh[:, 0:BUCKETS - 1], rp_d[P:NP].rearrange("(b p) -> b p", p=P)[:, 0]
                 .unsqueeze(0).to_broadcast([P, BUCKETS - 1]), "rp_in")
            sp.wait_ge(S("items_ready"), 1)
            for r in range(2):
                sp.dma_start(item_d[r].rearrange("(c p) -> p c", p=P),
                             item_i[:, r * IBLK:(r + 1) * IBLK]).then_inc(S("item_out"), 16)
            sp.wait_ge(S("item_out"), 32)
            load(bk_row[:], item_d[0:1, :], "item_in")
            sp.wait_ge(S("nodevec_ready"), 1)
            sp.wait_ge(S("slots_free"), 1)
            sp.dma_start(nodevec_d[0].rearrange("(b p) -> p b", p=P), invdeg).then_inc(S("nodevec_out"), 16)
            sp.dma_start(nodevec_d[1].rearrange("(b p) -> p b", p=P), dinv).then_inc(S("nodevec_out"), 16)
            sp.wait_ge(S("nodevec_out"), 32)
            load(invdeg_bc, nodevec_d[0:1, :].to_broadcast([P, NP]), "nodevec_in")
            load(dinv_bc, nodevec_d[1:2, :].to_broadcast([P, NP]), "nodevec_in")

            def store_table(i):
                sp.wait_ge(S("table_rows"), i)
                sp.dma_start(tabs[i].rearrange("(b p) f -> p b f", p=P),
                             G[4].rearrange("p (b f) -> p b f", f=D)).then_inc(S("table_out"), 16)

            for i in range(1, 6):
                store_table(i)
            sp.wait_ge(S("layer_done"), 2)
            load(attr_bc, io["attr"].to_broadcast([P, NP]), "attr_in")
            store_table(6)
            with sp.Fori(0, TURNS) as i:
                for u in range(RING):
                    t = sp.value_load(item_d[1:2, bass.ds(i * RING + u, 1)], min_val=0, max_val=TILES - 1)
                    sp.wait_ge(S("hid_ps"), i * RING + (u + 1))
                    sp.dma_start(ea_ring[:, u * P:(u + 1) * P],
                                 io["ea10T"][:, bass.ds(t * P, P)]).then_inc(S(f"ea_in{u}"), 16)
            sp.wait_ge(S("layer_done"), 3)
            load(t_time, io["ew_jp"].rearrange("(p j) -> p j", p=P), "ew_in")
            load(edgew[:, 0:2 * D], io["edgew"], "ew_in")
            load(edgew[:, 2 * D:4 * D], io["att_edge"].to_broadcast([P, 2 * D]), "ew_in")
            sp.wait_ge(S("tw_rows"), 1)
            for r, row in enumerate((t_tr, t_r, t_one)):
                sp.dma_start(tw_d[r].rearrange("(p j) -> p j", p=P), row).then_inc(S("tw_out"), 16)
            sp.wait_ge(S("tw_out"), 48)
            with sp.Fori(0, ZTURNS // 2) as i:
                for s in range(2):
                    sp.wait_ge(S("tw1"), i * (2 * TW_STEPS) + (s + 1) * TW_STEPS)
                    sp.dma_start(tw_ring[:, s * ZR * P:(s + 1) * ZR * P],
                                 tw_d[:, bass.ds((i * 2 + s) * (ZR * P), ZR * P)]).then_inc(S(f"tw_in{s}"), 16)
            sp.wait_ge(S("fill_zero"), 1)
            sp.dma_start(seg_d.rearrange("(p j) h -> p (j h)", p=P), fillw).then_inc(S("seg_zeroed"), 16)
            sp.wait_ge(S("run8"), 1)
            sp.dma_start(run8_d.rearrange("(p j) h -> p (j h)", p=P), fillw).then_inc(S("run8_out"), 16)
            for g in range(2):
                sp.wait_ge(S("a8"), g + 1)
                sp.dma_start(asrc_d[g].rearrange("(b p) h -> p b h", p=P),
                             a8.rearrange("p (b h) -> p b h", h=8)[:, :, 0:4]).then_inc(S("asrc_out"), 16)
                store_table(7 + g)
                sp.wait_ge(S("runmax"), g + 1)
                sp.dma_start(run4_d[2 * g].rearrange("(p j) h -> p (j h)", p=P), run).then_inc(S("runmax_out"), 16)
                sp.wait_ge(S("seg_out"), 16 * BUCKETS * (g + 1))
                sp.wait_ge(S("run8_out"), 16)
                load(fillw, seg_d.rearrange("(p j) h -> p (j h)", p=P), "seg_in")
                sp.wait_ge(S("prob"), g + 1)
                sp.dma_start(p_d[g].rearrange("(p j) h -> p (j h)", p=P), z).then_inc(S("p_out"), 16)
                sp.wait_ge(S("runsum"), g + 1)
                sp.dma_start(run4_d[2 * g + 1].rearrange("(p j) h -> p (j h)", p=P), run).then_inc(S("runsum_out"), 16)
            sp.wait_ge(S("out_rows"), 1)
            sp.dma_start(out.rearrange("(b p) f -> p b f", p=P),
                         G[4].rearrange("p (b f) -> p b f", f=D)).then_inc(S("out_done"), 16)
            sp.wait_ge(S("out_done"), 16)

        @block.gpsimd
        def _(pool):
            pool.iota(iota[:], [[1, P]], base=0, channel_multiplier=0,
                      allow_small_or_imprecise_dtypes=True).then_inc(S("iotas"), 1)
            pool.iota(nodeid, [[P, BUCKETS]], base=0, channel_multiplier=1,
                      allow_small_or_imprecise_dtypes=True).then_inc(S("iotas"), 1)
            pool.iota(item_f[:, 0:IBLK], [[P, IBLK]], base=0, channel_multiplier=1,
                      allow_small_or_imprecise_dtypes=True).then_inc(S("iotas"), 1)

            def gather(dst, table, index, sem):
                pool.indirect_dma_start(dst, None, table, bass.IndirectOffsetOnAxis(index, 0)).then_inc(S(sem), 16)

            pool.wait_ge(S("rowsel_ready"), 1)
            for b in range(BUCKETS):
                gather(G[2][:, b * P:(b + 1) * P].bitcast(I32), io["dst_rows"], rowsel[:, b:b + 1], "ptr_rows")
            pool.wait_ge(S("items_ready"), 1)
            for c in range(IBLK):
                ix = item_i[:, IBLK + c:IBLK + c + 1]
                gather(G[3][:, c * P:(c + 1) * P].bitcast(I32), io["dst_rows"], ix, "item_rows")
                gather(G[4][:, c * P:(c + 1) * P].bitcast(I32), io["src_rows"], ix, "item_rows")
                gather(sh_rows[:, c * 512:(c + 1) * 512], io["ea4_rows"], ix, "sh_rows")

            def gather_pass(n, table):
                with pool.Fori(0, TURNS) as i:
                    for u in range(RING):
                        if u % HALF == 0:
                            hold(pool, S("idx_ready"), i * 2 + (2 * n * TURNS + u // HALF + 1))
                        gather(rows[:, u * P:(u + 1) * P], table, idx_ring[:, u:u + 1], f"row_in{u}")

            def node_gather(dst, table, sem, width):
                for b in range(BUCKETS):
                    gather(dst[:, b * width:(b + 1) * width], table, end_i[:, b:b + 1], sem)

            for n in range(7):
                if n:
                    pool.wait_ge(S("table_out"), 16 * n)
                gather_pass(n, tabs[n])
            pool.wait_ge(S("run8_out"), 16)
            node_gather(aeloop8, run8_d, "aeloop_rows", 8)
            for g in range(2):
                pool.wait_ge(S("asrc_out"), 16 * (g + 1))
                with pool.Fori(0, ZTURNS // 2) as i:
                    for s in range(2):
                        hold(pool, S("zidx_ready"), i * 2 + (g * ZTURNS + s + 1))
                        for u in range(s * ZR, (s + 1) * ZR):
                            gather(zring[:, u * 4:(u + 1) * 4], asrc_d[g], idx_ring[:, u:u + 1], f"z_in{s}")
                pool.wait_ge(S("runmax_out"), 16 * (g + 1))
                node_gather(zmax, run4_d[2 * g], "zmax_rows", 4)
                pool.wait_ge(S("am"), g + 1)
                pool.wait_ge(S("seg_zeroed"), 16)
                for b in range(BUCKETS):
                    pool.indirect_dma_start(
                        seg_d, bass.IndirectOffsetOnAxis(start_i[:, b:b + 1], 0), am[:, b * 8:(b + 1) * 8], None,
                        bounds_check=EP - 1, oob_is_err=False).then_inc(S("seg_out"), 16)
                pool.wait_ge(S("runsum_out"), 16 * (g + 1))
                node_gather(sseg, run4_d[2 * g + 1], "sseg_rows", 4)
                pool.wait_ge(S("p_out"), 16 * (g + 1))
                for c in range(IBLK):
                    gather(prob_rows[:, c * 512:(c + 1) * 512], p_d[g].rearrange("(t e) h -> t (e h)", e=P),
                           item_i[:, IBLK + c:IBLK + c + 1], "prob_rows")
                pool.wait_ge(S("table_out"), 16 * (7 + g))
                gather_pass(7 + g, tabs[7 + g])

        @block.tensor
        def _(pe):
            def dense(pairs, sem):
                for a, b in CHUNKS:
                    for k, (wt, x) in enumerate(pairs):
                        last = pe.matmul(ps[:, a:b], wt, x[:, a:b], start=(k == 0), stop=(k == len(pairs) - 1))
                last.then_inc(S(sem), 1)

            def turn(x, sem):
                for b in range(BUCKETS):
                    last = pe.transpose(ps[:, b * P:(b + 1) * P], x[:, b * P:(b + 1) * P], ident)
                last.then_inc(S(sem), 1)

            def item_turn(x, sem):
                for c in range(IBLK):
                    xc = x[:, c * 512:(c + 1) * 512].rearrange("p (e h) -> p h e", h=4)
                    for h in range(4):
                        k = 4 * c + h
                        last = pe.transpose(ps[:, k * P:(k + 1) * P], xc[:, h, :], ident)
                last.then_inc(S(sem), 1)

            def norm(xs, n):
                avg = ones[:, 0:P] if len(xs) == 1 else ones[:, P:2 * P]
                dense([(avg, x) for x, _ in xs], "norm_mean")
                pe.wait_ge(S("norm_sq"), n)
                dense([(avg, q) for _, q in xs], "norm_var")

            def small_turn(n, k):
                pe.wait_ge(S("scan_last"), n)
                pe.transpose(side[0:k, 0:P], small[:, 32:32 + k], ident).then_inc(S("scan_lastT"), 1)
                pe.wait_ge(S("scan_carry"), n)
                pe.transpose(side[:, 256:256 + k], carry[0:k, 0:P], ident[0:k, 0:k]).then_inc(S("scan_carryT"), 1)

            def gather_pass(n, m, by_node=False):
                for k in range(7):
                    pe.matmul(ps[:, k * 512:(k + 1) * 512], zeros[:], W[0:1, 0:512], start=True, stop=False,
                              skip_group_check=True)
                with pe.Fori(0, TURNS) as i:
                    for u in range(RING):
                        b = pe.value_load(bk_row[0:1, bass.ds(i * RING + u, 1)], min_val=0, max_val=BUCKETS - 1)
                        if not by_node:
                            pe.wait_ge(S(f"row_in{u}"), i * 16 + 16 * (n * TURNS + 1))
                        pe.wait_ge(S("item_ready"), i * RING + (m * ITEMS_RUN + u + 1))
                        one, row = hot[:, u * P:(u + 1) * P], rows[:, u * P:(u + 1) * P]
                        lhs, rhs = (one, row) if by_node else (row, one)
                        pe.matmul(ps[:, bass.ds(b * P, P)], lhs, rhs, start=False, stop=False,
                                  skip_group_check=True).then_inc(S("item_done"), 1)

            pe.sem_inc(S("item_done"), RING)
            pe.wait_ge(S("loads"), 16 * LOADS)
            pe.wait_ge(S("keep_last"), 1)
            pe.transpose(side[0:8, 0:P], small[:, 32:40], ident).then_inc(S("keepT_ps"), 1)
            pe.wait_ge(S("item_f32"), 1)
            for k in range(2):
                for c in range(IBLK):
                    last = pe.transpose(ps[:, k * 1024 + c * P:k * 1024 + (c + 1) * P],
                                        G[3 + k][:, c * P:(c + 1) * P], ident)
            last.then_inc(S("itemsT"), 1)
            pe.wait_ge(S("itemsT_used"), 1)
            pe.wait_ge(S("sh_rows"), 16 * IBLK)
            item_turn(sh_rows, "shT_ps")
            pe.wait_ge(S("shT"), 1)
            pe.wait_ge(S("item_in"), 16)
            gather_pass(0, 0)
            pe.wait_ge(S("agg"), 1)
            dense([(w["wn1"], G[2]), (w["ws1"], G[5])], "lin")
            pe.wait_ge(S("hid"), 1)
            turn(G[3], "rowsT")
            pe.wait_ge(S("table_rows"), 1)
            gather_pass(1, 1)
            pe.wait_ge(S("agg"), 2)
            dense([(w["wn2"], G[2]), (w["ws2"], G[3])], "lin")
            pe.wait_ge(S("norm_in"), 1)
            norm([(G[5], G[2])], 1)
            for k in range(4):
                pe.wait_ge(S("conv_in"), k + 1)
                dense([(w[f"gcn{k}"], G[3] if k else G[5])], "lin")
                pe.wait_ge(S("scaled"), k + 1)
                turn(G[2], "rowsT")
                pe.wait_ge(S("table_rows"), 2 + k)
                gather_pass(2 + k, 2 + k)
            pe.wait_ge(S("norm_in"), 2)
            norm([(G[5], G[2])], 2)
            pe.wait_ge(S("conv_in"), 5)
            dense([(w["wsc"], G[5])], "lin")
            pe.wait_ge(S("scaled"), 5)
            dense([(w["wy"], G[5])], "lin")
            pe.wait_ge(S("scaled"), 6)
            turn(G[2], "rowsT")
            pe.wait_ge(S("table_rows"), 6)

            def hidden(i, k, u):
                pe.wait_ge(S(f"ea_in{u}"), i * 16 + 16)
                pe.wait_ge(S("silu"), k + 1)
                pe.matmul(ps[0:100, (u % 2) * 512:(u % 2) * 512 + P], wfc1[:], ea_ring[:, u * P:(u + 1) * P],
                          start=True, stop=True).then_inc(S("hid_ps"), 1)

            def edge_w(i, k, u):
                pe.wait_ge(S("silu"), k + 3)
                pe.wait_ge(S("msg"), k + 1)
                pe.matmul(ps[:, (2 + u % 2) * 512:(2 + u % 2) * 512 + P], hid_ring[:, (u % 4) * P:(u % 4 + 1) * P],
                          w["wfc2"][0:100, :], start=True, stop=True).then_inc(S("w_ps"), 1)

            def by_dest(i, k, u):
                pe.wait_ge(S("msg"), k + 3)
                pe.wait_ge(S("summed"), k + 1)
                o = (4 + u % 4) * 512
                for hf in range(2):
                    last = pe.matmul(ps[:, o + hf * P:o + (hf + 1) * P],
                                     msg_ring[:, (u % 4) * 256 + hf * P:(u % 4) * 256 + (hf + 1) * P],
                                     hot[:, u * P:(u + 1) * P], start=True, stop=True, skip_group_check=True)
                last.then_inc(S("sums_ps"), 1)

            def item_step(i, u, parts, first=False):
                for part, lag in parts:
                    if u >= lag:
                        part(i, i * RING + (u - lag), u - lag)
                    elif not first:
                        part(i - 1, i * RING + (u - lag), u - lag + RING)

            pe.sem_inc(S("hid_ps"), RING)
            pe.sem_inc(S("w_ps"), 4)
            pe.sem_inc(S("sums_ps"), 4)
            parts = [(hidden, 0), (edge_w, 1), (by_dest, 3)]
            for u in range(RING):
                item_step(0, u, parts, first=True)
            with pe.Fori(1, TURNS) as i:
                for u in range(RING):
                    item_step(i, u, parts)
            for u in range(3):
                item_step(TURNS, u, [x for x in parts if x[1] > u])
            pe.wait_ge(S("agg"), 3)
            dense([(w["walpha"], accA)], "lin")
            pe.wait_ge(S("scaled"), 7)
            dense([(w["wl2a"], accA), (w["wl2b"], accB)], "lin")
            pe.wait_ge(S("norm_in"), 3)
            norm([(G[5], G[2])], 3)
            pe.wait_ge(S("layer_done"), 3)
            pe.matmul(side[:, 0:2], ones[:, 0:P], small[:, 16:18], start=True, stop=True).then_inc(S("tw_mean"), 1)
            pe.wait_ge(S("tw_sqs"), 1)
            pe.matmul(side[:, 8:11], ones[:, 0:P], small[:, 22:25], start=True, stop=True).then_inc(S("tw_moments"), 1)
            pe.wait_ge(S("tw_cols"), 1)
            pe.transpose(side[0:3, 128:256], small[:, 29:32], ident).then_inc(S("tw_colsT"), 1)
            pe.wait_ge(S("taln"), 1)

            def tw_first(i, s, q):
                if q == 0:
                    pe.wait_ge(S(f"tw_in{s}"), i * 16 + 16)
                pe.wait_ge(S("tw_relu"), i * (2 * TW_STEPS) + (s * TW_STEPS + q + 1))
                a = s * ZR * P + q * TW_COLS
                pe.matmul(ps[:, (q % 2) * 512:(q % 2) * 512 + TW_COLS], taln, tw_ring[:, a:a + TW_COLS],
                          start=True, stop=True).then_inc(S("tw1"), 1)

            def tw_second(i, s, q):
                pe.wait_ge(S("tw_relu"), i * (2 * TW_STEPS) + (s * TW_STEPS + q + 3))
                pe.wait_ge(S("tw_tanh"), i * (2 * TW_STEPS) + (s * TW_STEPS + q + 1))
                pe.matmul(ps[:, (2 + q % 2) * 512:(2 + q % 2) * 512 + TW_COLS], w["taw2"],
                          tw_act[:, q * TW_COLS:(q + 1) * TW_COLS], start=True, stop=True).then_inc(S("tw2"), 1)

            def tw_third(i, s):
                pe.wait_ge(S("tw_tanh"), i * (2 * TW_STEPS) + (s * TW_STEPS + TW_STEPS + 2))
                pe.wait_ge(S("tw_copied"), i * 2 + (s + 1))
                for c in range(ZR):
                    last = pe.matmul(ps[:, (4 + s) * 512 + c * 8:(4 + s) * 512 + c * 8 + 8],
                                     tw_th[:, c * P:(c + 1) * P], attw[:], start=True, stop=True, skip_group_check=True)
                last.then_inc(S("tw3"), 1)

            def tw_turns(i, first):
                for s in range(2):
                    tw_first(i, s, 0)
                    tw_first(i, s, 1)
                    if s == 1:
                        tw_third(i, 0)
                    elif not first:
                        tw_third(i - 1, 1)
                    tw_second(i, s, 0)
                    tw_first(i, s, 2)
                    tw_second(i, s, 1)
                    tw_first(i, s, 3)
                    tw_second(i, s, 2)
                    tw_second(i, s, 3)

            pe.sem_inc(S("tw1"), 2 * TW_STEPS)
            pe.sem_inc(S("tw2"), TW_STEPS)
            pe.sem_inc(S("tw3"), 1)
            tw_turns(0, True)
            with pe.Fori(1, ZTURNS // 2) as i:
                tw_turns(i, False)
            tw_third(ZTURNS // 2 - 1, 1)
            small_turn(1, 8)
            dense([(w["ipw1a"], G[5])], "lin")
            pe.wait_ge(S("ip_hid"), 1)
            dense([(w["ipw1b"], G[5])], "lin")
            pe.wait_ge(S("ip_hid"), 2)
            norm([(G[0], G[2]), (G[1], G[3])], 4)
            pe.wait_ge(S("ip_norm"), 1)
            dense([(w["ipw2a"], G[0]), (w["ipw2b"], G[1])], "lin")
            pe.wait_ge(S("norm_in"), 4)
            norm([(G[0], G[2])], 5)
            for g in range(2):
                pe.wait_ge(S("gat_in"), g + 1)
                dense([(w[f"gw{g}"], G[0])], "lin")
                pe.wait_ge(S("gat_hT"), g + 1)
                for b in range(BUCKETS):
                    last = pe.matmul(side[:, b * 8:(b + 1) * 8], G[1][:, b * P:(b + 1) * P], att[:, 8 * g:8 * g + 8],
                                     start=True, stop=True, skip_group_check=True)
                last.then_inc(S("a8_ps"), 1)
                turn(G[1], "rowsT")
                pe.wait_ge(S("a8"), g + 1)
                small_turn(2 + 3 * g, 4)
                small_turn(3 + 3 * g, 8)
                small_turn(4 + 3 * g, 4)
                pe.wait_ge(S("prob_rows"), 16 * IBLK * (g + 1))
                pe.wait_ge(S("table_rows"), 7 + g)
                item_turn(prob_rows, "pT_ps")
                pe.wait_ge(S("pT"), g + 1)
                gather_pass(7 + g, 6 + g, by_node=True)
                pe.wait_ge(S("gat_rows"), g + 1)
                turn(G[2], "gatT")
                pe.wait_ge(S("norm_in"), 5 + g)
                norm([(G[0], G[2])], 6 + g)
            pe.wait_ge(S("norm_in"), 7)
            norm([(G[0], G[2])], 8)
            pe.wait_ge(S("layer_done"), 4)
            turn(G[0], "outT")

        @block.scalar
        def _(act):
            def norm(xs, n):
                act.wait_ge(S("norm_cent"), n)
                for x, q in xs:
                    last = nc.scalar.activation(q, x, ACT.Square)
                last.then_inc(S("norm_sq"), 1)
                act.wait_ge(S("norm_var"), n)
                nc.scalar.activation(xs[0][1], acc, ACT.Sqrt, bias=eps[:]).then_inc(S("norm_std"), 1)

            def rows_out(n):
                act.wait_ge(S("rowsT"), n)
                if n > 1:
                    act.wait_ge(S("table_out"), 16 * (n - 1))
                nc.scalar.copy(G[4], acc).then_inc(S("table_rows"), 1)

            act.wait_ge(S("deg"), 1)
            nc.scalar.activation(dinv, deg, ACT.Sqrt, bias=1.0).then_inc(S("sqrt_deg"), 1)
            act.wait_ge(S("bias"), 1)
            act.wait_ge(S("lin"), 1)
            nc.scalar.activation(G[3], acc, ACT.Relu, bias=v["bn1"]).then_inc(S("hid"), 1)
            rows_out(1)
            norm([(G[5], G[2])], 1)
            for k in range(4):
                rows_out(2 + k)
                if k < 3:
                    act.wait_ge(S("agg_conv"), k + 1)
                    nc.scalar.activation(G[3], G[2], ACT.Identity if k == 1 else ACT.Relu,
                                         bias=v[f"gb{k}"]).then_inc(S("conv_in"), 1)
            norm([(G[5], G[2])], 2)
            rows_out(6)
            act.sem_inc(S("silu"), 2)
            with act.Fori(0, TURNS) as i:
                for u in range(RING):
                    act.wait_ge(S("hid_ps"), i * RING + (u + RING + 1))
                    act.wait_ge(S("w_ps"), i * RING + (u + 1))
                    nc.scalar.activation(hid_ring[:, (u % 4) * P:(u % 4 + 1) * P],
                                         ps[0:100, (u % 2) * 512:(u % 2) * 512 + P], ACT.Silu,
                                         scale=float(1 / np.sqrt(10.0))).then_inc(S("silu"), 1)
            norm([(G[5], G[2])], 3)
            act.wait_ge(S("tw_var"), 1)
            nc.scalar.activation(t_std, t_var, ACT.Sqrt, bias=eps[:]).then_inc(S("tw_std"), 1)
            act.sem_inc(S("tw_tanh"), 2)
            with act.Fori(0, ZTURNS) as i:
                for q in range(TW_STEPS):
                    act.wait_ge(S("tw2"), i * TW_STEPS + (q + TW_STEPS + 1))
                    act.wait_ge(S("tw3"), i + 1)
                    nc.scalar.activation(tw_th[:, q * TW_COLS:(q + 1) * TW_COLS],
                                         ps[:, (2 + q % 2) * 512:(2 + q % 2) * 512 + TW_COLS],
                                         ACT.Tanh, bias=v["tab2"]).then_inc(S("tw_tanh"), 1)
            act.wait_ge(S("lin"), 11)
            nc.scalar.activation(G[0], acc, ACT.Relu, bias=v["ipb1a"]).then_inc(S("ip_hid"), 1)
            act.wait_ge(S("lin"), 12)
            nc.scalar.activation(G[1], acc, ACT.Relu, bias=v["ipb1b"]).then_inc(S("ip_hid"), 1)
            norm([(G[0], G[2]), (G[1], G[3])], 4)
            norm([(G[0], G[2])], 5)
            for g in range(2):
                act.wait_ge(S("lin"), 14 + g)
                nc.scalar.copy(G[1], acc).then_inc(S("gat_hT"), 1)
                rows_out(7 + g)
                act.wait_ge(S("lp"), g + 1)
                nc.scalar.activation(ploop, ploop, ACT.Exp).then_inc(S("ploop"), 1)
                act.wait_ge(S("alpha"), g + 1)
                nc.scalar.activation(z, z, ACT.Exp).then_inc(S("prob"), 1)
                norm([(G[0], G[2])], 6 + g)
                act.wait_ge(S("elu_min"), g + 1)
                nc.scalar.activation(G[2], G[2], ACT.Exp).then_inc(S("elu_exp"), 1)
            norm([(G[0], G[2])], 8)
            act.wait_ge(S("outT"), 1)
            act.wait_ge(S("table_out"), 16 * 8)
            nc.scalar.copy(G[4], acc).then_inc(S("out_rows"), 1)

        @block.vector
        def _(dve):
            vec = nc.vector
            count = [0]

            def link(ins):
                count[0] += 1
                ins.then_inc(S("dve_link"), 1)
                dve.wait_ge(S("dve_link"), count[0])

            def wide(a, k):
                return a.unsqueeze(2).to_broadcast([P, a.shape[1], k])

            def cut(a, k):
                return a.rearrange("p (a b) -> p a b", b=k)

            vec.memset(zeros[:], 0.0)
            vec.memset(ones[:, 0:P], 1.0 / P)
            vec.memset(ones[:, P:2 * P], 0.5 / P)
            vec.memset(eps[:], LN_EPS)
            link(vec.memset(small[:, 0:1], float(E)))
            dve.wait_ge(S("scan_loads"), 48)
            link(vec.tensor_copy(big[:, SLOT:SLOT + 3 * RUN], big[:, 0:3 * RUN].bitcast(I32)))
            prev, cur, first = (big[:, SLOT + i * RUN:SLOT + (i + 1) * RUN] for i in range(3))
            link(vec.tensor_tensor(keep[:], prev, cur, ALU.is_equal))
            link(vec.tensor_tensor_scan(still[:], keep[:], keep[:], 1.0, ALU.mult, ALU.mult))
            vec.tensor_copy(small[:, 32:40], still[:, RUN - 1:RUN].to_broadcast([P, 8])).then_inc(S("keep_last"), 1)
            dve.wait_ge(S("keepT_ps"), 1)
            link(vec.tensor_copy(keepT[:, 0:P], side[0:8, 0:P]))
            link(vec.tensor_scalar(keepT[:, P:2 * P], keepT[:, 0:P], 1.0, BIG, ALU.subtract, ALU.mult))
            dve.wait_ge(S("iotas"), 3)
            for b in range(BUCKETS):
                link(vec.tensor_scalar(hot[:, 0:RUN], first, nodeid[:, b:b + 1], None, ALU.is_lt, ALU.add,
                                       accum_out=cnt[:, b:b + 1]))
            link(vec.tensor_scalar(cnt, cnt, 1.0, 0.0, ALU.subtract, ALU.max))
            vec.tensor_copy(rowsel, cnt).then_inc(S("rowsel_ready"), 1)
            dve.wait_ge(S("ptr_rows"), 16 * BUCKETS)
            link(vec.tensor_copy(G[3], G[2].bitcast(I32)))
            link(vec.tensor_tensor(cut(G[3], P), cut(G[3], P), wide(nodeid, P), ALU.is_lt))
            link(vec.tensor_reduce(deg, cut(G[3], P), AX, ALU.add))
            vec.scalar_tensor_tensor(rowptr, cnt, float(P), deg, ALU.mult, ALU.add).then_inc(S("rowptr_ready"), 1)
            dve.wait_ge(S("rowptr_ready"), 1)
            dve.wait_ge(S("rp_in"), 32)
            vec.tensor_tensor(deg, nextptr, rowptr, ALU.subtract).then_inc(S("deg"), 1)
            dve.wait_ge(S("deg"), 1)
            link(vec.tensor_scalar(invdeg, deg, 1.0, None, ALU.max))
            link(vec.reciprocal(invdeg, invdeg))
            link(vec.tensor_scalar(has, deg, 1.0, None, ALU.min))
            link(vec.tensor_scalar(cnt, nextptr, 1.0, 0.0, ALU.subtract, ALU.max))
            link(vec.tensor_copy(end_i, cnt))
            link(vec.tensor_scalar(cnt, has, 1.0, -FAR, ALU.subtract, ALU.mult))
            link(vec.tensor_tensor(cnt, cnt, rowptr, ALU.add))
            link(vec.tensor_copy(start_i, cnt))
            dve.wait_ge(S("sqrt_deg"), 1)
            vec.reciprocal(dinv, dinv).then_inc(S("nodevec_ready"), 1)
            th = thresh[:, 0:BUCKETS - 1]
            link(vec.tensor_copy(thresh_i[:], th))
            link(vec.tensor_scalar(thresh_i[:], thresh_i[:], 7, None, ALU.arith_shift_right))
            link(vec.tensor_copy(th, thresh_i[:]))
            link(vec.tensor_tensor(th, th, iota[:, 0:BUCKETS - 1], ALU.add))
            item_n, item_b, item_t, item_off = (item_f[:, i * IBLK:(i + 1) * IBLK] for i in range(4))
            past = cut(hot[:, 0:IBLK * (BUCKETS - 1)], BUCKETS - 1)
            link(vec.tensor_tensor(past, th.unsqueeze(1).to_broadcast([P, IBLK, BUCKETS - 1]),
                                   wide(item_n, BUCKETS - 1), ALU.is_lt))
            link(vec.tensor_reduce(item_b, past, AX, ALU.add))
            link(vec.tensor_tensor(item_t, item_n, item_b, ALU.subtract))
            link(vec.tensor_scalar(item_t, item_t, float(TILES - 1), None, ALU.min))
            link(vec.tensor_copy(item_i[:, 0:IBLK], item_b))
            vec.tensor_copy(item_i[:, IBLK:2 * IBLK], item_t).then_inc(S("items_ready"), 1)
            link(vec.tensor_scalar(item_off, item_n, float(ITEMS - 1), FAR, ALU.is_gt, ALU.mult))
            link(vec.scalar_tensor_tensor(item_off, item_b, float(P), item_off, ALU.mult, ALU.add))
            dve.wait_ge(S("item_rows"), 16 * 2 * IBLK)
            link(vec.tensor_copy(G[3][:, 0:IPAD], G[3][:, 0:IPAD].bitcast(I32)))
            link(vec.tensor_copy(G[4][:, 0:IPAD], G[4][:, 0:IPAD].bitcast(I32)))
            vec.tensor_tensor(cut(G[3][:, 0:IPAD], P), cut(G[3][:, 0:IPAD], P), wide(item_off, P),
                              ALU.subtract).then_inc(S("item_f32"), 1)
            dve.wait_ge(S("item_f32"), 1)
            dve.sem_inc(S("slots_free"), 1)
            dve.wait_ge(S("itemsT"), 1)
            vec.tensor_copy(dloc[:], ps[:, 0:IPAD])
            vec.tensor_copy(srcI[:], ps[:, 1024:1024 + IPAD]).then_inc(S("itemsT_used"), 1)

            def item_columns(dst, sem, n):
                vec.tensor_copy(dst.rearrange("p (c k h) -> p c h k", c=IBLK, h=4),
                                ps[:, 0:4 * IPAD].rearrange("p (c h k) -> p c h k", c=IBLK, h=4)).then_inc(S(sem), 1)
                dve.wait_ge(S(sem), n)

            dve.wait_ge(S("shT_ps"), 1)
            item_columns(shT, "shT", 1)
            dve.wait_ge(S("loads"), 16 * LOADS)
            link(vec.tensor_scalar(w["wfc2"], w["wfc2"], 0.1, None, ALU.mult))
            link(vec.tensor_scalar(w["wfc2"][:, MUL:2 * MUL], w["wfc2"][:, MUL:2 * MUL], float(1 / np.sqrt(3.0)),
                                   None, ALU.mult))
            link(vec.tensor_tensor(v["bn2"], v["bn2"], v["bs2"], ALU.add))
            vec.tensor_tensor(v["bn1"], v["bn1"], v["bs1"], ALU.add).then_inc(S("bias"), 1)

            def indices(n, i, u):
                vec.tensor_copy(idx_ring[:, u:u + HALF], srcI[:, bass.ds(i * RING + u, HALF)]).then_inc(S("idx_ready"), 1)

            def one_hot(i, u):
                return vec.tensor_scalar(hot[:, u * P:(u + 1) * P], iota[:], dloc[:, bass.ds(i * RING + u, 1)], None,
                                         ALU.is_equal)

            def passed(m):
                dve.wait_ge(S("item_done"), RING + (m + 1) * ITEMS_RUN)

            def gather_pass(n, m):
                with dve.Fori(0, TURNS) as i:
                    for u in range(RING):
                        if u % HALF == 0:
                            hold(dve, S("item_done"), i * RING + (m * ITEMS_RUN + u + HALF))
                            indices(n, i, u)
                        one_hot(i, u).then_inc(S("item_ready"), 1)
                passed(m)

            def weighted_pass(n, m):
                def turn_(i, first):
                    for u in range(RING + (HALF if i is TURNS else 0)):
                        if i is not TURNS and u % HALF == 0:
                            hold(dve, S("item_done"), i * RING + (m * ITEMS_RUN + u + HALF))
                            indices(n, i, u)
                        if i is not TURNS:
                            one_hot(i, u)
                        if u >= HALF:
                            weigh(i, i * RING + (u - HALF), u - HALF)
                        elif not first:
                            weigh(i - 1, i * RING + (u - HALF), u + HALF)

                def weigh(i, k, u):
                    row = rows[:, u * P:(u + 1) * P]
                    dve.wait_ge(S(f"row_in{u}"), i * 16 + 16 * (n * TURNS + 1))
                    vec.tensor_tensor(cut(row, C), cut(row, C), wide(pT[:, bass.ds(k * 4, 4)], C),
                                      ALU.mult).then_inc(S("item_ready"), 1)

                turn_(0, True)
                with dve.Fori(1, TURNS) as i:
                    turn_(i, False)
                for u in range(HALF):
                    weigh(TURNS - 1, TURNS * RING + u - HALF, u + HALF)
                passed(m)

            def norm(xs, n):
                dve.wait_ge(S("norm_mean"), n)
                for x, q in xs:
                    last = vec.tensor_tensor(x, x, acc, ALU.subtract)
                last.then_inc(S("norm_cent"), 1)
                dve.wait_ge(S("norm_std"), n)
                link(vec.reciprocal(xs[0][1], xs[0][1]))
                for x, q in xs:
                    link(vec.tensor_tensor(x, x, xs[0][1], ALU.mult))

            gather_pass(0, 0)
            dve.wait_ge(S("nodevec_in"), 32)
            vec.tensor_tensor(G[2], acc, invdeg_bc, ALU.mult).then_inc(S("agg"), 1)
            gather_pass(1, 1)
            vec.tensor_tensor(G[2], acc, invdeg_bc, ALU.mult).then_inc(S("agg"), 1)
            dve.wait_ge(S("lin"), 2)
            vec.scalar_tensor_tensor(G[5], acc, v["bn2"], G[5], ALU.add, ALU.add).then_inc(S("norm_in"), 1)
            norm([(G[5], G[2])], 1)
            dve.sem_inc(S("layer_done"), 1)
            dve.sem_inc(S("conv_in"), 1)
            for k in range(4):
                dve.wait_ge(S("lin"), 3 + k)
                vec.tensor_tensor(G[2], acc, dinv_bc, ALU.mult).then_inc(S("scaled"), 1)
                dve.wait_ge(S("scaled"), k + 1)
                gather_pass(2 + k, 2 + k)
                link(vec.tensor_tensor(G[2], acc, G[2], ALU.add))
                vec.tensor_tensor(G[2], G[2], dinv_bc, ALU.mult).then_inc(S("agg_conv"), 1)
            dve.wait_ge(S("agg_conv"), 4)
            vec.scalar_tensor_tensor(G[5], G[2], v["gb3"], G[5], ALU.add, ALU.add).then_inc(S("norm_in"), 1)
            norm([(G[5], G[2])], 2)
            dve.sem_inc(S("layer_done"), 1)
            dve.sem_inc(S("conv_in"), 1)
            dve.wait_ge(S("attr_in"), 16)
            dve.wait_ge(S("lin"), 7)
            vec.scalar_tensor_tensor(scT, acc, INV, attr_bc, ALU.mult, ALU.mult).then_inc(S("scaled"), 1)
            dve.wait_ge(S("lin"), 8)
            vec.scalar_tensor_tensor(G[2], acc, INV, attr_bc, ALU.mult, ALU.mult).then_inc(S("scaled"), 1)
            link(vec.memset(accAB, 0.0))

            def messages(i, k, u):
                row = rows[:, u * P:(u + 1) * P]
                y0, y1 = row[:, 0:MUL], cut(row[:, MUL:P], MUL)
                o = (2 + u % 2) * 512
                w00, w11, w01, w10 = (ps[:, o + j * MUL:o + (j + 1) * MUL] for j in range(4))
                msg = msg_ring[:, (u % 4) * 256:(u % 4 + 1) * 256]
                m00, m11, m01, m10 = msg[:, 0:32], msg[:, 32:64], cut(msg[:, 64:160], MUL), cut(msg[:, 160:256], MUL)
                tmp = mul_tmp[:, (u % 2) * 160:(u % 2 + 1) * 160]
                dot, t01, d = cut(tmp[:, 0:96], MUL), tmp[:, 96:128], tmp[:, 128:160]
                sh0 = shT[:, bass.ds(k * 4, 1)]
                sh1 = wide(shT[:, bass.ds(k * 4 + 1, 3)], MUL)
                dve.wait_ge(S(f"row_in{u}"), i * 16 + 16 * (6 * TURNS + 1))
                vec.tensor_tensor(dot, y1, sh1, ALU.mult).then_inc(S("prod"), 1)
                dve.wait_ge(S("w_ps"), k + 5)
                vec.tensor_tensor(t01, w01, y0, ALU.mult).then_inc(S("prod"), 1)
                dve.wait_ge(S("sums_ps"), k + 1)
                vec.scalar_tensor_tensor(m00, y0, sh0, w00, ALU.mult, ALU.mult)
                vec.scalar_tensor_tensor(m10, y1, sh0, w10.unsqueeze(1).to_broadcast([P, 3, MUL]), ALU.mult, ALU.mult)
                dve.wait_ge(S("prod"), k * 3 + 1)
                vec.tensor_reduce(d, tmp[:, 0:96].rearrange("p (c u) -> p u c", c=3), AX,
                                  ALU.add).then_inc(S("prod"), 1)
                dve.wait_ge(S("prod"), k * 3 + 3)
                vec.tensor_tensor(m01, t01.unsqueeze(1).to_broadcast([P, 3, MUL]), sh1, ALU.mult)
                vec.tensor_tensor(m11, d, w11, ALU.mult).then_inc(S("msg"), 1)

            def add_up(i, k, u):
                b = dve.value_load(bk_row[0:1, bass.ds(k, 1)], min_val=0, max_val=BUCKETS - 1)
                dst = accAB.rearrange("p (h n) -> p h n", h=2)[:, :, bass.ds(b * P, P)]
                o = (4 + u % 4) * 512
                dve.wait_ge(S("sums_ps"), k + 5)
                dve.wait_ge(S("summed"), k + 4)
                vec.tensor_tensor(dst, dst, cut(ps[:, o:o + 256], P), ALU.add).then_inc(S("summed"), 1)

            def l2_step(i, u, first=False, last=False):
                if not last:
                    if u % HALF == 0:
                        indices(6, i, u)
                    one_hot(i, u)
                for part, lag in ((messages, HALF), (add_up, HALF + 2)):
                    if u >= lag:
                        if not last:
                            part(i, i * RING + (u - lag), u - lag)
                    elif not first:
                        part(i - 1, i * RING + (u - lag), u - lag + RING)

            dve.sem_inc(S("msg"), 2)
            dve.sem_inc(S("summed"), 4)
            for u in range(RING):
                l2_step(0, u, first=True)
            with dve.Fori(1, TURNS) as i:
                for u in range(RING):
                    l2_step(i, u)
            for u in range(HALF + 2):
                l2_step(TURNS, u, last=True)
            dve.wait_ge(S("summed"), ITEMS_RUN + 4)
            vec.tensor_tensor(accAB.rearrange("p (h n) -> p h n", h=2), accAB.rearrange("p (h n) -> p h n", h=2),
                              invdeg_bc.unsqueeze(1).to_broadcast([P, 2, NP]), ALU.mult).then_inc(S("agg"), 1)
            dve.wait_ge(S("lin"), 9)
            vec.scalar_tensor_tensor(G[2], acc, INV2, attr_bc, ALU.mult, ALU.mult).then_inc(S("scaled"), 1)
            dve.wait_ge(S("lin"), 10)
            link(vec.scalar_tensor_tensor(G[3], acc, INV2, attr_bc, ALU.mult, ALU.mult))
            link(vec.tensor_tensor(G[3], G[3], G[2], ALU.mult))
            link(vec.tensor_tensor(G[3], G[3], scT, ALU.add))
            vec.tensor_tensor(G[5], G[5], G[3], ALU.add).then_inc(S("norm_in"), 1)
            norm([(G[5], G[2])], 3)
            dve.sem_inc(S("layer_done"), 1)
            dve.wait_ge(S("tw_mean"), 1)
            w1b1, lnw = small[:, 20:22], small[:, 18:19]
            link(vec.tensor_tensor(w1b1, small[:, 16:18], side[:, 0:2], ALU.subtract))
            vec.tensor_tensor(small[:, 22:24], w1b1, w1b1[:, 0:1].to_broadcast([P, 2]), ALU.mult)
            vec.tensor_tensor(small[:, 24:25], w1b1[:, 1:2], w1b1[:, 1:2], ALU.mult).then_inc(S("tw_sqs"), 1)
            dve.wait_ge(S("tw_moments"), 1)
            link(vec.tensor_copy(small[:, 25:28], side[:, 8:11]))
            link(vec.tensor_scalar(small[:, 28:29], small[:, 26:27], 2.0, None, ALU.mult))
            vec.tensor_tensor(small[:, 29:31], w1b1, lnw.to_broadcast([P, 2]), ALU.mult)
            vec.tensor_copy(small[:, 31:32], small[:, 19:20]).then_inc(S("tw_cols"), 1)
            dve.wait_ge(S("tw_colsT"), 1)
            link(vec.tensor_copy(taln, side[0:3, 128:256]))
            dve.wait_ge(S("ew_in"), 48)
            link(vec.tensor_tensor(edgew[:, 0:2 * D], edgew[:, 0:2 * D], edgew[:, 2 * D:4 * D], ALU.mult))
            vec.tensor_reduce(attw[:], cut(edgew[:, 0:2 * D], C), AX, ALU.add).then_inc(S("taln"), 1)
            link(vec.tensor_scalar(t_var, t_time, small[:, 25:26], small[:, 28:29], ALU.mult, ALU.add))
            link(vec.tensor_tensor(t_var, t_var, t_time, ALU.mult))
            vec.tensor_scalar(t_var, t_var, small[:, 27:28], 0.0, ALU.add, ALU.max).then_inc(S("tw_var"), 1)
            dve.wait_ge(S("tw_std"), 1)
            vec.memset(t_one, 1.0)
            link(vec.reciprocal(t_r, t_std))
            vec.tensor_tensor(t_tr, t_time, t_r, ALU.mult).then_inc(S("tw_rows"), 1)

            def tw_relu(i, s, q):
                n = i * (2 * TW_STEPS) + (s * TW_STEPS + q)
                dve.wait_ge(S("tw1"), n + (2 * TW_STEPS + 1))
                dve.wait_ge(S("tw2"), n + 1)
                vec.tensor_scalar(tw_act[:, q * TW_COLS:(q + 1) * TW_COLS],
                                  ps[:, (q % 2) * 512:(q % 2) * 512 + TW_COLS], 0.0, None, ALU.max).then_inc(S("tw_relu"), 1)

            def tw_copy(i, s):
                hold(dve, S("tw3"), i * 2 + (s + 2))
                vec.tensor_copy(ae[:, bass.ds((i * 2 + s) * (ZR * 8), ZR * 8)],
                                ps[:, (4 + s) * 512:(4 + s) * 512 + ZR * 8]).then_inc(S("tw_copied"), 1)

            def tw_turns(i, first):
                for s in range(2):
                    tw_relu(i, s, 0)
                    tw_relu(i, s, 1)
                    if s == 1:
                        tw_copy(i, 0)
                    elif not first:
                        tw_copy(i - 1, 1)
                    tw_relu(i, s, 2)
                    tw_relu(i, s, 3)

            dve.sem_inc(S("tw_relu"), 2)
            dve.sem_inc(S("tw_copied"), 2)
            tw_turns(0, True)
            with dve.Fori(1, ZTURNS // 2) as i:
                tw_turns(i, False)
            tw_copy(ZTURNS // 2 - 1, 1)
            dve.wait_ge(S("tw_copied"), ZTURNS + 2)

            scans = [0]

            def across(dst, k, penal, op0, op1, init):
                scans[0] += 1
                n = scans[0]
                link(vec.memset(carry[:, 0:1], init))
                vec.tensor_copy(small[:, 32:32 + k], dst[:, RUN - 1, 0:k]).then_inc(S("scan_last"), 1)
                dve.wait_ge(S("scan_lastT"), n)
                vec.tensor_tensor_scan(carry[0:k, 1:P + 1], keepT[0:k, (P if penal else 0):(2 * P if penal else P)],
                                       side[0:k, 0:P], init, op0, op1).then_inc(S("scan_carry"), 1)
                dve.wait_ge(S("scan_carryT"), n)
                link(vec.tensor_copy(carry_in[:, 0:k], side[:, 256:256 + k]))
                for h in range(k):
                    last = vec.scalar_tensor_tensor(dst[:, :, h], pen_still if penal else still[:],
                                                    carry_in[:, h:h + 1], dst[:, :, h], op0, op1)
                return last

            vec.memset(fillw, 0.0).then_inc(S("fill_zero"), 1)
            dve.wait_ge(S("seg_zeroed"), 16)
            for h in range(8):
                last = vec.tensor_tensor_scan(fill_v[:, :, h], keep[:], ae_v[:, :, h], 0.0, ALU.mult, ALU.add)
            link(last)
            across(fill_v, 8, False, ALU.mult, ALU.add, 0.0).then_inc(S("run8"), 1)
            norm([(G[0], G[2]), (G[1], G[3])], 4)
            vec.tensor_scalar(G[0], G[0], v["lnwa"], v["lnba"], ALU.mult, ALU.add)
            vec.tensor_scalar(G[1], G[1], v["lnwb"], v["lnbb"], ALU.mult, ALU.add).then_inc(S("ip_norm"), 1)
            dve.wait_ge(S("lin"), 13)
            vec.tensor_scalar(G[0], acc, v["ipb2"], None, ALU.add).then_inc(S("norm_in"), 1)
            norm([(G[0], G[2])], 5)
            link(vec.tensor_scalar(G[0], G[0], v["pnw"], v["pnb"], ALU.mult, ALU.add))
            link(vec.tensor_copy(G[3], G[5]))
            vec.tensor_scalar(G[0], G[0], 0.0, 10.0, ALU.max, ALU.min).then_inc(S("gat_in"), 1)
            dve.wait_ge(S("aeloop_rows"), 16 * BUCKETS)
            link(vec.tensor_tensor(cut(aeloop8, 8), cut(aeloop8, 8), wide(invdeg, 8), ALU.mult))
            link(vec.tensor_tensor(cut(aeloop8, 8), cut(aeloop8, 8), wide(has, 8), ALU.mult))
            for g in range(2):
                a8v, loop8 = cut(a8, 8), cut(aeloop8, 8)
                asrc, adst, aloop = a8v[:, :, 0:4], a8v[:, :, 4:8], loop8[:, :, 4 * g:4 * g + 4]
                dve.wait_ge(S("a8_ps"), g + 1)
                vec.tensor_copy(a8, side[:, 0:8 * BUCKETS]).then_inc(S("a8"), 1)
                dve.wait_ge(S("a8"), g + 1)

                def z_take(i, s):
                    hold(dve, S(f"z_in{s}"), i * (16 * ZR) + 16 * ZR * (g * (ZTURNS // 2) + 1))
                    vec.tensor_copy(z[:, bass.ds((i * 2 + s) * (ZR * 4), ZR * 4)],
                                    zring[:, s * ZR * 4:(s + 1) * ZR * 4]).then_inc(S("z_taken"), 1)

                def z_index(i, s):
                    vec.tensor_copy(idx_ring[:, s * ZR:(s + 1) * ZR],
                                    src_scan[:, bass.ds((i * 2 + s) * ZR, ZR)]).then_inc(S("zidx_ready"), 1)

                for s in range(2):
                    z_index(0, s)
                with dve.Fori(1, ZTURNS // 2) as i:
                    for s in range(2):
                        z_take(i - 1, s)
                        z_index(i, s)
                for s in range(2):
                    z_take(ZTURNS // 2 - 1, s)
                dve.wait_ge(S("z_taken"), ZTURNS * (g + 1))
                link(vec.tensor_tensor(z_v, z_v, ae_v[:, :, 4 * g:4 * g + 4], ALU.add))
                link(vec.tensor_scalar(pen_keep, keep[:], 1.0, BIG, ALU.subtract, ALU.mult))
                link(vec.tensor_scalar(pen_still, still[:], 1.0, BIG, ALU.subtract, ALU.mult))
                for h in range(4):
                    last = vec.tensor_tensor_scan(run_v[:, :, h], pen_keep, z_v[:, :, h], -BIG, ALU.add, ALU.max)
                link(last)
                across(run_v, 4, True, ALU.add, ALU.max, -BIG).then_inc(S("runmax"), 1)
                zm, pl, sg, amv = cut(zmax, 4), cut(ploop, 4), cut(sseg, 4), cut(am, 8)
                link(vec.tensor_scalar(cnt, has, 1.0, BIG, ALU.subtract, ALU.mult))
                dve.wait_ge(S("zmax_rows"), 16 * BUCKETS * (g + 1))
                link(vec.tensor_tensor(zm, zm, wide(has, 4), ALU.mult))
                link(vec.tensor_tensor(zm, zm, wide(cnt, 4), ALU.add))
                link(vec.tensor_tensor(pl, asrc, aloop, ALU.add))
                link(vec.tensor_tensor(zm, zm, pl, ALU.max))
                link(vec.tensor_tensor(zm, zm, adst, ALU.add))
                link(vec.tensor_tensor(pl, pl, adst, ALU.add))
                link(vec.tensor_copy(amv[:, :, 0:4], adst))
                vec.scalar_tensor_tensor(amv[:, :, 4:8], zm, 0.2, zm, ALU.mult, ALU.max).then_inc(S("am"), 1)
                dve.wait_ge(S("am"), g + 1)
                link(vec.scalar_tensor_tensor(pl, pl, 0.2, pl, ALU.mult, ALU.max))
                vec.tensor_tensor(pl, pl, amv[:, :, 4:8], ALU.subtract).then_inc(S("lp"), 1)
                dve.wait_ge(S("seg_in"), 16 * (g + 1))
                for h in range(8):
                    last = vec.tensor_tensor_scan(fill_v[:, :, h], keep[:], fill_v[:, :, h], 0.0, ALU.mult, ALU.add)
                link(last)
                link(across(fill_v, 8, False, ALU.mult, ALU.add, 0.0))
                link(vec.tensor_tensor(z_v, z_v, fill_v[:, :, 0:4], ALU.add))
                link(vec.scalar_tensor_tensor(z, z, 0.2, z, ALU.mult, ALU.max))
                link(vec.tensor_tensor(z_v, z_v, fill_v[:, :, 4:8], ALU.subtract))
                vec.tensor_scalar(z, z, 0.0, None, ALU.min).then_inc(S("alpha"), 1)
                dve.wait_ge(S("prob"), g + 1)
                dve.wait_ge(S("runmax_out"), 16 * (g + 1))
                for h in range(4):
                    last = vec.tensor_tensor_scan(run_v[:, :, h], keep[:], z_v[:, :, h], 0.0, ALU.mult, ALU.add)
                link(last)
                across(run_v, 4, False, ALU.mult, ALU.add, 0.0).then_inc(S("runsum"), 1)
                dve.wait_ge(S("sseg_rows"), 16 * BUCKETS * (g + 1))
                dve.wait_ge(S("ploop"), g + 1)
                link(vec.tensor_tensor(sg, sg, wide(has, 4), ALU.mult))
                link(vec.tensor_tensor(sg, sg, pl, ALU.add))
                link(vec.tensor_scalar(sseg, sseg, 1e-16, None, ALU.add))
                link(vec.reciprocal(rs, sseg))
                dve.wait_ge(S("pT_ps"), g + 1)
                item_columns(pT, "pT", g + 1)
                weighted_pass(7 + g, 6 + g)
                link(vec.tensor_tensor(cut(G[2], C), cut(G[4], C), wide(ploop, C), ALU.mult))
                link(vec.tensor_tensor(G[2], G[2], acc, ALU.add))
                vec.tensor_tensor(cut(G[2], C), cut(G[2], C), wide(rs, C), ALU.mult).then_inc(S("gat_rows"), 1)
                dve.wait_ge(S("gatT"), g + 1)
                link(vec.scalar_tensor_tensor(G[0], acc, v[f"g{g + 1}b"], G[0], ALU.add, ALU.add))
                vec.tensor_scalar(G[0], G[0], 10.0, -10.0, ALU.min, ALU.max).then_inc(S("norm_in"), 1)
                norm([(G[0], G[2])], 6 + g)
                link(vec.tensor_scalar(G[0], G[0], v[f"n{g + 1}w"], v[f"n{g + 1}b"], ALU.mult, ALU.add))
                vec.tensor_scalar(G[2], G[0], 0.0, None, ALU.min).then_inc(S("elu_min"), 1)
                dve.wait_ge(S("elu_exp"), g + 1)
                link(vec.scalar_tensor_tensor(G[0], G[0], 0.0, G[2], ALU.max, ALU.add))
                last = vec.tensor_scalar(G[0], G[0], 1.0, None, ALU.subtract)
                if g == 0:
                    last.then_inc(S("gat_in"), 1)
                    dve.wait_ge(S("gat_in"), 2)
                else:
                    link(last)
            vec.tensor_tensor(G[0], G[0], G[3], ALU.add).then_inc(S("norm_in"), 1)
            norm([(G[0], G[2])], 8)
            dve.sem_inc(S("layer_done"), 1)


def layouts(x):
    def pad(a, *shape):
        out = np.zeros(shape, a.dtype)
        out[tuple(slice(0, n) for n in a.shape)] = a
        return out

    dst = np.full(EP + 1, NP, np.int32)
    dst[0] = -1
    dst[1:E + 1] = x["dst"]
    src = pad(x["src"], EP)
    w2 = "L2_gnn_W_"

    def blocks(w0, w1, rows0, rows1, cols0, cols1):
        out = np.zeros((P, P), np.float32)
        out[np.ix_(rows0, cols0)] = w0
        for c in range(3):
            out[np.ix_(rows1[c], cols1[c])] = w1
        return out

    u = np.arange(MUL)
    mixed = [MUL + 3 * u + c for c in range(3)]
    split = [MUL + MUL * c + u for c in range(3)]
    wl1 = x[w2 + "l2_1"]
    wl2a, wl2b = np.zeros((P, P), np.float32), np.zeros((P, P), np.float32)
    wl2a[np.ix_(np.arange(2 * MUL), u)] = x[w2 + "l2_0"]
    for c in range(3):
        at, to = (wl2a, 2 * MUL + MUL * c) if c < 2 else (wl2b, 0)
        at[np.ix_(to + u, mixed[c])] = wl1[:MUL]
        wl2b[np.ix_(MUL + MUL * c + u, mixed[c])] = wl1[MUL:]
    walpha = np.zeros((P, P), np.float32)
    walpha[:2 * MUL, :] = x[w2 + "alpha"]
    mats = {
        "wn1": x["L0_gnn_W_neigh1"].T, "ws1": x["L0_gnn_W_self1"].T,
        "wn2": x["L0_gnn_W_neigh2"].T, "ws2": x["L0_gnn_W_self2"].T,
        "wy": blocks(x[w2 + "l1_0"], x[w2 + "l1_1"], u, mixed, u, split),
        "wsc": blocks(x[w2 + "sc0"], x[w2 + "sc1"], u, mixed, u, mixed),
        "wl2a": wl2a, "wl2b": wl2b, "walpha": walpha, "wfc2": pad(x[w2 + "fc2"], P, P),
        "ipw1a": x["L3_gnn_ip_w1"][:, :P], "ipw1b": x["L3_gnn_ip_w1"][:, P:],
        "ipw2a": x["L3_gnn_ip_w2"][:P], "ipw2b": x["L3_gnn_ip_w2"][P:],
        "taw2": x["L3_gnn_ta_w2"], "gw0": x["L3_gnn_g1_w"], "gw1": x["L3_gnn_g2_w"], "ident": np.eye(P, dtype=np.float32),
    }
    for k in range(4):
        mats[f"gcn{k}"] = pad(x[f"L1_gnn_W{k + 1}"], P, P)
    vecs = {
        "bn1": x["L0_gnn_b_neigh1"], "bs1": x["L0_gnn_b_self1"], "bn2": x["L0_gnn_b_neigh2"], "bs2": x["L0_gnn_b_self2"],
        "ipb1a": x["L3_gnn_ip_b1"][:P], "ipb1b": x["L3_gnn_ip_b1"][P:], "lnwa": x["L3_gnn_ip_ln_w"][:P],
        "lnwb": x["L3_gnn_ip_ln_w"][P:], "lnba": x["L3_gnn_ip_ln_b"][:P], "lnbb": x["L3_gnn_ip_ln_b"][P:],
        "ipb2": x["L3_gnn_ip_b2"], "pnw": x["L3_gnn_pn_w"], "pnb": x["L3_gnn_pn_b"], "tab2": x["L3_gnn_ta_b2"],
        "g1b": x["L3_gnn_g1_b"], "g2b": x["L3_gnn_g2_b"], "n1w": x["L3_gnn_n1_w"], "n1b": x["L3_gnn_n1_b"],
        "n2w": x["L3_gnn_n2_w"], "n2b": x["L3_gnn_n2_b"],
    }
    for k in range(4):
        vecs[f"gb{k}"] = pad(x[f"L1_gnn_b{k + 1}"], P)
    att = np.zeros((P, 16), np.float32)
    for g in range(2):
        for j, name in enumerate(("src", "dst")):
            for h in range(HEADS):
                att[h * C:(h + 1) * C, 8 * g + 4 * j + h] = x[f"L3_gnn_g{g + 1}_att_{name}"][h]
    return {
        "x_rows": pad(x["x"], NP, D),
        "xT": pad(x["x"], NP, D).T,
        "dst_ext": dst, "dst_rows": dst[1:].reshape(TILES, P), "dst_first": dst[1::P],
        "src_rows": src.reshape(TILES, P),
        "ea4_rows": pad(x["edge_attr_4"], EP, 4).reshape(TILES, 4 * P),
        "ea10T": pad(x["edge_attr_10"], EP, 10).T,
        "ew_jp": pad(x["edge_weight"], EP).reshape(P, RUN).T.reshape(-1),
        "attr": pad(x["node_vec1"], NP, 1).T,
        "weights": np.concatenate([mats[n] for n in WEIGHTS], axis=1),
        "vectors": np.stack([vecs[n] for n in VECS], axis=1),
        "wfc1": x[w2 + "fc1"], "att": att,
        "edgew": np.concatenate([x["L3_gnn_g1_ew"], x["L3_gnn_g2_ew"]], axis=1),
        "att_edge": np.concatenate([x["L3_gnn_g1_att_edge"].reshape(1, D), x["L3_gnn_g2_att_edge"].reshape(1, D)], axis=1),
        "ta_cols": np.stack([x["L3_gnn_ta_w1"][0], x["L3_gnn_ta_b1"], x["L3_gnn_ta_ln_w"], x["L3_gnn_ta_ln_b"]], axis=1),
    }


def kernel(**inputs):
    import concourse.bacc as bacc
    from concourse.bass_utils import run_bass_kernel_spmd

    arrays = {k: np.ascontiguousarray(a) for k, a in layouts({k: np.asarray(a) for k, a in inputs.items()}).items()}
    nc = bacc.Bacc("TRN2", target_bir_lowering=False, num_devices=1)
    io = {k: nc.dram_tensor(f"in_{k}", a.shape, mybir.dt.from_np(a.dtype), kind="ExternalInput").ap()
          for k, a in arrays.items()}
    out = nc.dram_tensor("out", [NP, D], F32, kind="ExternalOutput").ap()
    gnn_kernel(nc, io, out)
    r = run_bass_kernel_spmd(nc, [{f"in_{k}": a for k, a in arrays.items()}], core_ids=[0])
    return r.results[0]["out"][:N]
```

```python
from contextlib import ExitStack

import numpy as np
import concourse.bass as bass
from concourse import mybir

F32 = mybir.dt.float32
I32 = mybir.dt.int32
BF16 = mybir.dt.bfloat16
F16 = mybir.dt.float16
F8 = mybir.dt.float8e4
ALU = mybir.AluOpType
ACT = mybir.ActivationFunctionType
AX = mybir.AxisListType.X

P = 128
N = 3125
E = 103125
D = 128
MUL = 32
HEADS = 4
C = D // HEADS
BUCKETS = -(-N // P)
NP = BUCKETS * P
TILES = -(-E // P)
EP = TILES * P
RUN = TILES
ITEMS = TILES + BUCKETS - 1
RING = 16
TURNS = -(-ITEMS // RING)
ITEMS_RUN = TURNS * RING
IBLK = -(-ITEMS_RUN // P)
IPAD = IBLK * P
ZR = 13
ZTURNS = RUN // ZR
assert ZTURNS * ZR == RUN
BIG = 1e30
FAR = float(1 << 20)
LN_EPS = 1e-5
CHUNKS = [(c, min(c + 512, NP)) for c in range(0, NP, 512)]
TW_COLS = 416
TW_STEPS = ZR * P // TW_COLS
SLOT = 3232
MID = NP // 2
GROUP = 4
CRING = 4
MOST = 15
CSPLIT = NP // 2
PASSES = 6
COUNTS = BUCKETS * NP // 4

WEIGHTS = ["wn1", "ws1", "wn2", "ws2", "gcn0", "gcn1", "gcn2", "gcn3", "wy", "wsc", "wl2a", "wl2b",
           "walpha", "wfc2", "ipw1a", "ipw1b", "ipw2a", "ipw2b", "taw2", "gw0", "gw1", "ident"]
VECS = ["bn1", "bs1", "bn2", "bs2", "gb0", "gb1", "gb2", "gb3", "ipb1a", "ipb1b", "lnwa", "lnwb", "lnba",
        "lnbb", "ipb2", "pnw", "pnb", "tab2", "g1b", "g2b", "n1w", "n1b", "n2w", "n2b"]


def gnn_kernel(nc, io, out):
    with ExitStack() as ctx:
        def sb(name, shape, dt=F32):
            return ctx.enter_context(nc.sbuf_tensor(name, shape, dt))

        sems = {}

        def S(name):
            if name not in sems:
                sems[name] = ctx.enter_context(nc.semaphore(name))
            return sems[name]

        def dram(name, shape, dt=F32):
            return nc.dram_tensor(name, shape, dt).ap()

        ps = ctx.enter_context(nc.psum_tensor("ps", [P, 8 * 512], F32))
        acc = ps[:, 0:NP]
        side = ps[:, 7 * 512:8 * 512]
        W = sb("weights", [P, len(WEIGHTS) * P])
        V = sb("vectors", [P, len(VECS)])
        w = {n: W[:, i * P:(i + 1) * P] for i, n in enumerate(WEIGHTS)}
        v = {n: V[:, i:i + 1] for i, n in enumerate(VECS)}
        ident = w["ident"]
        wfc1 = sb("wfc1", [10, 100])
        att = sb("att", [P, 16])
        attw = sb("attw", [P, 8])
        ones = sb("ones", [P, 2 * P])
        zeros = sb("zeros", [1, P])
        iota = sb("iota", [P, P])
        eps = sb("eps", [P, 1])
        mem = sb("mem", [P, 7 * SLOT + 20 * RUN])
        big = mem[:, 0:7 * SLOT]
        G = [big[:, i * SLOT:i * SLOT + NP] for i in range(7)]
        edge = mem[:, 7 * SLOT:7 * SLOT + 20 * RUN]
        fillw = edge[:, 0:8 * RUN]
        ae = edge[:, 8 * RUN:16 * RUN]
        z = edge[:, 16 * RUN:20 * RUN]
        dloc = sb("dloc", [P, IPAD])
        srcI = sb("srcI", [P, IPAD], I32)
        src_scan = sb("src_scan", [P, RUN], I32)
        keep = sb("keep", [P, RUN])
        still = sb("still", [P, RUN])
        bk_row = sb("bk_row", [1, IPAD], I32)
        rings = sb("rings", [P, 2 * RING * P])
        rows = rings[:, 0:RING * P]
        hot = rings[:, RING * P:2 * RING * P]
        idx_ring = sb("idx_ring", [P, 2 * ZR], I32)
        node = sb("node", [P, 24 * BUCKETS])

        def nd(i, k=1):
            return node[:, i * BUCKETS:(i + k) * BUCKETS]

        nodeid, cnt, rowptr, nextptr, deg, invdeg, has, dinv = (nd(i) for i in range(8))
        a8, aeloop8 = nd(8, 8), nd(16, 8)
        nodei = sb("nodei", [P, 3 * BUCKETS], I32)
        rowsel, end_i, start_i = (nodei[:, i * BUCKETS:(i + 1) * BUCKETS] for i in range(3))
        gat = sb("gat", [P, 24 * BUCKETS])
        zmax, sseg, ploop, rs = (gat[:, 4 * i * BUCKETS:4 * (i + 1) * BUCKETS] for i in range(4))
        am = gat[:, 16 * BUCKETS:24 * BUCKETS]
        small = sb("small", [P, 48])
        over = gat[:, 0:BUCKETS + 1]
        flag = sb("flag", [1, 1], I32)
        item_f, thresh = rows[:, 0:8 * IBLK], rows[:, P:P + BUCKETS]
        item_i = sb("item_i", [P, 2 * IBLK], I32)
        thresh_i = sb("thresh_i", [P, BUCKETS - 1], I32)
        keepT = sb("keepT", [8, 2 * P])
        carry = hot[0:8, 0:P + 1]
        carry_in = sb("carry_in", [P, 8])

        rp_d = dram("rp_d", [NP + P])
        item_d = dram("item_d", [2, IPAD], I32)
        alt_tab = dram("alt_tab", [NP, D])
        nodevec_d = dram("nodevec_d", [2, NP])
        tabs = [dram(f"tab{i}", [NP, D]) for i in range(3)]
        seg_d = dram("seg_d", [EP, 8])
        run8_d = dram("run8_d", [EP, 8])
        run4_d = [dram(f"run4_{i}", [EP, 4]) for i in range(4)]
        p_d = [dram(f"p_{i}", [EP, 4]) for i in range(2)]
        asrc_d = [dram(f"asrc_{i}", [NP, 4]) for i in range(2)]
        tw_d = dram("tw_d", [3, EP])

        deg_bc, xT, attr_bc = G[0], G[1], G[5]
        parts16 = [mem[:, 4 * SLOT + i * CSPLIT:4 * SLOT + (i + 1) * CSPLIT].bitcast(BF16) for i in range(3)]
        rest = rings[:, 0:NP]
        counts = mem[:, 7 * SLOT + 20 * RUN - COUNTS:7 * SLOT + 20 * RUN].bitcast(F8) \
            .rearrange("p (s d) -> p s d", s=BUCKETS)
        assert 4 * SLOT + 3 * CSPLIT <= 7 * SLOT + 20 * RUN - COUNTS
        src_hot = mem[:, 2 * SLOT:2 * SLOT + CRING * CSPLIT].bitcast(BF16)
        dst_hot = hot[:, 0:CRING * P // 2].bitcast(BF16)
        node_iota = G[5]
        node_iota16 = G[4][:, 0:CSPLIT].bitcast(F16)
        src_f = G[4][:, CSPLIT:CSPLIT + IPAD]
        over_junk = G[5][:, 0:CSPLIT].bitcast(BF16)
        tw_ring = big[0:3, 0:2 * ZR * P]
        tw_act, tw_th = G[2][:, 0:ZR * P], G[3][:, 0:ZR * P]
        run = big[:, 5 * SLOT:5 * SLOT + 4 * RUN]
        pen_keep = big[:, 6 * SLOT:6 * SLOT + RUN]
        pen_still = big[:, 6 * SLOT + RUN:6 * SLOT + 2 * RUN]
        prob_rows = big[:, 5 * SLOT:5 * SLOT + IBLK * 512]
        ea_ring = big[0:10, 6 * SLOT:6 * SLOT + RING * P]
        accAB, scT = edge[:, 0:2 * NP], edge[:, 2 * NP:3 * NP]
        accA, accB = edge[:, 0:NP], edge[:, NP:2 * NP]
        sh_rows = edge[:, 0:IBLK * 512]
        shT = edge[:, 3 * NP:3 * NP + 4 * IPAD]
        after = 3 * NP + 4 * IPAD
        msg_ring = edge[:, after:after + 4 * 256]
        hid_ring = edge[0:100, after + 1024:after + 1024 + 4 * P]
        mul_tmp = edge[:, after + 1536:after + 1536 + 2 * 160]
        pT = edge[:, 0:4 * IPAD]
        zring = rows[:, 0:2 * ZR * 4]
        taln = rows[0:3, 4 * D:5 * D]
        edgew = rows[:, 0:4 * D]
        z_v, run_v = (a.rearrange("p (j h) -> p j h", h=4) for a in (z, run))
        fill_v, ae_v = (a.rearrange("p (j h) -> p j h", h=8) for a in (fillw, ae))
        t_time, t_tr, t_r, t_one, t_std, t_var = (fillw[:, i * RUN:(i + 1) * RUN] for i in range(6))
        LOADS = 6
        HALF = RING // 2
        INV, INV2 = float(1 / np.sqrt(MUL)), float(1 / np.sqrt(2 * MUL))

        def hold(eng, sem, val):
            eng.wait_ge(sem, val)
            eng.sem_inc(S("holds"), 1)

        def alt_flag(eng):
            eng.wait_ge(S("flag"), 1)
            return eng.value_load(flag[0:1, 0:1], min_val=0, max_val=1)

        ctx.enter_context(nc.allow_non_contiguous_dma(reason="small node-major arrays"))
        block = ctx.enter_context(nc.Block())

        @block.sync
        def _(sp):
            def load(dst, src, sem="loads"):
                sp.dma_start(dst, src).then_inc(S(sem), 16)

            load(big[:, 0:RUN].bitcast(I32), io["dst_ext"][0:EP].rearrange("(p j) -> p j", p=P), "scan_loads")
            load(big[:, RUN:2 * RUN].bitcast(I32), io["dst_ext"][1:EP + 1].rearrange("(p j) -> p j", p=P), "scan_loads")
            load(big[:, 2 * RUN:3 * RUN].bitcast(I32), io["dst_first"].unsqueeze(0).to_broadcast([P, TILES]), "scan_loads")
            load(W[:], io["weights"])
            load(V[:], io["vectors"])
            load(src_scan[:], io["src_rows"].rearrange("t e -> (t e)").rearrange("(p j) -> p j", p=P))
            load(wfc1[:], io["wfc1"])
            load(att[:], io["att"])
            load(small[:, 16:20], io["ta_cols"])
            sp.wait_ge(S("rowptr_ready"), 1)
            sp.dma_start(rp_d[0:NP].rearrange("(b p) -> p b", p=P), rowptr).then_inc(S("rp_out"), 16)
            sp.dma_start(rp_d[NP:NP + P].rearrange("(p b) -> p b", p=P), small[:, 0:1]).then_inc(S("rp_out"), 16)
            sp.wait_ge(S("rp_out"), 32)
            load(nextptr, rp_d[1:NP + 1].rearrange("(b p) -> p b", p=P), "rp_in")
            load(thresh[:, 0:BUCKETS - 1], rp_d[P:NP].rearrange("(b p) -> b p", p=P)[:, 0]
                 .unsqueeze(0).to_broadcast([P, BUCKETS - 1]), "rp_in")
            sp.wait_ge(S("items_ready"), 1)
            for r in range(2):
                sp.dma_start(item_d[r].rearrange("(c p) -> p c", p=P),
                             item_i[:, r * IBLK:(r + 1) * IBLK]).then_inc(S("item_out"), 16)
            sp.wait_ge(S("item_out"), 32)
            load(bk_row[:], item_d[0:1, :], "item_in")
            sp.wait_ge(S("nodevec_ready"), 1)
            sp.wait_ge(S("slots_free"), 1)
            sp.dma_start(nodevec_d[0].rearrange("(b p) -> p b", p=P), invdeg).then_inc(S("nodevec_out"), 16)
            sp.dma_start(nodevec_d[1].rearrange("(b p) -> p b", p=P), dinv).then_inc(S("nodevec_out"), 16)
            sp.wait_ge(S("nodevec_out"), 32)
            load(deg_bc, nodevec_d[0:1, :].to_broadcast([P, NP]), "nodevec_in")
            load(xT, io["xT"], "x_in")

            def store_table(i):
                sp.wait_ge(S("table_rows"), i)
                sp.dma_start(tabs[i - 1].rearrange("(b p) f -> p b f", p=P),
                             G[4].rearrange("p (b f) -> p b f", f=D)).then_inc(S("table_out"), 16)

            def alt_table(n):
                sp.wait_ge(S("y"), n + 1)
                sp.dma_start(alt_tab.rearrange("(b p) f -> p b f", p=P),
                             G[2].rearrange("p (b f) -> p b f", f=D)).then_inc(S("alt_table_out"), 16)

            alt = alt_flag(sp)
            for n in range(2):
                with sp.If(alt > 0):
                    alt_table(n)
            sp.wait_ge(S("agg"), 2)
            load(deg_bc, nodevec_d[1:2, :].to_broadcast([P, NP]), "nodevec_in")
            for n in range(2, PASSES):
                with sp.If(alt > 0):
                    alt_table(n)
            sp.wait_ge(S("layer_done"), 2)
            load(deg_bc, nodevec_d[0:1, :].to_broadcast([P, NP]), "nodevec_in")
            load(attr_bc, io["attr"].to_broadcast([P, NP]), "attr_in")
            store_table(1)
            with sp.Fori(0, TURNS) as i:
                for u in range(RING):
                    t = sp.value_load(item_d[1:2, bass.ds(i * RING + u, 1)], min_val=0, max_val=TILES - 1)
                    sp.wait_ge(S("hid_ps"), i * RING + (u + 1))
                    sp.dma_start(ea_ring[:, u * P:(u + 1) * P],
                                 io["ea10T"][:, bass.ds(t * P, P)]).then_inc(S(f"ea_in{u // 4}"), 16)
            sp.wait_ge(S("layer_done"), 3)
            load(t_time, io["ew_jp"].rearrange("(p j) -> p j", p=P), "ew_in")
            load(edgew[:, 0:2 * D], io["edgew"], "ew_in")
            load(edgew[:, 2 * D:4 * D], io["att_edge"].to_broadcast([P, 2 * D]), "ew_in")
            sp.wait_ge(S("tw_rows"), 1)
            for r, row in enumerate((t_tr, t_r, t_one)):
                sp.dma_start(tw_d[r].rearrange("(p j) -> p j", p=P), row).then_inc(S("tw_out"), 16)
            sp.wait_ge(S("tw_out"), 48)
            with sp.Fori(0, ZTURNS // 2) as i:
                for s in range(2):
                    sp.wait_ge(S("tw1"), i * (2 * TW_STEPS) + (s + 1) * TW_STEPS)
                    sp.dma_start(tw_ring[:, s * ZR * P:(s + 1) * ZR * P],
                                 tw_d[:, bass.ds((i * 2 + s) * (ZR * P), ZR * P)]).then_inc(S(f"tw_in{s}"), 16)
            sp.wait_ge(S("fill_zero"), 1)
            sp.dma_start(seg_d.rearrange("(p j) h -> p (j h)", p=P), fillw).then_inc(S("seg_zeroed"), 16)
            sp.wait_ge(S("run8"), 1)
            sp.dma_start(run8_d.rearrange("(p j) h -> p (j h)", p=P), fillw).then_inc(S("run8_out"), 16)
            for g in range(2):
                sp.wait_ge(S("a8"), g + 1)
                sp.dma_start(asrc_d[g].rearrange("(b p) h -> p b h", p=P),
                             a8.rearrange("p (b h) -> p b h", h=8)[:, :, 0:4]).then_inc(S("asrc_out"), 16)
                store_table(2 + g)
                sp.wait_ge(S("runmax"), g + 1)
                sp.dma_start(run4_d[2 * g].rearrange("(p j) h -> p (j h)", p=P), run).then_inc(S("runmax_out"), 16)
                sp.wait_ge(S("seg_out"), 16 * BUCKETS * (g + 1))
                sp.wait_ge(S("run8_out"), 16)
                load(fillw, seg_d.rearrange("(p j) h -> p (j h)", p=P), "seg_in")
                sp.wait_ge(S("prob"), g + 1)
                sp.dma_start(p_d[g].rearrange("(p j) h -> p (j h)", p=P), z).then_inc(S("p_out"), 16)
                sp.wait_ge(S("runsum"), g + 1)
                sp.dma_start(run4_d[2 * g + 1].rearrange("(p j) h -> p (j h)", p=P), run).then_inc(S("runsum_out"), 16)
            sp.wait_ge(S("out_rows"), 1)
            sp.dma_start(out.rearrange("(b p) f -> p b f", p=P),
                         G[4].rearrange("p (b f) -> p b f", f=D)).then_inc(S("out_done"), 16)
            sp.wait_ge(S("out_done"), 16)

        @block.gpsimd
        def _(pool):
            pool.iota(iota[:], [[1, P]], base=0, channel_multiplier=0,
                      allow_small_or_imprecise_dtypes=True).then_inc(S("iotas"), 1)
            pool.iota(nodeid, [[P, BUCKETS]], base=0, channel_multiplier=1,
                      allow_small_or_imprecise_dtypes=True).then_inc(S("iotas"), 1)
            pool.iota(item_f[:, 0:IBLK], [[P, IBLK]], base=0, channel_multiplier=1,
                      allow_small_or_imprecise_dtypes=True).then_inc(S("iotas"), 1)

            pool.iota(node_iota, [[1, NP]], base=-MID, channel_multiplier=0,
                      allow_small_or_imprecise_dtypes=True).then_inc(S("node_iota"), 1)

            def gather(dst, table, index, sem):
                pool.indirect_dma_start(dst, None, table, bass.IndirectOffsetOnAxis(index, 0)).then_inc(S(sem), 16)

            pool.wait_ge(S("rowsel_ready"), 1)
            for b in range(BUCKETS):
                gather(G[2][:, b * P:(b + 1) * P].bitcast(I32), io["dst_rows"], rowsel[:, b:b + 1], "ptr_rows")
            pool.wait_ge(S("items_ready"), 1)
            for c in range(IBLK):
                ix = item_i[:, IBLK + c:IBLK + c + 1]
                gather(G[3][:, c * P:(c + 1) * P].bitcast(I32), io["dst_rows"], ix, "item_rows")
                gather(G[4][:, c * P:(c + 1) * P].bitcast(I32), io["src_rows"], ix, "item_rows")

            def gather_pass(n, table, pre=""):
                with pool.Fori(0, TURNS) as i:
                    for u in range(RING):
                        if u % HALF == 0:
                            hold(pool, S(pre + "idx_ready"), i * 2 + (2 * n * TURNS + u // HALF + 1))
                        gather(rows[:, u * P:(u + 1) * P], table, idx_ring[:, u:u + 1], f"{pre}row_in{u // GROUP}")

            def node_gather(dst, table, sem, width):
                for b in range(BUCKETS):
                    gather(dst[:, b * width:(b + 1) * width], table, end_i[:, b:b + 1], sem)

            alt = alt_flag(pool)
            for n in range(PASSES):
                with pool.If(alt > 0):
                    pool.wait_ge(S("alt_table_out"), 16 * (n + 1))
                    gather_pass(n, alt_tab, "alt_")
            pool.wait_ge(S("layer_done"), 2)
            for c in range(IBLK):
                gather(sh_rows[:, c * 512:(c + 1) * 512], io["ea4_rows"], item_i[:, IBLK + c:IBLK + c + 1], "sh_rows")
            pool.wait_ge(S("table_out"), 16)
            gather_pass(0, tabs[0])
            pool.wait_ge(S("run8_out"), 16)
            node_gather(aeloop8, run8_d, "aeloop_rows", 8)
            for g in range(2):
                pool.wait_ge(S("asrc_out"), 16 * (g + 1))
                with pool.Fori(0, ZTURNS // 2) as i:
                    for s in range(2):
                        hold(pool, S("zidx_ready"), i * 2 + (g * ZTURNS + s + 1))
                        for u in range(s * ZR, (s + 1) * ZR):
                            gather(zring[:, u * 4:(u + 1) * 4], asrc_d[g], idx_ring[:, u:u + 1], f"z_in{s}")
                pool.wait_ge(S("runmax_out"), 16 * (g + 1))
                node_gather(zmax, run4_d[2 * g], "zmax_rows", 4)
                pool.wait_ge(S("am"), g + 1)
                pool.wait_ge(S("seg_zeroed"), 16)
                for b in range(BUCKETS):
                    pool.indirect_dma_start(
                        seg_d, bass.IndirectOffsetOnAxis(start_i[:, b:b + 1], 0), am[:, b * 8:(b + 1) * 8], None,
                        bounds_check=EP - 1, oob_is_err=False).then_inc(S("seg_out"), 16)
                pool.wait_ge(S("runsum_out"), 16 * (g + 1))
                node_gather(sseg, run4_d[2 * g + 1], "sseg_rows", 4)
                pool.wait_ge(S("p_out"), 16 * (g + 1))
                for c in range(IBLK):
                    gather(prob_rows[:, c * 512:(c + 1) * 512], p_d[g].rearrange("(t e) h -> t (e h)", e=P),
                           item_i[:, IBLK + c:IBLK + c + 1], "prob_rows")
                pool.wait_ge(S("table_out"), 16 * (2 + g))
                gather_pass(1 + g, tabs[1 + g])

        @block.tensor
        def _(pe):
            def dense(pairs, sem):
                for a, b in CHUNKS:
                    for k, (wt, x) in enumerate(pairs):
                        last = pe.matmul(ps[:, a:b], wt, x[:, a:b], start=(k == 0), stop=(k == len(pairs) - 1))
                last.then_inc(S(sem), 1)

            def turn(x, sem):
                for b in range(BUCKETS):
                    last = pe.transpose(ps[:, b * P:(b + 1) * P], x[:, b * P:(b + 1) * P], ident)
                last.then_inc(S(sem), 1)

            def item_turn(x, sem):
                for c in range(IBLK):
                    xc = x[:, c * 512:(c + 1) * 512].rearrange("p (e h) -> p h e", h=4)
                    for h in range(4):
                        k = 4 * c + h
                        last = pe.transpose(ps[:, k * P:(k + 1) * P], xc[:, h, :], ident)
                last.then_inc(S(sem), 1)

            def norm(xs, n):
                avg = ones[:, 0:P] if len(xs) == 1 else ones[:, P:2 * P]
                dense([(avg, x) for x, _ in xs], "norm_mean")
                pe.wait_ge(S("norm_sq"), n)
                dense([(avg, q) for _, q in xs], "norm_var")

            def small_turn(n, k):
                pe.wait_ge(S("scan_last"), n)
                pe.transpose(side[0:k, 0:P], small[:, 32:32 + k], ident).then_inc(S("scan_lastT"), 1)
                pe.wait_ge(S("scan_carry"), n)
                pe.transpose(side[:, 256:256 + k], carry[0:k, 0:P], ident[0:k, 0:k]).then_inc(S("scan_carryT"), 1)

            def gather_pass(n, m, by_node=False, pre=""):
                clear()
                with pe.Fori(0, TURNS) as i:
                    for u in range(RING):
                        b = pe.value_load(bk_row[0:1, bass.ds(i * RING + u, 1)], min_val=0, max_val=BUCKETS - 1)
                        if not by_node and u % GROUP == 0:
                            pe.wait_ge(S(f"{pre}row_in{u // GROUP}"), i * (16 * GROUP) + 16 * GROUP * (n * TURNS + 1))
                        pe.wait_ge(S(pre + "item_ready"), i * RING + (m * ITEMS_RUN + u + 1))
                        one, row = hot[:, u * P:(u + 1) * P], rows[:, u * P:(u + 1) * P]
                        lhs, rhs = (one, row) if by_node else (row, one)
                        pe.matmul(ps[:, bass.ds(b * P, P)], lhs, rhs, start=False, stop=False,
                                  skip_group_check=True).then_inc(S(pre + "item_done"), 1)

            def clear():
                for k in range(7):
                    last = pe.matmul(ps[:, k * 512:(k + 1) * 512], zeros[:], W[0:1, 0:512], start=True, stop=False,
                                     skip_group_check=True)
                return last

            def count_edges():
                clear()
                with pe.Fori(0, ITEMS_RUN // CRING) as i:
                    for u in range(CRING):
                        b = pe.value_load(bk_row[0:1, bass.ds(i * CRING + u, 1)], min_val=0, max_val=BUCKETS - 1)
                        pe.wait_ge(S("count_zeroed"), b + 1)
                        pe.wait_ge(S("count_ready"), i * CRING + (u + 1))
                        for k in range(BUCKETS):
                            last = pe.matmul(ps[:, k * P:(k + 1) * P], src_hot[:, u * NP + k * P:u * NP + (k + 1) * P],
                                             dst_hot[:, u * P:(u + 1) * P], start=False, stop=False,
                                             skip_group_check=True)
                        last.then_inc(S("count_done"), 1)

            def sum_rows(n, alt):
                with pe.If(alt > 0):
                    pe.wait_ge(S("y"), n + 1)
                    gather_pass(n, n, pre="alt_")
                with pe.Else():
                    for part, sem in ((0, "high_part"), (1, "middle_part"), (2, "low_part")):
                        pe.wait_ge(S(sem), n + 1)
                        for k in range(BUCKETS):
                            for a, b in CHUNKS:
                                pe.matmul(ps[:, a:b], parts16[part][:, k * P:(k + 1) * P], counts[:, k, a:b],
                                          start=(part == 0 and k == 0), stop=False, skip_group_check=True)

            pe.sem_inc(S("item_done"), RING)
            pe.sem_inc(S("alt_item_done"), RING)
            pe.sem_inc(S("count_done"), CRING)
            pe.wait_ge(S("loads"), 16 * LOADS)
            pe.wait_ge(S("keep_last"), 1)
            pe.transpose(side[0:8, 0:P], small[:, 32:40], ident).then_inc(S("keepT_ps"), 1)
            pe.wait_ge(S("item_f32"), 1)
            for k in range(2):
                for c in range(IBLK):
                    last = pe.transpose(ps[:, k * 1024 + c * P:k * 1024 + (c + 1) * P],
                                        G[3 + k][:, c * P:(c + 1) * P], ident)
            last.then_inc(S("itemsT"), 1)
            pe.wait_ge(S("itemsT_used"), 1)
            pe.wait_ge(S("item_in"), 16)
            count_edges()
            pe.wait_ge(S("over"), 1)
            pe.matmul(side[:, 0:1], ones[:, 0:P], over[:, BUCKETS:BUCKETS + 1], start=True, stop=True).then_inc(S("over_ps"), 1)
            alt = alt_flag(pe)
            pe.wait_ge(S("x_in"), 16)
            for n in range(2):
                turn(G[3] if n else xT, "y_ps")
                sum_rows(n, alt)
                pe.matmul(ps[:, 0:8], zeros[:], W[0:1, 0:8], start=False, stop=True,
                          skip_group_check=True).then_inc(S("agg_ps"), 1)
                pe.wait_ge(S("agg"), n + 1)
                dense([(w[f"wn{n + 1}"], G[2]), (w[f"ws{n + 1}"], G[3] if n else xT)], "lin")
                if n == 0:
                    pe.wait_ge(S("hid"), 1)
            pe.wait_ge(S("norm_in"), 1)
            norm([(xT, G[2])], 1)
            for k in range(4):
                pe.wait_ge(S("conv_in"), k + 1)
                for b in range(BUCKETS):
                    last = pe.matmul(ps[:, b * P:(b + 1) * P], (G[3] if k else xT)[:, b * P:(b + 1) * P], w[f"gcn{k}"],
                                     start=True, stop=True, skip_group_check=True)
                last.then_inc(S("y_ps"), 1)
                sum_rows(2 + k, alt)
                for b in range(BUCKETS):
                    last = pe.matmul(ps[:, b * P:(b + 1) * P], G[2][:, b * P:(b + 1) * P], ident, start=False,
                                     stop=(b == BUCKETS - 1), skip_group_check=True)
                last.then_inc(S("agg_ps"), 1)
            pe.wait_ge(S("norm_in"), 2)
            norm([(xT, G[2])], 2)
            pe.wait_ge(S("conv_in"), 5)
            dense([(w["wsc"], xT)], "lin")
            pe.wait_ge(S("scaled"), 1)
            dense([(w["wy"], xT)], "lin")
            pe.wait_ge(S("scaled"), 2)
            turn(G[2], "rowsT")
            pe.wait_ge(S("table_rows"), 1)
            pe.wait_ge(S("sh_rows"), 16 * IBLK)
            item_turn(sh_rows, "shT_ps")
            pe.wait_ge(S("shT"), 1)

            def hidden(i, k, u):
                if u % 4 == 0:
                    pe.wait_ge(S(f"ea_in{u // 4}"), i * 64 + 64)
                pe.wait_ge(S("silu"), k + 1)
                pe.matmul(ps[0:100, (u % 2) * 512:(u % 2) * 512 + P], wfc1[:], ea_ring[:, u * P:(u + 1) * P],
                          start=True, stop=True).then_inc(S("hid_ps"), 1)

            def edge_w(i, k, u):
                pe.wait_ge(S("silu"), k + 3)
                pe.wait_ge(S("msg"), k + 1)
                pe.matmul(ps[:, (2 + u % 2) * 512:(2 + u % 2) * 512 + P], hid_ring[:, (u % 4) * P:(u % 4 + 1) * P],
                          w["wfc2"][0:100, :], start=True, stop=True).then_inc(S("w_ps"), 1)

            def by_dest(i, k, u):
                pe.wait_ge(S("msg"), k + 3)
                pe.wait_ge(S("summed"), k + 1)
                o = (4 + u % 4) * 512
                for hf in range(2):
                    last = pe.matmul(ps[:, o + hf * P:o + (hf + 1) * P],
                                     msg_ring[:, (u % 4) * 256 + hf * P:(u % 4) * 256 + (hf + 1) * P],
                                     hot[:, u * P:(u + 1) * P], start=True, stop=True, skip_group_check=True)
                last.then_inc(S("sums_ps"), 1)

            def item_step(i, u, parts, first=False):
                for part, lag in parts:
                    if u >= lag:
                        part(i, i * RING + (u - lag), u - lag)
                    elif not first:
                        part(i - 1, i * RING + (u - lag), u - lag + RING)

            pe.sem_inc(S("hid_ps"), RING)
            pe.sem_inc(S("w_ps"), 4)
            pe.sem_inc(S("sums_ps"), 4)
            parts = [(hidden, 0), (edge_w, 1), (by_dest, 3)]
            for u in range(RING):
                item_step(0, u, parts, first=True)
            with pe.Fori(1, TURNS) as i:
                for u in range(RING):
                    item_step(i, u, parts)
            for u in range(3):
                item_step(TURNS, u, [x for x in parts if x[1] > u])
            pe.wait_ge(S("agg"), 3)
            dense([(w["walpha"], accA)], "lin")
            pe.wait_ge(S("scaled"), 3)
            dense([(w["wl2a"], accA), (w["wl2b"], accB)], "lin")
            pe.wait_ge(S("norm_in"), 3)
            norm([(G[5], G[2])], 3)
            pe.wait_ge(S("layer_done"), 3)
            pe.matmul(side[:, 0:2], ones[:, 0:P], small[:, 16:18], start=True, stop=True).then_inc(S("tw_mean"), 1)
            pe.wait_ge(S("tw_sqs"), 1)
            pe.matmul(side[:, 8:11], ones[:, 0:P], small[:, 22:25], start=True, stop=True).then_inc(S("tw_moments"), 1)
            pe.wait_ge(S("tw_cols"), 1)
            pe.transpose(side[0:3, 128:256], small[:, 29:32], ident).then_inc(S("tw_colsT"), 1)
            pe.wait_ge(S("taln"), 1)

            def tw_first(i, s, q):
                if q == 0:
                    pe.wait_ge(S(f"tw_in{s}"), i * 16 + 16)
                pe.wait_ge(S("tw_relu"), i * (2 * TW_STEPS) + (s * TW_STEPS + q + 1))
                a = s * ZR * P + q * TW_COLS
                pe.matmul(ps[:, (q % 2) * 512:(q % 2) * 512 + TW_COLS], taln, tw_ring[:, a:a + TW_COLS],
                          start=True, stop=True).then_inc(S("tw1"), 1)

            def tw_second(i, s, q):
                pe.wait_ge(S("tw_relu"), i * (2 * TW_STEPS) + (s * TW_STEPS + q + 3))
                pe.wait_ge(S("tw_tanh"), i * (2 * TW_STEPS) + (s * TW_STEPS + q + 1))
                pe.matmul(ps[:, (2 + q % 2) * 512:(2 + q % 2) * 512 + TW_COLS], w["taw2"],
                          tw_act[:, q * TW_COLS:(q + 1) * TW_COLS], start=True, stop=True).then_inc(S("tw2"), 1)

            def tw_third(i, s):
                pe.wait_ge(S("tw_tanh"), i * (2 * TW_STEPS) + (s * TW_STEPS + TW_STEPS + 2))
                pe.wait_ge(S("tw_copied"), i * 2 + (s + 1))
                for c in range(ZR):
                    last = pe.matmul(ps[:, (4 + s) * 512 + c * 8:(4 + s) * 512 + c * 8 + 8],
                                     tw_th[:, c * P:(c + 1) * P], attw[:], start=True, stop=True, skip_group_check=True)
                last.then_inc(S("tw3"), 1)

            def tw_turns(i, first):
                for s in range(2):
                    tw_first(i, s, 0)
                    tw_first(i, s, 1)
                    if s == 1:
                        tw_third(i, 0)
                    elif not first:
                        tw_third(i - 1, 1)
                    tw_second(i, s, 0)
                    tw_first(i, s, 2)
                    tw_second(i, s, 1)
                    tw_first(i, s, 3)
                    tw_second(i, s, 2)
                    tw_second(i, s, 3)

            pe.sem_inc(S("tw1"), 2 * TW_STEPS)
            pe.sem_inc(S("tw2"), TW_STEPS)
            pe.sem_inc(S("tw3"), 1)
            tw_turns(0, True)
            with pe.Fori(1, ZTURNS // 2) as i:
                tw_turns(i, False)
            tw_third(ZTURNS // 2 - 1, 1)
            small_turn(1, 8)
            dense([(w["ipw1a"], G[5])], "lin")
            pe.wait_ge(S("ip_hid"), 1)
            dense([(w["ipw1b"], G[5])], "lin")
            pe.wait_ge(S("ip_hid"), 2)
            norm([(G[0], G[2]), (G[1], G[3])], 4)
            pe.wait_ge(S("ip_norm"), 1)
            dense([(w["ipw2a"], G[0]), (w["ipw2b"], G[1])], "lin")
            pe.wait_ge(S("norm_in"), 4)
            norm([(G[0], G[2])], 5)
            for g in range(2):
                pe.wait_ge(S("gat_in"), g + 1)
                dense([(w[f"gw{g}"], G[0])], "lin")
                pe.wait_ge(S("gat_hT"), g + 1)
                for b in range(BUCKETS):
                    last = pe.matmul(side[:, b * 8:(b + 1) * 8], G[1][:, b * P:(b + 1) * P], att[:, 8 * g:8 * g + 8],
                                     start=True, stop=True, skip_group_check=True)
                last.then_inc(S("a8_ps"), 1)
                turn(G[1], "rowsT")
                pe.wait_ge(S("a8"), g + 1)
                small_turn(2 + 3 * g, 4)
                small_turn(3 + 3 * g, 8)
                small_turn(4 + 3 * g, 4)
                pe.wait_ge(S("prob_rows"), 16 * IBLK * (g + 1))
                pe.wait_ge(S("table_rows"), 2 + g)
                item_turn(prob_rows, "pT_ps")
                pe.wait_ge(S("pT"), g + 1)
                gather_pass(1 + g, g, by_node=True)
                pe.wait_ge(S("gat_rows"), g + 1)
                turn(G[2], "gatT")
                pe.wait_ge(S("norm_in"), 5 + g)
                norm([(G[0], G[2])], 6 + g)
            pe.wait_ge(S("norm_in"), 7)
            norm([(G[0], G[2])], 8)
            pe.wait_ge(S("layer_done"), 4)
            turn(G[0], "outT")

        @block.scalar
        def _(act):
            def norm(xs, n):
                act.wait_ge(S("norm_cent"), n)
                for x, q in xs:
                    last = nc.scalar.activation(q, x, ACT.Square)
                last.then_inc(S("norm_sq"), 1)
                act.wait_ge(S("norm_var"), n)
                nc.scalar.activation(xs[0][1], acc, ACT.Sqrt, bias=eps[:]).then_inc(S("norm_std"), 1)

            def rows_out(n):
                act.wait_ge(S("rowsT"), n)
                if n > 1:
                    act.wait_ge(S("table_out"), 16 * (n - 1))
                nc.scalar.copy(G[4], acc).then_inc(S("table_rows"), 1)

            act.wait_ge(S("deg"), 1)
            nc.scalar.activation(dinv, deg, ACT.Sqrt, bias=1.0).then_inc(S("sqrt_deg"), 1)
            act.sem_inc(S("count_zeroed"), 1)
            act.wait_ge(S("items_ready"), 1)
            for b in range(BUCKETS):
                if b < BUCKETS - 1:
                    last_item = act.value_load(thresh_i[0:1, b:b + 1], min_val=0, max_val=ITEMS)
                    hold(act, S("count_done"), last_item + (CRING + 1))
                else:
                    act.wait_ge(S("count_done"), ITEMS_RUN + CRING)
                column = counts[:, :, b * P:(b + 1) * P]
                nc.scalar.activation(column, acc.rearrange("p (s d) -> p s d", d=P), ACT.Copy,
                                     saturate=True).then_inc(S("count_copied"), 1)
                act.wait_ge(S("count_copied"), b + 1)
                nc.scalar.activation(acc, acc, ACT.Copy, scale=0.0).then_inc(S("count_zeroed"), 1)
                if b:
                    act.wait_ge(S("over_seen"), b)
                nc.scalar.activation(over_junk.rearrange("p (s d) -> p s d", d=P), column, ACT.Relu, bias=small[:, 1:2],
                                     accum_out=over[:, b:b + 1]).then_inc(S("over_seen"), 1)
            alt = alt_flag(act)

            def split(n):
                with act.If(alt > 0):
                    act.sem_inc(S("holds"), 1)
                with act.Else():
                    act.wait_ge(S("y"), n + 1)
                    nc.scalar.copy(parts16[0], G[2]).then_inc(S("high_part"), 1)
                    act.wait_ge(S("rest"), n + 1)
                    nc.scalar.copy(parts16[1], rest).then_inc(S("middle_part"), 1)

            act.wait_ge(S("bias"), 1)
            for n in range(2):
                act.wait_ge(S("y_ps"), n + 1)
                nc.scalar.copy(G[2], acc).then_inc(S("y"), 1)
                split(n)
                if n == 0:
                    act.wait_ge(S("lin"), 1)
                    nc.scalar.activation(G[3], acc, ACT.Relu, bias=v["bn1"]).then_inc(S("hid"), 1)
            norm([(xT, G[2])], 1)
            for k in range(4):
                split(2 + k)
                if k < 3:
                    act.wait_ge(S("agg_conv"), k + 1)
                    nc.scalar.activation(G[3], G[2], ACT.Identity if k == 1 else ACT.Relu,
                                         bias=v[f"gb{k}"]).then_inc(S("conv_in"), 1)
            norm([(xT, G[2])], 2)
            rows_out(1)
            act.sem_inc(S("silu"), 2)
            with act.Fori(0, TURNS) as i:
                for u in range(RING):
                    act.wait_ge(S("hid_ps"), i * RING + (u + RING + 1))
                    act.wait_ge(S("w_ps"), i * RING + (u + 1))
                    nc.scalar.activation(hid_ring[:, (u % 4) * P:(u % 4 + 1) * P],
                                         ps[0:100, (u % 2) * 512:(u % 2) * 512 + P], ACT.Silu,
                                         scale=float(1 / np.sqrt(10.0))).then_inc(S("silu"), 1)
            norm([(G[5], G[2])], 3)
            act.wait_ge(S("tw_var"), 1)
            nc.scalar.activation(t_std, t_var, ACT.Sqrt, bias=eps[:]).then_inc(S("tw_std"), 1)
            act.sem_inc(S("tw_tanh"), 2)
            with act.Fori(0, ZTURNS) as i:
                for q in range(TW_STEPS):
                    act.wait_ge(S("tw2"), i * TW_STEPS + (q + TW_STEPS + 1))
                    act.wait_ge(S("tw3"), i + 1)
                    nc.scalar.activation(tw_th[:, q * TW_COLS:(q + 1) * TW_COLS],
                                         ps[:, (2 + q % 2) * 512:(2 + q % 2) * 512 + TW_COLS],
                                         ACT.Tanh, bias=v["tab2"]).then_inc(S("tw_tanh"), 1)
            act.wait_ge(S("lin"), 7)
            nc.scalar.activation(G[0], acc, ACT.Relu, bias=v["ipb1a"]).then_inc(S("ip_hid"), 1)
            act.wait_ge(S("lin"), 8)
            nc.scalar.activation(G[1], acc, ACT.Relu, bias=v["ipb1b"]).then_inc(S("ip_hid"), 1)
            norm([(G[0], G[2]), (G[1], G[3])], 4)
            norm([(G[0], G[2])], 5)
            for g in range(2):
                act.wait_ge(S("lin"), 10 + g)
                nc.scalar.copy(G[1], acc).then_inc(S("gat_hT"), 1)
                rows_out(2 + g)
                act.wait_ge(S("lp"), g + 1)
                nc.scalar.activation(ploop, ploop, ACT.Exp).then_inc(S("ploop"), 1)
                act.wait_ge(S("alpha"), g + 1)
                nc.scalar.activation(z, z, ACT.Exp).then_inc(S("prob"), 1)
                norm([(G[0], G[2])], 6 + g)
                act.wait_ge(S("elu_min"), g + 1)
                nc.scalar.activation(G[2], G[2], ACT.Exp).then_inc(S("elu_exp"), 1)
            norm([(G[0], G[2])], 8)
            act.wait_ge(S("outT"), 1)
            act.wait_ge(S("table_out"), 16 * 3)
            nc.scalar.copy(G[4], acc).then_inc(S("out_rows"), 1)

        @block.vector
        def _(dve):
            vec = nc.vector
            count = [0]

            def link(ins):
                count[0] += 1
                ins.then_inc(S("dve_link"), 1)
                dve.wait_ge(S("dve_link"), count[0])

            def wide(a, k):
                return a.unsqueeze(2).to_broadcast([P, a.shape[1], k])

            def cut(a, k):
                return a.rearrange("p (a b) -> p a b", b=k)

            vec.memset(zeros[:], 0.0)
            vec.memset(small[:, 1:2], -float(MOST))
            vec.memset(ones[:, 0:P], 1.0 / P)
            vec.memset(ones[:, P:2 * P], 0.5 / P)
            vec.memset(eps[:], LN_EPS)
            link(vec.memset(small[:, 0:1], float(E)))
            dve.wait_ge(S("scan_loads"), 48)
            link(vec.tensor_copy(big[:, SLOT:SLOT + 3 * RUN], big[:, 0:3 * RUN].bitcast(I32)))
            prev, cur, first = (big[:, SLOT + i * RUN:SLOT + (i + 1) * RUN] for i in range(3))
            link(vec.tensor_tensor(keep[:], prev, cur, ALU.is_equal))
            link(vec.tensor_tensor_scan(still[:], keep[:], keep[:], 1.0, ALU.mult, ALU.mult))
            vec.tensor_copy(small[:, 32:40], still[:, RUN - 1:RUN].to_broadcast([P, 8])).then_inc(S("keep_last"), 1)
            dve.wait_ge(S("keepT_ps"), 1)
            link(vec.tensor_copy(keepT[:, 0:P], side[0:8, 0:P]))
            link(vec.tensor_scalar(keepT[:, P:2 * P], keepT[:, 0:P], 1.0, BIG, ALU.subtract, ALU.mult))
            dve.wait_ge(S("iotas"), 3)
            for b in range(BUCKETS):
                link(vec.tensor_scalar(hot[:, 0:RUN], first, nodeid[:, b:b + 1], None, ALU.is_lt, ALU.add,
                                       accum_out=cnt[:, b:b + 1]))
            link(vec.tensor_scalar(cnt, cnt, 1.0, 0.0, ALU.subtract, ALU.max))
            vec.tensor_copy(rowsel, cnt).then_inc(S("rowsel_ready"), 1)
            dve.wait_ge(S("ptr_rows"), 16 * BUCKETS)
            link(vec.tensor_copy(G[3], G[2].bitcast(I32)))
            link(vec.tensor_tensor(cut(G[3], P), cut(G[3], P), wide(nodeid, P), ALU.is_lt))
            link(vec.tensor_reduce(deg, cut(G[3], P), AX, ALU.add))
            vec.scalar_tensor_tensor(rowptr, cnt, float(P), deg, ALU.mult, ALU.add).then_inc(S("rowptr_ready"), 1)
            dve.wait_ge(S("rowptr_ready"), 1)
            dve.wait_ge(S("rp_in"), 32)
            vec.tensor_tensor(deg, nextptr, rowptr, ALU.subtract).then_inc(S("deg"), 1)
            dve.wait_ge(S("deg"), 1)
            link(vec.tensor_scalar(invdeg, deg, 1.0, None, ALU.max))
            link(vec.reciprocal(invdeg, invdeg))
            link(vec.tensor_scalar(has, deg, 1.0, None, ALU.min))
            link(vec.tensor_scalar(cnt, nextptr, 1.0, 0.0, ALU.subtract, ALU.max))
            link(vec.tensor_copy(end_i, cnt))
            link(vec.tensor_scalar(cnt, has, 1.0, -FAR, ALU.subtract, ALU.mult))
            link(vec.tensor_tensor(cnt, cnt, rowptr, ALU.add))
            link(vec.tensor_copy(start_i, cnt))
            dve.wait_ge(S("sqrt_deg"), 1)
            vec.reciprocal(dinv, dinv).then_inc(S("nodevec_ready"), 1)
            th = thresh[:, 0:BUCKETS - 1]
            link(vec.tensor_copy(thresh_i[:], th))
            link(vec.tensor_scalar(thresh_i[:], thresh_i[:], 7, None, ALU.arith_shift_right))
            link(vec.tensor_copy(th, thresh_i[:]))
            link(vec.tensor_tensor(th, th, iota[:, 0:BUCKETS - 1], ALU.add))
            link(vec.tensor_copy(thresh_i[:], th))
            item_n, item_b, item_t, item_off = (item_f[:, i * IBLK:(i + 1) * IBLK] for i in range(4))
            past = cut(hot[:, 0:IBLK * (BUCKETS - 1)], BUCKETS - 1)
            link(vec.tensor_tensor(past, th.unsqueeze(1).to_broadcast([P, IBLK, BUCKETS - 1]),
                                   wide(item_n, BUCKETS - 1), ALU.is_lt))
            link(vec.tensor_reduce(item_b, past, AX, ALU.add))
            link(vec.tensor_tensor(item_t, item_n, item_b, ALU.subtract))
            link(vec.tensor_scalar(item_t, item_t, float(TILES - 1), None, ALU.min))
            link(vec.tensor_copy(item_i[:, 0:IBLK], item_b))
            vec.tensor_copy(item_i[:, IBLK:2 * IBLK], item_t).then_inc(S("items_ready"), 1)
            link(vec.tensor_scalar(item_off, item_n, float(ITEMS - 1), FAR, ALU.is_gt, ALU.mult))
            link(vec.scalar_tensor_tensor(item_off, item_b, float(P), item_off, ALU.mult, ALU.add))
            dve.wait_ge(S("item_rows"), 16 * 2 * IBLK)
            link(vec.tensor_copy(G[3][:, 0:IPAD], G[3][:, 0:IPAD].bitcast(I32)))
            link(vec.tensor_copy(G[4][:, 0:IPAD], G[4][:, 0:IPAD].bitcast(I32)))
            vec.tensor_tensor(cut(G[3][:, 0:IPAD], P), cut(G[3][:, 0:IPAD], P), wide(item_off, P),
                              ALU.subtract).then_inc(S("item_f32"), 1)
            dve.wait_ge(S("item_f32"), 1)
            dve.sem_inc(S("slots_free"), 1)
            dve.wait_ge(S("itemsT"), 1)
            vec.tensor_copy(dloc[:], ps[:, 0:IPAD])
            vec.tensor_scalar(src_f, ps[:, 1024:1024 + IPAD], float(MID), None, ALU.subtract)
            vec.tensor_copy(srcI[:], ps[:, 1024:1024 + IPAD]).then_inc(S("itemsT_used"), 1)
            dve.wait_ge(S("itemsT_used"), 1)
            dve.wait_ge(S("node_iota"), 1)
            link(vec.tensor_copy(node_iota16, node_iota))
            with dve.Fori(0, ITEMS_RUN // CRING) as i:
                for u in range(CRING):
                    dve.wait_ge(S("count_done"), i * CRING + (u + 1))
                    vec.tensor_scalar(src_hot[:, u * NP:(u + 1) * NP], node_iota16,
                                      src_f[:, bass.ds(i * CRING + u, 1)], None, ALU.is_equal)
                    vec.tensor_scalar(dst_hot[:, u * P:(u + 1) * P], iota[:], dloc[:, bass.ds(i * CRING + u, 1)], None,
                                      ALU.is_equal).then_inc(S("count_ready"), 1)
            dve.wait_ge(S("over_seen"), BUCKETS)
            vec.tensor_reduce(over[:, BUCKETS:BUCKETS + 1], over[:, 0:BUCKETS], AX, ALU.add).then_inc(S("over"), 1)
            dve.wait_ge(S("over_ps"), 1)
            vec.tensor_scalar(flag[:], side[0:1, 0:1], 0.0, None, ALU.is_gt).then_inc(S("flag"), 1)
            alt = alt_flag(dve)

            def item_columns(dst, sem, n):
                vec.tensor_copy(dst.rearrange("p (c k h) -> p c h k", c=IBLK, h=4),
                                ps[:, 0:4 * IPAD].rearrange("p (c h k) -> p c h k", c=IBLK, h=4)).then_inc(S(sem), 1)
                dve.wait_ge(S(sem), n)

            dve.wait_ge(S("loads"), 16 * LOADS)
            link(vec.tensor_scalar(w["wfc2"], w["wfc2"], 0.1, None, ALU.mult))
            link(vec.tensor_scalar(w["wfc2"][:, MUL:2 * MUL], w["wfc2"][:, MUL:2 * MUL], float(1 / np.sqrt(3.0)),
                                   None, ALU.mult))
            link(vec.tensor_tensor(v["bn2"], v["bn2"], v["bs2"], ALU.add))
            vec.tensor_tensor(v["bn1"], v["bn1"], v["bs1"], ALU.add).then_inc(S("bias"), 1)

            def indices(i, u, pre=""):
                vec.tensor_copy(idx_ring[:, u:u + HALF],
                                srcI[:, bass.ds(i * RING + u, HALF)]).then_inc(S(pre + "idx_ready"), 1)

            def one_hot(i, u):
                return vec.tensor_scalar(hot[:, u * P:(u + 1) * P], iota[:], dloc[:, bass.ds(i * RING + u, 1)], None,
                                         ALU.is_equal)

            def passed(m):
                dve.wait_ge(S("item_done"), RING + (m + 1) * ITEMS_RUN)

            def sum_rows(n):
                with dve.If(alt > 0):
                    with dve.Fori(0, TURNS) as i:
                        for u in range(RING):
                            if u % HALF == 0:
                                hold(dve, S("alt_item_done"), i * RING + (n * ITEMS_RUN + u + HALF))
                                indices(i, u, "alt_")
                            one_hot(i, u).then_inc(S("alt_item_ready"), 1)
                with dve.Else():
                    dve.wait_ge(S("high_part"), n + 1)
                    vec.tensor_tensor(rest, G[2], parts16[0], ALU.subtract).then_inc(S("rest"), 1)
                    dve.wait_ge(S("middle_part"), n + 1)
                    vec.tensor_tensor(parts16[2], rest, parts16[1], ALU.subtract).then_inc(S("low_part"), 1)
                dve.wait_ge(S("agg_ps"), n + 1)

            def weighted_pass(n, m):
                def turn_(i, first):
                    for u in range(RING + (HALF if i is TURNS else 0)):
                        if i is not TURNS and u % HALF == 0:
                            hold(dve, S("item_done"), i * RING + (m * ITEMS_RUN + u + HALF))
                            indices(i, u)
                        if i is not TURNS:
                            one_hot(i, u)
                        if u >= HALF:
                            weigh(i, i * RING + (u - HALF), u - HALF)
                        elif not first:
                            weigh(i - 1, i * RING + (u - HALF), u + HALF)

                def weigh(i, k, u):
                    row = rows[:, u * P:(u + 1) * P]
                    if u % GROUP == 0:
                        dve.wait_ge(S(f"row_in{u // GROUP}"), i * (16 * GROUP) + 16 * GROUP * (n * TURNS + 1))
                    vec.tensor_tensor(cut(row, C), cut(row, C), wide(pT[:, bass.ds(k * 4, 4)], C),
                                      ALU.mult).then_inc(S("item_ready"), 1)

                turn_(0, True)
                with dve.Fori(1, TURNS) as i:
                    turn_(i, False)
                for u in range(HALF):
                    weigh(TURNS - 1, TURNS * RING + u - HALF, u + HALF)
                passed(m)

            def norm(xs, n):
                dve.wait_ge(S("norm_mean"), n)
                for x, q in xs:
                    last = vec.tensor_tensor(x, x, acc, ALU.subtract)
                last.then_inc(S("norm_cent"), 1)
                dve.wait_ge(S("norm_std"), n)
                link(vec.reciprocal(xs[0][1], xs[0][1]))
                for x, q in xs:
                    link(vec.tensor_tensor(x, x, xs[0][1], ALU.mult))

            dve.wait_ge(S("nodevec_in"), 16)
            for n in range(2):
                sum_rows(n)
                vec.tensor_tensor(G[2], acc, deg_bc, ALU.mult).then_inc(S("agg"), 1)
            dve.wait_ge(S("lin"), 2)
            vec.scalar_tensor_tensor(xT, acc, v["bn2"], xT, ALU.add, ALU.add).then_inc(S("norm_in"), 1)
            norm([(xT, G[2])], 1)
            dve.sem_inc(S("layer_done"), 1)
            dve.sem_inc(S("conv_in"), 1)
            dve.wait_ge(S("nodevec_in"), 32)
            for k in range(4):
                dve.wait_ge(S("y_ps"), 3 + k)
                vec.tensor_tensor(cut(G[2], P), cut(acc, P), wide(dinv, P), ALU.mult).then_inc(S("y"), 1)
                sum_rows(2 + k)
                vec.tensor_tensor(G[2], acc, deg_bc, ALU.mult).then_inc(S("agg_conv"), 1)
            dve.wait_ge(S("agg_conv"), 4)
            vec.scalar_tensor_tensor(xT, G[2], v["gb3"], xT, ALU.add, ALU.add).then_inc(S("norm_in"), 1)
            norm([(xT, G[2])], 2)
            dve.sem_inc(S("layer_done"), 1)
            dve.sem_inc(S("conv_in"), 1)
            dve.wait_ge(S("nodevec_in"), 48)
            dve.wait_ge(S("attr_in"), 16)
            dve.wait_ge(S("lin"), 3)
            vec.scalar_tensor_tensor(scT, acc, INV, attr_bc, ALU.mult, ALU.mult).then_inc(S("scaled"), 1)
            dve.wait_ge(S("lin"), 4)
            vec.scalar_tensor_tensor(G[2], acc, INV, attr_bc, ALU.mult, ALU.mult).then_inc(S("scaled"), 1)
            dve.wait_ge(S("shT_ps"), 1)
            item_columns(shT, "shT", 1)
            link(vec.memset(accAB, 0.0))

            def messages(i, k, u):
                row = rows[:, u * P:(u + 1) * P]
                y0, y1 = row[:, 0:MUL], cut(row[:, MUL:P], MUL)
                o = (2 + u % 2) * 512
                w00, w11, w01, w10 = (ps[:, o + j * MUL:o + (j + 1) * MUL] for j in range(4))
                msg = msg_ring[:, (u % 4) * 256:(u % 4 + 1) * 256]
                m00, m11, m01, m10 = msg[:, 0:32], msg[:, 32:64], cut(msg[:, 64:160], MUL), cut(msg[:, 160:256], MUL)
                tmp = mul_tmp[:, (u % 2) * 160:(u % 2 + 1) * 160]
                dot, t01, d = cut(tmp[:, 0:96], MUL), tmp[:, 96:128], tmp[:, 128:160]
                sh0 = shT[:, bass.ds(k * 4, 1)]
                sh1 = wide(shT[:, bass.ds(k * 4 + 1, 3)], MUL)
                if u % GROUP == 0:
                    dve.wait_ge(S(f"row_in{u // GROUP}"), i * (16 * GROUP) + 16 * GROUP)
                vec.tensor_tensor(dot, y1, sh1, ALU.mult).then_inc(S("prod"), 1)
                dve.wait_ge(S("w_ps"), k + 5)
                vec.tensor_tensor(t01, w01, y0, ALU.mult).then_inc(S("prod"), 1)
                dve.wait_ge(S("sums_ps"), k + 1)
                vec.scalar_tensor_tensor(m00, y0, sh0, w00, ALU.mult, ALU.mult)
                vec.scalar_tensor_tensor(m10, y1, sh0, w10.unsqueeze(1).to_broadcast([P, 3, MUL]), ALU.mult, ALU.mult)
                dve.wait_ge(S("prod"), k * 3 + 1)
                vec.tensor_reduce(d, tmp[:, 0:96].rearrange("p (c u) -> p u c", c=3), AX,
                                  ALU.add).then_inc(S("prod"), 1)
                dve.wait_ge(S("prod"), k * 3 + 3)
                vec.tensor_tensor(m01, t01.unsqueeze(1).to_broadcast([P, 3, MUL]), sh1, ALU.mult)
                vec.tensor_tensor(m11, d, w11, ALU.mult).then_inc(S("msg"), 1)

            def add_up(i, k, u):
                b = dve.value_load(bk_row[0:1, bass.ds(k, 1)], min_val=0, max_val=BUCKETS - 1)
                dst = accAB.rearrange("p (h n) -> p h n", h=2)[:, :, bass.ds(b * P, P)]
                o = (4 + u % 4) * 512
                dve.wait_ge(S("sums_ps"), k + 5)
                dve.wait_ge(S("summed"), k + 4)
                vec.tensor_tensor(dst, dst, cut(ps[:, o:o + 256], P), ALU.add).then_inc(S("summed"), 1)

            def l2_step(i, u, first=False, last=False):
                if not last:
                    if u % HALF == 0:
                        indices(i, u)
                    one_hot(i, u)
                for part, lag in ((messages, HALF), (add_up, HALF + 2)):
                    if u >= lag:
                        if not last:
                            part(i, i * RING + (u - lag), u - lag)
                    elif not first:
                        part(i - 1, i * RING + (u - lag), u - lag + RING)

            dve.sem_inc(S("msg"), 2)
            dve.sem_inc(S("summed"), 4)
            for u in range(RING):
                l2_step(0, u, first=True)
            with dve.Fori(1, TURNS) as i:
                for u in range(RING):
                    l2_step(i, u)
            for u in range(HALF + 2):
                l2_step(TURNS, u, last=True)
            dve.wait_ge(S("summed"), ITEMS_RUN + 4)
            vec.tensor_tensor(accAB.rearrange("p (h n) -> p h n", h=2), accAB.rearrange("p (h n) -> p h n", h=2),
                              deg_bc.unsqueeze(1).to_broadcast([P, 2, NP]), ALU.mult).then_inc(S("agg"), 1)
            dve.wait_ge(S("lin"), 5)
            vec.scalar_tensor_tensor(G[2], acc, INV2, attr_bc, ALU.mult, ALU.mult).then_inc(S("scaled"), 1)
            dve.wait_ge(S("lin"), 6)
            link(vec.scalar_tensor_tensor(G[3], acc, INV2, attr_bc, ALU.mult, ALU.mult))
            link(vec.tensor_tensor(G[3], G[3], G[2], ALU.mult))
            link(vec.tensor_tensor(G[3], G[3], scT, ALU.add))
            vec.tensor_tensor(G[5], xT, G[3], ALU.add).then_inc(S("norm_in"), 1)
            norm([(G[5], G[2])], 3)
            dve.sem_inc(S("layer_done"), 1)
            dve.wait_ge(S("tw_mean"), 1)
            w1b1, lnw = small[:, 20:22], small[:, 18:19]
            link(vec.tensor_tensor(w1b1, small[:, 16:18], side[:, 0:2], ALU.subtract))
            vec.tensor_tensor(small[:, 22:24], w1b1, w1b1[:, 0:1].to_broadcast([P, 2]), ALU.mult)
            vec.tensor_tensor(small[:, 24:25], w1b1[:, 1:2], w1b1[:, 1:2], ALU.mult).then_inc(S("tw_sqs"), 1)
            dve.wait_ge(S("tw_moments"), 1)
            link(vec.tensor_copy(small[:, 25:28], side[:, 8:11]))
            link(vec.tensor_scalar(small[:, 28:29], small[:, 26:27], 2.0, None, ALU.mult))
            vec.tensor_tensor(small[:, 29:31], w1b1, lnw.to_broadcast([P, 2]), ALU.mult)
            vec.tensor_copy(small[:, 31:32], small[:, 19:20]).then_inc(S("tw_cols"), 1)
            dve.wait_ge(S("tw_colsT"), 1)
            link(vec.tensor_copy(taln, side[0:3, 128:256]))
            dve.wait_ge(S("ew_in"), 48)
            link(vec.tensor_tensor(edgew[:, 0:2 * D], edgew[:, 0:2 * D], edgew[:, 2 * D:4 * D], ALU.mult))
            vec.tensor_reduce(attw[:], cut(edgew[:, 0:2 * D], C), AX, ALU.add).then_inc(S("taln"), 1)
            link(vec.tensor_scalar(t_var, t_time, small[:, 25:26], small[:, 28:29], ALU.mult, ALU.add))
            link(vec.tensor_tensor(t_var, t_var, t_time, ALU.mult))
            vec.tensor_scalar(t_var, t_var, small[:, 27:28], 0.0, ALU.add, ALU.max).then_inc(S("tw_var"), 1)
            dve.wait_ge(S("tw_std"), 1)
            vec.memset(t_one, 1.0)
            link(vec.reciprocal(t_r, t_std))
            vec.tensor_tensor(t_tr, t_time, t_r, ALU.mult).then_inc(S("tw_rows"), 1)

            def tw_relu(i, s, q):
                n = i * (2 * TW_STEPS) + (s * TW_STEPS + q)
                dve.wait_ge(S("tw1"), n + (2 * TW_STEPS + 1))
                dve.wait_ge(S("tw2"), n + 1)
                vec.tensor_scalar(tw_act[:, q * TW_COLS:(q + 1) * TW_COLS],
                                  ps[:, (q % 2) * 512:(q % 2) * 512 + TW_COLS], 0.0, None, ALU.max).then_inc(S("tw_relu"), 1)

            def tw_copy(i, s):
                hold(dve, S("tw3"), i * 2 + (s + 2))
                vec.tensor_copy(ae[:, bass.ds((i * 2 + s) * (ZR * 8), ZR * 8)],
                                ps[:, (4 + s) * 512:(4 + s) * 512 + ZR * 8]).then_inc(S("tw_copied"), 1)

            def tw_turns(i, first):
                for s in range(2):
                    tw_relu(i, s, 0)
                    tw_relu(i, s, 1)
                    if s == 1:
                        tw_copy(i, 0)
                    elif not first:
                        tw_copy(i - 1, 1)
                    tw_relu(i, s, 2)
                    tw_relu(i, s, 3)

            dve.sem_inc(S("tw_relu"), 2)
            dve.sem_inc(S("tw_copied"), 2)
            tw_turns(0, True)
            with dve.Fori(1, ZTURNS // 2) as i:
                tw_turns(i, False)
            tw_copy(ZTURNS // 2 - 1, 1)
            dve.wait_ge(S("tw_copied"), ZTURNS + 2)

            scans = [0]

            def across(dst, k, penal, op0, op1, init):
                scans[0] += 1
                n = scans[0]
                link(vec.memset(carry[:, 0:1], init))
                vec.tensor_copy(small[:, 32:32 + k], dst[:, RUN - 1, 0:k]).then_inc(S("scan_last"), 1)
                dve.wait_ge(S("scan_lastT"), n)
                vec.tensor_tensor_scan(carry[0:k, 1:P + 1], keepT[0:k, (P if penal else 0):(2 * P if penal else P)],
                                       side[0:k, 0:P], init, op0, op1).then_inc(S("scan_carry"), 1)
                dve.wait_ge(S("scan_carryT"), n)
                link(vec.tensor_copy(carry_in[:, 0:k], side[:, 256:256 + k]))
                for h in range(k):
                    last = vec.scalar_tensor_tensor(dst[:, :, h], pen_still if penal else still[:],
                                                    carry_in[:, h:h + 1], dst[:, :, h], op0, op1)
                return last

            vec.memset(fillw, 0.0).then_inc(S("fill_zero"), 1)
            dve.wait_ge(S("seg_zeroed"), 16)
            for h in range(8):
                last = vec.tensor_tensor_scan(fill_v[:, :, h], keep[:], ae_v[:, :, h], 0.0, ALU.mult, ALU.add)
            link(last)
            across(fill_v, 8, False, ALU.mult, ALU.add, 0.0).then_inc(S("run8"), 1)
            norm([(G[0], G[2]), (G[1], G[3])], 4)
            vec.tensor_scalar(G[0], G[0], v["lnwa"], v["lnba"], ALU.mult, ALU.add)
            vec.tensor_scalar(G[1], G[1], v["lnwb"], v["lnbb"], ALU.mult, ALU.add).then_inc(S("ip_norm"), 1)
            dve.wait_ge(S("lin"), 9)
            vec.tensor_scalar(G[0], acc, v["ipb2"], None, ALU.add).then_inc(S("norm_in"), 1)
            norm([(G[0], G[2])], 5)
            link(vec.tensor_scalar(G[0], G[0], v["pnw"], v["pnb"], ALU.mult, ALU.add))
            link(vec.tensor_copy(G[3], G[5]))
            vec.tensor_scalar(G[0], G[0], 0.0, 10.0, ALU.max, ALU.min).then_inc(S("gat_in"), 1)
            dve.wait_ge(S("aeloop_rows"), 16 * BUCKETS)
            link(vec.tensor_tensor(cut(aeloop8, 8), cut(aeloop8, 8), wide(invdeg, 8), ALU.mult))
            link(vec.tensor_tensor(cut(aeloop8, 8), cut(aeloop8, 8), wide(has, 8), ALU.mult))
            for g in range(2):
                a8v, loop8 = cut(a8, 8), cut(aeloop8, 8)
                asrc, adst, aloop = a8v[:, :, 0:4], a8v[:, :, 4:8], loop8[:, :, 4 * g:4 * g + 4]
                dve.wait_ge(S("a8_ps"), g + 1)
                vec.tensor_copy(a8, side[:, 0:8 * BUCKETS]).then_inc(S("a8"), 1)
                dve.wait_ge(S("a8"), g + 1)

                def z_take(i, s):
                    hold(dve, S(f"z_in{s}"), i * (16 * ZR) + 16 * ZR * (g * (ZTURNS // 2) + 1))
                    vec.tensor_copy(z[:, bass.ds((i * 2 + s) * (ZR * 4), ZR * 4)],
                                    zring[:, s * ZR * 4:(s + 1) * ZR * 4]).then_inc(S("z_taken"), 1)

                def z_index(i, s):
                    vec.tensor_copy(idx_ring[:, s * ZR:(s + 1) * ZR],
                                    src_scan[:, bass.ds((i * 2 + s) * ZR, ZR)]).then_inc(S("zidx_ready"), 1)

                for s in range(2):
                    z_index(0, s)
                with dve.Fori(1, ZTURNS // 2) as i:
                    for s in range(2):
                        z_take(i - 1, s)
                        z_index(i, s)
                for s in range(2):
                    z_take(ZTURNS // 2 - 1, s)
                dve.wait_ge(S("z_taken"), ZTURNS * (g + 1))
                link(vec.tensor_tensor(z_v, z_v, ae_v[:, :, 4 * g:4 * g + 4], ALU.add))
                link(vec.tensor_scalar(pen_keep, keep[:], 1.0, BIG, ALU.subtract, ALU.mult))
                link(vec.tensor_scalar(pen_still, still[:], 1.0, BIG, ALU.subtract, ALU.mult))
                for h in range(4):
                    last = vec.tensor_tensor_scan(run_v[:, :, h], pen_keep, z_v[:, :, h], -BIG, ALU.add, ALU.max)
                link(last)
                across(run_v, 4, True, ALU.add, ALU.max, -BIG).then_inc(S("runmax"), 1)
                zm, pl, sg, amv = cut(zmax, 4), cut(ploop, 4), cut(sseg, 4), cut(am, 8)
                link(vec.tensor_scalar(cnt, has, 1.0, BIG, ALU.subtract, ALU.mult))
                dve.wait_ge(S("zmax_rows"), 16 * BUCKETS * (g + 1))
                link(vec.tensor_tensor(zm, zm, wide(has, 4), ALU.mult))
                link(vec.tensor_tensor(zm, zm, wide(cnt, 4), ALU.add))
                link(vec.tensor_tensor(pl, asrc, aloop, ALU.add))
                link(vec.tensor_tensor(zm, zm, pl, ALU.max))
                link(vec.tensor_tensor(zm, zm, adst, ALU.add))
                link(vec.tensor_tensor(pl, pl, adst, ALU.add))
                link(vec.tensor_copy(amv[:, :, 0:4], adst))
                vec.scalar_tensor_tensor(amv[:, :, 4:8], zm, 0.2, zm, ALU.mult, ALU.max).then_inc(S("am"), 1)
                dve.wait_ge(S("am"), g + 1)
                link(vec.scalar_tensor_tensor(pl, pl, 0.2, pl, ALU.mult, ALU.max))
                vec.tensor_tensor(pl, pl, amv[:, :, 4:8], ALU.subtract).then_inc(S("lp"), 1)
                dve.wait_ge(S("seg_in"), 16 * (g + 1))
                for h in range(8):
                    last = vec.tensor_tensor_scan(fill_v[:, :, h], keep[:], fill_v[:, :, h], 0.0, ALU.mult, ALU.add)
                link(last)
                link(across(fill_v, 8, False, ALU.mult, ALU.add, 0.0))
                link(vec.tensor_tensor(z_v, z_v, fill_v[:, :, 0:4], ALU.add))
                link(vec.scalar_tensor_tensor(z, z, 0.2, z, ALU.mult, ALU.max))
                link(vec.tensor_tensor(z_v, z_v, fill_v[:, :, 4:8], ALU.subtract))
                vec.tensor_scalar(z, z, 0.0, None, ALU.min).then_inc(S("alpha"), 1)
                dve.wait_ge(S("prob"), g + 1)
                dve.wait_ge(S("runmax_out"), 16 * (g + 1))
                for h in range(4):
                    last = vec.tensor_tensor_scan(run_v[:, :, h], keep[:], z_v[:, :, h], 0.0, ALU.mult, ALU.add)
                link(last)
                across(run_v, 4, False, ALU.mult, ALU.add, 0.0).then_inc(S("runsum"), 1)
                dve.wait_ge(S("sseg_rows"), 16 * BUCKETS * (g + 1))
                dve.wait_ge(S("ploop"), g + 1)
                link(vec.tensor_tensor(sg, sg, wide(has, 4), ALU.mult))
                link(vec.tensor_tensor(sg, sg, pl, ALU.add))
                link(vec.tensor_scalar(sseg, sseg, 1e-16, None, ALU.add))
                link(vec.reciprocal(rs, sseg))
                dve.wait_ge(S("pT_ps"), g + 1)
                item_columns(pT, "pT", g + 1)
                weighted_pass(1 + g, g)
                link(vec.tensor_tensor(cut(G[2], C), cut(G[4], C), wide(ploop, C), ALU.mult))
                link(vec.tensor_tensor(G[2], G[2], acc, ALU.add))
                vec.tensor_tensor(cut(G[2], C), cut(G[2], C), wide(rs, C), ALU.mult).then_inc(S("gat_rows"), 1)
                dve.wait_ge(S("gatT"), g + 1)
                link(vec.scalar_tensor_tensor(G[0], acc, v[f"g{g + 1}b"], G[0], ALU.add, ALU.add))
                vec.tensor_scalar(G[0], G[0], 10.0, -10.0, ALU.min, ALU.max).then_inc(S("norm_in"), 1)
                norm([(G[0], G[2])], 6 + g)
                link(vec.tensor_scalar(G[0], G[0], v[f"n{g + 1}w"], v[f"n{g + 1}b"], ALU.mult, ALU.add))
                vec.tensor_scalar(G[2], G[0], 0.0, None, ALU.min).then_inc(S("elu_min"), 1)
                dve.wait_ge(S("elu_exp"), g + 1)
                link(vec.scalar_tensor_tensor(G[0], G[0], 0.0, G[2], ALU.max, ALU.add))
                last = vec.tensor_scalar(G[0], G[0], 1.0, None, ALU.subtract)
                if g == 0:
                    last.then_inc(S("gat_in"), 1)
                    dve.wait_ge(S("gat_in"), 2)
                else:
                    link(last)
            vec.tensor_tensor(G[0], G[0], G[3], ALU.add).then_inc(S("norm_in"), 1)
            norm([(G[0], G[2])], 8)
            dve.sem_inc(S("layer_done"), 1)


def layouts(x):
    def pad(a, *shape):
        out = np.zeros(shape, a.dtype)
        out[tuple(slice(0, n) for n in a.shape)] = a
        return out

    dst = np.full(EP + 1, NP, np.int32)
    dst[0] = -1
    dst[1:E + 1] = x["dst"]
    src = pad(x["src"], EP)
    w2 = "L2_gnn_W_"

    def blocks(w0, w1, rows0, rows1, cols0, cols1):
        out = np.zeros((P, P), np.float32)
        out[np.ix_(rows0, cols0)] = w0
        for c in range(3):
            out[np.ix_(rows1[c], cols1[c])] = w1
        return out

    u = np.arange(MUL)
    mixed = [MUL + 3 * u + c for c in range(3)]
    split = [MUL + MUL * c + u for c in range(3)]
    wl1 = x[w2 + "l2_1"]
    wl2a, wl2b = np.zeros((P, P), np.float32), np.zeros((P, P), np.float32)
    wl2a[np.ix_(np.arange(2 * MUL), u)] = x[w2 + "l2_0"]
    for c in range(3):
        at, to = (wl2a, 2 * MUL + MUL * c) if c < 2 else (wl2b, 0)
        at[np.ix_(to + u, mixed[c])] = wl1[:MUL]
        wl2b[np.ix_(MUL + MUL * c + u, mixed[c])] = wl1[MUL:]
    walpha = np.zeros((P, P), np.float32)
    walpha[:2 * MUL, :] = x[w2 + "alpha"]
    mats = {
        "wn1": x["L0_gnn_W_neigh1"].T, "ws1": x["L0_gnn_W_self1"].T,
        "wn2": x["L0_gnn_W_neigh2"].T, "ws2": x["L0_gnn_W_self2"].T,
        "wy": blocks(x[w2 + "l1_0"], x[w2 + "l1_1"], u, mixed, u, split),
        "wsc": blocks(x[w2 + "sc0"], x[w2 + "sc1"], u, mixed, u, mixed),
        "wl2a": wl2a, "wl2b": wl2b, "walpha": walpha, "wfc2": pad(x[w2 + "fc2"], P, P),
        "ipw1a": x["L3_gnn_ip_w1"][:, :P], "ipw1b": x["L3_gnn_ip_w1"][:, P:],
        "ipw2a": x["L3_gnn_ip_w2"][:P], "ipw2b": x["L3_gnn_ip_w2"][P:],
        "taw2": x["L3_gnn_ta_w2"], "gw0": x["L3_gnn_g1_w"], "gw1": x["L3_gnn_g2_w"], "ident": np.eye(P, dtype=np.float32),
    }
    for k in range(4):
        mats[f"gcn{k}"] = pad(x[f"L1_gnn_W{k + 1}"], P, P)
    vecs = {
        "bn1": x["L0_gnn_b_neigh1"], "bs1": x["L0_gnn_b_self1"], "bn2": x["L0_gnn_b_neigh2"], "bs2": x["L0_gnn_b_self2"],
        "ipb1a": x["L3_gnn_ip_b1"][:P], "ipb1b": x["L3_gnn_ip_b1"][P:], "lnwa": x["L3_gnn_ip_ln_w"][:P],
        "lnwb": x["L3_gnn_ip_ln_w"][P:], "lnba": x["L3_gnn_ip_ln_b"][:P], "lnbb": x["L3_gnn_ip_ln_b"][P:],
        "ipb2": x["L3_gnn_ip_b2"], "pnw": x["L3_gnn_pn_w"], "pnb": x["L3_gnn_pn_b"], "tab2": x["L3_gnn_ta_b2"],
        "g1b": x["L3_gnn_g1_b"], "g2b": x["L3_gnn_g2_b"], "n1w": x["L3_gnn_n1_w"], "n1b": x["L3_gnn_n1_b"],
        "n2w": x["L3_gnn_n2_w"], "n2b": x["L3_gnn_n2_b"],
    }
    for k in range(4):
        vecs[f"gb{k}"] = pad(x[f"L1_gnn_b{k + 1}"], P)
    att = np.zeros((P, 16), np.float32)
    for g in range(2):
        for j, name in enumerate(("src", "dst")):
            for h in range(HEADS):
                att[h * C:(h + 1) * C, 8 * g + 4 * j + h] = x[f"L3_gnn_g{g + 1}_att_{name}"][h]
    return {
        "xT": pad(x["x"], NP, D).T,
        "dst_ext": dst, "dst_rows": dst[1:].reshape(TILES, P), "dst_first": dst[1::P],
        "src_rows": src.reshape(TILES, P),
        "ea4_rows": pad(x["edge_attr_4"], EP, 4).reshape(TILES, 4 * P),
        "ea10T": pad(x["edge_attr_10"], EP, 10).T,
        "ew_jp": pad(x["edge_weight"], EP).reshape(P, RUN).T.reshape(-1),
        "attr": pad(x["node_vec1"], NP, 1).T,
        "weights": np.concatenate([mats[n] for n in WEIGHTS], axis=1),
        "vectors": np.stack([vecs[n] for n in VECS], axis=1),
        "wfc1": x[w2 + "fc1"], "att": att,
        "edgew": np.concatenate([x["L3_gnn_g1_ew"], x["L3_gnn_g2_ew"]], axis=1),
        "att_edge": np.concatenate([x["L3_gnn_g1_att_edge"].reshape(1, D), x["L3_gnn_g2_att_edge"].reshape(1, D)], axis=1),
        "ta_cols": np.stack([x["L3_gnn_ta_w1"][0], x["L3_gnn_ta_b1"], x["L3_gnn_ta_ln_w"], x["L3_gnn_ta_ln_b"]], axis=1),
    }


def kernel(**inputs):
    import concourse.bacc as bacc
    from concourse.bass_utils import run_bass_kernel_spmd

    arrays = {k: np.ascontiguousarray(a) for k, a in layouts({k: np.asarray(a) for k, a in inputs.items()}).items()}
    nc = bacc.Bacc("TRN2", target_bir_lowering=False, num_devices=1)
    io = {k: nc.dram_tensor(f"in_{k}", a.shape, mybir.dt.from_np(a.dtype), kind="ExternalInput").ap()
          for k, a in arrays.items()}
    out = nc.dram_tensor("out", [NP, D], F32, kind="ExternalOutput").ap()
    gnn_kernel(nc, io, out)
    r = run_bass_kernel_spmd(nc, [{f"in_{k}": a for k, a in arrays.items()}], core_ids=[0])
    return r.results[0]["out"][:N]
```

```python
from contextlib import ExitStack

import numpy as np
import concourse.bass as bass
from concourse import mybir

F32 = mybir.dt.float32
I32 = mybir.dt.int32
BF16 = mybir.dt.bfloat16
F16 = mybir.dt.float16
F8 = mybir.dt.float8e4
ALU = mybir.AluOpType
ACT = mybir.ActivationFunctionType
AX = mybir.AxisListType.X

P = 128
N = 3125
E = 103125
D = 128
MUL = 32
HEADS = 4
C = D // HEADS
BUCKETS = -(-N // P)
NP = BUCKETS * P
TILES = -(-E // P)
EP = TILES * P
RUN = TILES
ITEMS = TILES + BUCKETS - 1
RING = 16
TURNS = -(-ITEMS // RING)
ITEMS_RUN = TURNS * RING
IBLK = -(-ITEMS_RUN // P)
IPAD = IBLK * P
ZR = 13
ZTURNS = RUN // ZR
assert ZTURNS * ZR == RUN
ZLOOK = 42
ZHALF = ((0, 7), (7, ZR))
assert ZLOOK + ZLOOK // 2 - 1 == ZTURNS
BIG = 1e30
FAR = float(1 << 20)
LN_EPS = 1e-5
CHUNKS = [(c, min(c + 512, NP)) for c in range(0, NP, 512)]
TW_COLS = 416
TW_STEPS = ZR * P // TW_COLS
SLOT = 3232
MID = NP // 2
GROUP = 4
QUADS = RING // GROUP
CRING = 4
MOST = 15
CSPLIT = NP // 2
PASSES = 6
COUNTS = BUCKETS * NP // 4

WEIGHTS = ["wn1", "ws1", "wn2", "ws2", "gcn0", "gcn1", "gcn2", "gcn3", "wy", "wsc", "wl2a", "wl2b",
           "walpha", "wfc2", "ipw1a", "ipw1b", "ipw2a", "ipw2b", "taw2", "gw0", "gw1", "ident"]
VECS = ["bn1", "bs1", "bn2", "bs2", "gb0", "gb1", "gb2", "gb3", "ipb1a", "ipb1b", "lnwa", "lnwb", "lnba",
        "lnbb", "ipb2", "pnw", "pnb", "tab2", "g1b", "g2b", "n1w", "n1b", "n2w", "n2b"]


def gnn_kernel(nc, io, out):
    with ExitStack() as ctx:
        def sb(name, shape, dt=F32):
            return ctx.enter_context(nc.sbuf_tensor(name, shape, dt))

        sems = {}

        def S(name):
            if name not in sems:
                sems[name] = ctx.enter_context(nc.semaphore(name))
            return sems[name]

        def dram(name, shape, dt=F32):
            return nc.dram_tensor(name, shape, dt).ap()

        ps = ctx.enter_context(nc.psum_tensor("ps", [P, 8 * 512], F32))
        acc = ps[:, 0:NP]
        side = ps[:, 7 * 512:8 * 512]
        W = sb("weights", [P, len(WEIGHTS) * P])
        V = sb("vectors", [P, len(VECS)])
        w = {n: W[:, i * P:(i + 1) * P] for i, n in enumerate(WEIGHTS)}
        v = {n: V[:, i:i + 1] for i, n in enumerate(VECS)}
        ident = w["ident"]
        wfc1 = sb("wfc1", [P, 100])
        att = sb("att", [P, 16])
        attw = sb("attw", [P, 8])
        ones = sb("ones", [P, 2 * P])
        zeros = sb("zeros", [1, P], BF16)
        iota = sb("iota", [P, P])
        eps = sb("eps", [P, 1])
        mem = sb("mem", [P, 7 * SLOT + 20 * RUN])
        big = mem[:, 0:7 * SLOT]
        G = [big[:, i * SLOT:i * SLOT + NP] for i in range(7)]
        edge = mem[:, 7 * SLOT:7 * SLOT + 20 * RUN]
        fillw = edge[:, 0:8 * RUN]
        ae = edge[:, 8 * RUN:16 * RUN]
        z = edge[:, 16 * RUN:20 * RUN]
        dloc = sb("dloc", [P, IPAD])
        srcI = sb("srcI", [P, IPAD], I32)
        src_scan = sb("src_scan", [P, RUN], I32)
        keep = sb("keep", [P, RUN])
        still = sb("still", [P, RUN])
        bk_row = sb("bk_row", [1, ITEMS_RUN], I32)
        quad_row = sb("quad_row", [1, ITEMS_RUN // GROUP], I32)
        rings = sb("rings", [P, 2 * RING * P])
        rows = rings[:, 0:RING * P]
        hot = rings[:, RING * P:2 * RING * P]
        idx_ring = sb("idx_ring", [P, 2 * ZR], I32)
        node = sb("node", [P, 24 * BUCKETS])

        def nd(i, k=1):
            return node[:, i * BUCKETS:(i + k) * BUCKETS]

        nodeid, cnt, rowptr, nextptr, deg, invdeg, has, dinv = (nd(i) for i in range(8))
        a8, aeloop8 = nd(8, 8), nd(16, 8)
        nodei = sb("nodei", [P, 3 * BUCKETS], I32)
        rowsel, end_i, start_i = (nodei[:, i * BUCKETS:(i + 1) * BUCKETS] for i in range(3))
        gat = sb("gat", [P, 24 * BUCKETS])
        zmax, sseg, ploop, rs = (gat[:, 4 * i * BUCKETS:4 * (i + 1) * BUCKETS] for i in range(4))
        am = gat[:, 16 * BUCKETS:24 * BUCKETS]
        small = sb("small", [P, 48])
        over = gat[:, 0:BUCKETS + 1]
        quad_tile = gat[0:1, 4 * BUCKETS:4 * BUCKETS + ITEMS_RUN // GROUP].bitcast(I32)
        first_tiles = rings[0:1, 2 * IPAD - ITEMS_RUN:2 * IPAD].bitcast(I32)
        acc1 = ps[:, P:NP + P]
        flag = sb("flag", [1, 1], I32)
        item_f, thresh = rows[:, 0:8 * IBLK], rows[:, P:P + BUCKETS]
        item_i = sb("item_i", [P, 2 * IBLK], I32)
        thresh_i = sb("thresh_i", [P, BUCKETS - 1], I32)
        keepT = sb("keepT", [8, 2 * P])
        carry = hot[0:8, 0:P + 1]
        carry_in = sb("carry_in", [P, 8])

        rp_d = dram("rp_d", [NP + P])
        item_d = dram("item_d", [2, IPAD], I32)
        alt_tab = dram("alt_tab", [NP, D])
        nodevec_d = dram("nodevec_d", [2, NP])
        tabs = [dram(f"tab{i}", [NP, D]) for i in range(3)]
        seg_d = dram("seg_d", [EP, 8])
        run8_d = dram("run8_d", [EP, 8])
        run4_d = [dram(f"run4_{i}", [EP, 4]) for i in range(4)]
        p_d = [dram(f"p_{i}", [EP, 4]) for i in range(2)]
        asrc_d = dram("asrc", [NP, 4])
        tw_d = dram("tw_d", [3, EP])

        deg_bc, xT, attr_bc = G[0], G[1], G[5]
        tile_row = G[2][0:1, 0:IPAD].bitcast(I32)
        parts16 = [mem[:, 4 * SLOT + i * CSPLIT:4 * SLOT + (i + 1) * CSPLIT].bitcast(BF16) for i in range(3)]
        rest = rings[:, 0:NP]
        counts = mem[:, 7 * SLOT + 20 * RUN - COUNTS:7 * SLOT + 20 * RUN].bitcast(F8) \
            .rearrange("p (s d) -> p s d", s=BUCKETS)
        assert 4 * SLOT + 3 * CSPLIT <= 7 * SLOT + 20 * RUN - COUNTS
        src_hot = mem[:, 2 * SLOT:2 * SLOT + CRING * CSPLIT].bitcast(BF16)
        dst_hot = hot[:, 0:CRING * P // 2].bitcast(BF16)
        node_iota = G[5]
        node_iota16 = G[4][:, 0:CSPLIT].bitcast(F16)
        src_f = G[4][:, CSPLIT:CSPLIT + IPAD]
        over_junk = G[5][:, 0:CSPLIT].bitcast(BF16)
        tw_ring = big[:, SLOT:SLOT + 2 * ZR * P]
        tw_act, tw_th = big[:, SLOT + 2 * ZR * P:SLOT + 3 * ZR * P], G[6][:, 0:ZR * P]
        run = big[:, 5 * SLOT:5 * SLOT + 4 * RUN]
        pen_keep = big[:, 6 * SLOT:6 * SLOT + RUN]
        pen_still = big[:, 6 * SLOT + RUN:6 * SLOT + 2 * RUN]
        prob_rows = big[:, 5 * SLOT:5 * SLOT + IBLK * 512]
        ea_ring = big[:, 6 * SLOT:6 * SLOT + RING * P]
        sums, scT = edge[:, 0:2 * NP], edge[:, 2 * NP:3 * NP]
        sums_from_1 = mem[:, 7 * SLOT - 256:7 * SLOT + 2 * NP]
        alphaT, convT = edge[:, 0:NP], edge[:, NP:2 * NP]
        sh_rows = edge[:, 0:IBLK * 512]
        shT = edge[:, 3 * NP:3 * NP + 4 * IPAD]
        after = 3 * NP + 4 * IPAD
        msg_ring = edge[:, after:after + 2 * GROUP * 256]
        mul_tmp = edge[:, after + 2 * GROUP * 256:after + 2 * GROUP * 256 + GROUP * 192]
        assert after + 2 * GROUP * 256 + GROUP * 192 <= 20 * RUN
        slot6 = 6 * SLOT + RING * P
        hid_ring = big[0:100, slot6:slot6 + 2 * GROUP * P]
        w_ring = G[3][:, 0:2 * GROUP * P]
        dot_sum = big[:, slot6 + 2 * GROUP * P:slot6 + 2 * GROUP * P + GROUP * MUL]
        pT = edge[:, 0:4 * IPAD]
        zhot = big[:, SLOT:SLOT + ZR * P].bitcast(BF16)
        zhotT = big[:, SLOT + ZR * P:SLOT + 2 * ZR * P].bitcast(BF16)
        zwork = big[:, SLOT + 2 * ZR * P:3 * SLOT]
        zprod, zmask = zwork[:, 0:ZR * 4 * BUCKETS], zwork[:, 1300:1300 + ZR * BUCKETS]
        zsum, zrest = zwork[:, 1632:1632 + 4 * ZR], zwork[:, 1700:1800]
        ztab = zwork[:, 1800:1950].bitcast(BF16)
        ident16, iota16 = zwork[:, 1952:2016].bitcast(BF16), zwork[:, 2016:2080].bitcast(F16)
        src_low, src_high = G[6][:, 0:RUN], G[6][:, RUN:2 * RUN]
        zring = rows[:, 0:2 * ZR * 4]
        taln = rows[:, 4 * D:5 * D]
        edgew = rows[:, 0:4 * D]
        z_v, run_v = (a.rearrange("p (j h) -> p j h", h=4) for a in (z, run))
        fill_v, ae_v = (a.rearrange("p (j h) -> p j h", h=8) for a in (fillw, ae))
        t_time, t_tr, t_r, t_one, t_std, t_var = (fillw[:, i * RUN:(i + 1) * RUN] for i in range(6))
        LOADS = 6
        HALF = RING // 2
        INV, INV2 = float(1 / np.sqrt(MUL)), float(1 / np.sqrt(2 * MUL))

        def cut(a, k):
            return a.rearrange("p (a b) -> p a b", b=k)

        zhot_ps = [ps[:, s * 1024:s * 1024 + ZR * P // 2].bitcast(BF16) for s in range(2)]

        def z_candidates(a, b):
            return ps[:, (4 + a // 5) * 512 + (a % 5) * 100:(4 + a // 5) * 512 + (a % 5 + b - a) * 100]

        def z_steps(eng, parts, most, gathered=lambda i, s, take, give: None):
            def step(i, s, parts, first=False):
                for part, lag in parts:
                    if s >= lag:
                        part(i, i * 2 + (s - lag), (s - lag) % 2)
                    elif not first:
                        part(i - 1, i * 2 + (s - lag), (s - lag) % 2)

            last = ZLOOK // 2 - 1
            for s in range(2):
                step(0, s, parts, first=True)
                gathered(0, s, False, True)
            with eng.Fori(1, last) as i:
                for s in range(2):
                    step(i, s, parts)
                    gathered(i, s, True, True)
            for s in range(2):
                step(last, s, parts)
                gathered(last, s, True, False)
            for s in range(most):
                step(last + 1, s, [x for x in parts if x[1] > s])

        def pass_done(n):
            return n + 1 if n < 2 else 2 + len(CHUNKS) * (n - 1)

        def conv_chunk(k, c):
            return k * len(CHUNKS) + c + 1

        def norm_chunk(n, c):
            return (n - 1) * len(CHUNKS) + c + 1

        def sums_at(g, j):
            return (4 + 2 * (g % 2)) * 512 + j * 256

        def group_step(i, g, parts, first=False):
            for part, lag in parts:
                if g >= lag:
                    part(i, i * QUADS + (g - lag), g - lag)
                elif not first:
                    part(i - 1, i * QUADS + (g - lag), g - lag + QUADS)

        def hold(eng, sem, val):
            eng.wait_ge(sem, val)
            eng.sem_inc(S("holds"), 1)

        def alt_flag(eng):
            eng.wait_ge(S("flag"), 1)
            return eng.value_load(flag[0:1, 0:1], min_val=0, max_val=1)

        ctx.enter_context(nc.allow_non_contiguous_dma(reason="small node-major arrays"))
        block = ctx.enter_context(nc.Block())

        @block.sync
        def _(sp):
            def load(dst, src, sem="loads"):
                sp.dma_start(dst, src).then_inc(S(sem), 16)

            load(big[:, 0:RUN].bitcast(I32), io["dst_ext"][0:EP].rearrange("(p j) -> p j", p=P), "scan_loads")
            load(big[:, RUN:2 * RUN].bitcast(I32), io["dst_ext"][1:EP + 1].rearrange("(p j) -> p j", p=P), "scan_loads")
            load(big[:, 2 * RUN:3 * RUN].bitcast(I32), io["dst_first"].unsqueeze(0).to_broadcast([P, TILES]), "scan_loads")
            load(W[:], io["weights"])
            load(V[:], io["vectors"])
            load(src_scan[:], io["src_rows"].rearrange("t e -> (t e)").rearrange("(p j) -> p j", p=P))
            load(wfc1[:], io["wfc1"])
            load(att[:], io["att"])
            load(small[:, 16:20], io["ta_cols"])
            sp.wait_ge(S("rowptr_ready"), 1)
            sp.dma_start(rp_d[0:NP].rearrange("(b p) -> p b", p=P), rowptr).then_inc(S("rp_out"), 16)
            sp.dma_start(rp_d[NP:NP + P].rearrange("(p b) -> p b", p=P), small[:, 0:1]).then_inc(S("rp_out"), 16)
            sp.wait_ge(S("rp_out"), 32)
            load(nextptr, rp_d[1:NP + 1].rearrange("(b p) -> p b", p=P), "rp_in")
            load(thresh[:, 0:BUCKETS - 1], rp_d[P:NP].rearrange("(b p) -> b p", p=P)[:, 0]
                 .unsqueeze(0).to_broadcast([P, BUCKETS - 1]), "rp_in")
            sp.wait_ge(S("items_ready"), 1)
            for r in range(2):
                sp.dma_start(item_d[r].rearrange("(c p) -> p c", p=P),
                             item_i[:, r * IBLK:(r + 1) * IBLK]).then_inc(S("item_out"), 16)
            sp.wait_ge(S("item_out"), 32)
            load(bk_row[:], item_d[0:1, 0:ITEMS_RUN], "item_in")
            load(first_tiles, item_d[1:2, 0:ITEMS_RUN], "item_in")
            sp.wait_ge(S("nodevec_ready"), 1)
            sp.wait_ge(S("slots_free"), 1)
            sp.dma_start(nodevec_d[0].rearrange("(b p) -> p b", p=P), invdeg).then_inc(S("nodevec_out"), 16)
            sp.dma_start(nodevec_d[1].rearrange("(b p) -> p b", p=P), dinv).then_inc(S("nodevec_out"), 16)
            sp.wait_ge(S("nodevec_out"), 32)
            load(deg_bc, nodevec_d[0:1, :].to_broadcast([P, NP]), "nodevec_in")
            load(xT, io["xT"], "x_in")

            def store_table(i):
                sp.wait_ge(S("table_rows"), i)
                sp.dma_start(tabs[i - 1].rearrange("(b p) f -> p b f", p=P),
                             G[4].rearrange("p (b f) -> p b f", f=D)).then_inc(S("table_out"), 16)

            def alt_table(n):
                sp.wait_ge(S("y"), pass_done(n))
                sp.dma_start(alt_tab.rearrange("(b p) f -> p b f", p=P),
                             G[2].rearrange("p (b f) -> p b f", f=D)).then_inc(S("alt_table_out"), 16)

            alt = alt_flag(sp)
            for n in range(2):
                with sp.If(alt > 0):
                    alt_table(n)
            sp.wait_ge(S("agg"), 2)
            load(deg_bc, nodevec_d[1:2, :].to_broadcast([P, NP]), "nodevec_in")
            for n in range(2, PASSES):
                with sp.If(alt > 0):
                    alt_table(n)
            sp.wait_ge(S("layer_done"), 2)
            load(deg_bc, nodevec_d[0:1, :].to_broadcast([P, NP]), "nodevec_in")
            load(attr_bc, io["attr"].to_broadcast([P, NP]), "attr_in")
            store_table(1)
            load(tile_row, item_d[1:2, :], "item_in")
            sp.wait_ge(S("item_in"), 48)
            sp.wait_ge(S("scaled"), 1)
            with sp.Fori(0, TURNS) as i:
                for g in range(QUADS):
                    def features(u, columns):
                        sp.dma_start(ea_ring[0:10, u * P:(u + 1) * P], columns).then_inc(S(f"ea_in{g}"), 16)

                    first = sp.value_load(quad_tile[0:1, bass.ds(i * QUADS + g, 1)], min_val=0, max_val=TILES)
                    with sp.If(first > 0):
                        hold(sp, S("hid_ps"), i * QUADS + (g + 1))
                        for j in range(GROUP):
                            features(g * GROUP + j, io["ea10T"][:, bass.ds(first * P + j * P, P)])
                    with sp.Else():
                        hold(sp, S("hid_ps"), i * QUADS + (g + 1))
                        for j in range(GROUP):
                            t = sp.value_load(tile_row[0:1, bass.ds(i * RING + g * GROUP + j, 1)], min_val=0,
                                              max_val=TILES - 1)
                            features(g * GROUP + j, io["ea10T"][:, bass.ds(t * P + P, P)])
            sp.wait_ge(S("layer_done"), 3)
            load(t_time, io["ew_jp"].rearrange("(p j) -> p j", p=P), "ew_in")
            load(edgew[:, 0:2 * D], io["edgew"], "ew_in")
            load(edgew[:, 2 * D:4 * D], io["att_edge"].to_broadcast([P, 2 * D]), "ew_in")
            sp.wait_ge(S("tw_prep"), 5)
            for r, row in enumerate((t_tr, t_r, t_one)):
                sp.dma_start(tw_d[r].rearrange("(p j) -> p j", p=P), row).then_inc(S("tw_out"), 16)
            sp.wait_ge(S("tw_out"), 48)

            def store_gat(g):
                sp.wait_ge(S("a8"), g + 1)
                sp.dma_start(asrc_d.rearrange("(b p) h -> p b h", p=P),
                             a8.rearrange("p (b h) -> p b h", h=8)[:, :, 0:4]).then_inc(S("asrc_out"), 16)
                store_table(2 + g)

            store_gat(0)
            sp.wait_ge(S("zidx_ready"), 1)
            with sp.Fori(0, ZTURNS // 2) as i:
                for s in range(2):
                    sp.wait_ge(S("tw1"), i * (2 * TW_STEPS) + (s + 1) * TW_STEPS)
                    sp.dma_start(tw_ring[0:3, s * ZR * P:(s + 1) * ZR * P],
                                 tw_d[:, bass.ds((i * 2 + s) * (ZR * P), ZR * P)]).then_inc(S(f"tw_in{s}"), 16)
            sp.wait_ge(S("fill_zero"), 1)
            sp.dma_start(seg_d.rearrange("(p j) h -> p (j h)", p=P), fillw).then_inc(S("seg_zeroed"), 16)
            sp.wait_ge(S("run8"), 1)
            sp.dma_start(run8_d.rearrange("(p j) h -> p (j h)", p=P), fillw).then_inc(S("run8_out"), 16)
            for g in range(2):
                if g:
                    store_gat(1)
                sp.wait_ge(S("runmax"), g + 1)
                sp.dma_start(run4_d[2 * g].rearrange("(p j) h -> p (j h)", p=P), run).then_inc(S("runmax_out"), 16)
                sp.wait_ge(S("seg_out"), 16 * BUCKETS * (g + 1))
                sp.wait_ge(S("run8_out"), 16)
                load(fillw, seg_d.rearrange("(p j) h -> p (j h)", p=P), "seg_in")
                sp.wait_ge(S("prob"), g + 1)
                sp.dma_start(p_d[g].rearrange("(p j) h -> p (j h)", p=P), z).then_inc(S("p_out"), 16)
                sp.wait_ge(S("runsum"), g + 1)
                sp.dma_start(run4_d[2 * g + 1].rearrange("(p j) h -> p (j h)", p=P), run).then_inc(S("runsum_out"), 16)
            for c, (a, b) in enumerate(CHUNKS):
                sp.wait_ge(S("out_rows"), c + 1)
                sp.dma_start(out[a:b].rearrange("(b p) f -> p b f", p=P),
                             G[4][:, a:b].rearrange("p (b f) -> p b f", f=D)).then_inc(S("out_done"), 16)
            sp.wait_ge(S("out_done"), 16 * len(CHUNKS))

        @block.gpsimd
        def _(pool):
            pool.iota(iota[:], [[1, P]], base=0, channel_multiplier=0,
                      allow_small_or_imprecise_dtypes=True).then_inc(S("iotas"), 1)
            pool.iota(nodeid, [[P, BUCKETS]], base=0, channel_multiplier=1,
                      allow_small_or_imprecise_dtypes=True).then_inc(S("iotas"), 1)
            pool.iota(item_f[:, 0:IBLK], [[P, IBLK]], base=0, channel_multiplier=1,
                      allow_small_or_imprecise_dtypes=True).then_inc(S("iotas"), 1)

            pool.iota(node_iota, [[1, NP]], base=-MID, channel_multiplier=0,
                      allow_small_or_imprecise_dtypes=True).then_inc(S("node_iota"), 1)

            def gather(dst, table, index, sem):
                pool.indirect_dma_start(dst, None, table, bass.IndirectOffsetOnAxis(index, 0)).then_inc(S(sem), 16)

            pool.wait_ge(S("rowsel_ready"), 1)
            for b in range(BUCKETS):
                gather(G[2][:, b * P:(b + 1) * P].bitcast(I32), io["dst_rows"], rowsel[:, b:b + 1], "ptr_rows")
            pool.wait_ge(S("items_ready"), 1)
            for c in range(IBLK):
                ix = item_i[:, IBLK + c:IBLK + c + 1]
                gather(G[3][:, c * P:(c + 1) * P].bitcast(I32), io["dst_rows"], ix, "item_rows")
                gather(G[4][:, c * P:(c + 1) * P].bitcast(I32), io["src_rows"], ix, "item_rows")

            def gather_pass(n, table, pre=""):
                with pool.Fori(0, TURNS) as i:
                    for u in range(RING):
                        if u % HALF == 0:
                            hold(pool, S(pre + "idx_ready"), i * 2 + (2 * n * TURNS + u // HALF + 1))
                        gather(rows[:, u * P:(u + 1) * P], table, idx_ring[:, u:u + 1], f"{pre}row_in{u // GROUP}")

            def node_gather(dst, table, sem, width):
                for b in range(BUCKETS):
                    gather(dst[:, b * width:(b + 1) * width], table, end_i[:, b:b + 1], sem)

            alt = alt_flag(pool)
            for n in range(PASSES):
                with pool.If(alt > 0):
                    pool.wait_ge(S("alt_table_out"), 16 * (n + 1))
                    gather_pass(n, alt_tab, "alt_")
            pool.wait_ge(S("layer_done"), 2)
            for c in range(IBLK):
                gather(sh_rows[:, c * 512:(c + 1) * 512], io["ea4_rows"], item_i[:, IBLK + c:IBLK + c + 1], "sh_rows")
            pool.wait_ge(S("table_out"), 16)
            gather_pass(0, tabs[0])
            for g in range(2):
                if g == 0:
                    pool.wait_ge(S("asrc_out"), 16)
                    with pool.Fori(0, ZTURNS // 2) as i:
                        for s in range(2):
                            hold(pool, S("zidx_ready"), i * 2 + (s + 1))
                            for u in range(s * ZR, (s + 1) * ZR):
                                gather(zring[:, u * 4:(u + 1) * 4], asrc_d, idx_ring[:, u:u + 1], f"z_in{s}")
                    pool.wait_ge(S("run8_out"), 16)
                    node_gather(aeloop8, run8_d, "aeloop_rows", 8)
                else:
                    pool.wait_ge(S("asrc_out"), 32)
                    with pool.Fori(0, ZTURNS - ZLOOK) as i:
                        for s, (a, b) in enumerate(ZHALF):
                            hold(pool, S("zidx_ready"), i * 2 + (ZTURNS + s + 1))
                            for u in range(a, b):
                                gather(zring[:, u * 4:(u + 1) * 4], asrc_d, idx_ring[:, u:u + 1], f"z_in{s}")
                pool.wait_ge(S("runmax_out"), 16 * (g + 1))
                node_gather(zmax, run4_d[2 * g], "zmax_rows", 4)
                pool.wait_ge(S("am"), g + 1)
                pool.wait_ge(S("seg_zeroed"), 16)
                for b in range(BUCKETS):
                    pool.indirect_dma_start(
                        seg_d, bass.IndirectOffsetOnAxis(start_i[:, b:b + 1], 0), am[:, b * 8:(b + 1) * 8], None,
                        bounds_check=EP - 1, oob_is_err=False).then_inc(S("seg_out"), 16)
                pool.wait_ge(S("p_out"), 16 * (g + 1))
                pool.wait_ge(S("runsum_out"), 16 * (g + 1))
                for c in range(IBLK):
                    gather(prob_rows[:, c * 512:(c + 1) * 512], p_d[g].rearrange("(t e) h -> t (e h)", e=P),
                           item_i[:, IBLK + c:IBLK + c + 1], "prob_rows")
                node_gather(sseg, run4_d[2 * g + 1], "sseg_rows", 4)
                pool.wait_ge(S("table_out"), 16 * (2 + g))
                gather_pass(1 + g, tabs[1 + g])

        @block.tensor
        def _(pe):
            def dense(pairs, sem):
                for a, b in CHUNKS:
                    for k, (wt, x) in enumerate(pairs):
                        last = pe.matmul(ps[:, a:b], wt, x[:, a:b], start=(k == 0), stop=(k == len(pairs) - 1))
                last.then_inc(S(sem), 1)

            def turn(x, sem):
                for b in range(BUCKETS):
                    last = pe.transpose(ps[:, b * P:(b + 1) * P], x[:, b * P:(b + 1) * P], ident)
                last.then_inc(S(sem), 1)

            def item_turn(x, sem):
                for c in range(IBLK):
                    xc = x[:, c * 512:(c + 1) * 512].rearrange("p (e h) -> p h e", h=4)
                    for h in range(4):
                        k = 4 * c + h
                        last = pe.transpose(ps[:, k * P:(k + 1) * P], xc[:, h, :], ident)
                last.then_inc(S(sem), 1)

            def norm(xs, n):
                avg = ones[:, 0:P] if len(xs) == 1 else ones[:, P:2 * P]
                for part, sem in ((0, "norm_mean"), (1, "norm_var")):
                    for c, (a, b) in enumerate(CHUNKS):
                        if part:
                            pe.wait_ge(S("norm_sq"), norm_chunk(n, c))
                        for k, pair in enumerate(xs):
                            last = pe.matmul(ps[:, a:b], avg, pair[part][:, a:b], start=(k == 0),
                                             stop=(k == len(xs) - 1))
                        last.then_inc(S(sem), 1)

            def small_turn(n, k):
                pe.wait_ge(S("scan_last"), n)
                pe.transpose(side[0:k, 0:P], small[:, 32:32 + k], ident).then_inc(S("scan_lastT"), 1)
                pe.wait_ge(S("scan_carry"), n)
                pe.transpose(side[:, 256:256 + k], carry[0:k, 0:P], ident[0:k, 0:k]).then_inc(S("scan_carryT"), 1)

            def clear():
                for k in range(BUCKETS + 1):
                    last = pe.matmul(ps[:, k * P:(k + 1) * P], zeros[:], zeros[:], start=True, stop=False,
                                     skip_group_check=True)
                return last

            def gather_pass(n):
                clear()
                with pe.Fori(0, TURNS) as i:
                    for u in range(RING):
                        b = pe.value_load(bk_row[0:1, bass.ds(i * RING + u, 1)], min_val=0, max_val=BUCKETS - 1)
                        if u % GROUP == 0:
                            pe.wait_ge(S(f"alt_row_in{u // GROUP}"), i * (16 * GROUP) + 16 * GROUP * (n * TURNS + 1))
                        pe.wait_ge(S("alt_item_ready"), i * RING + (n * ITEMS_RUN + u + 1))
                        pe.matmul(ps[:, bass.ds(b * P, P)], rows[:, u * P:(u + 1) * P], hot[:, u * P:(u + 1) * P],
                                  start=False, stop=False, skip_group_check=True).then_inc(S("alt_item_done"), 1)

            def weighted_pass(m):
                clear()
                with pe.Fori(0, TURNS) as i:
                    for g in range(QUADS):
                        one_bucket = pe.value_load(quad_row[0:1, bass.ds(i * QUADS + g, 1)], min_val=0, max_val=BUCKETS)

                        def product(place, u):
                            return pe.matmul(ps[:, bass.ds(place, P)], hot[:, u * P:(u + 1) * P],
                                             rows[:, u * P:(u + 1) * P], start=False, stop=False, skip_group_check=True)

                        with pe.If(one_bucket > 0):
                            pe.wait_ge(S("item_ready"), i * QUADS + (m * TURNS * QUADS + g + 1))
                            for u in range(g * GROUP, (g + 1) * GROUP):
                                last = product(one_bucket * P, u)
                            last.then_inc(S("item_done"), GROUP)
                        with pe.Else():
                            pe.wait_ge(S("item_ready"), i * QUADS + (m * TURNS * QUADS + g + 1))
                            for u in range(g * GROUP, (g + 1) * GROUP):
                                b = pe.value_load(bk_row[0:1, bass.ds(i * RING + u, 1)], min_val=0, max_val=BUCKETS - 1)
                                product(b * P + P, u).then_inc(S("item_done"), 1)

            def count_edges():
                clear()
                with pe.Fori(0, TURNS) as i:
                    for u in range(RING):
                        c = u % CRING
                        b = pe.value_load(bk_row[0:1, bass.ds(i * RING + u, 1)], min_val=0, max_val=BUCKETS - 1)
                        pe.wait_ge(S("count_zeroed"), b + 1)
                        pe.wait_ge(S("count_ready"), i * RING + (u + 1))
                        for k in range(BUCKETS):
                            last = pe.matmul(ps[:, k * P:(k + 1) * P], src_hot[:, c * NP + k * P:c * NP + (k + 1) * P],
                                             dst_hot[:, c * P:(c + 1) * P], start=False, stop=False,
                                             skip_group_check=True)
                        last.then_inc(S("count_done"), 1)

            def sum_rows(n, alt, finish):
                def product(part, k, a, b):
                    pe.matmul(ps[:, a:b], parts16[part][:, k * P:(k + 1) * P], counts[:, k, a:b],
                              start=(part == 0 and k == 0), stop=False, skip_group_check=True)

                with pe.If(alt > 0):
                    pe.wait_ge(S("y"), pass_done(n))
                    gather_pass(n)
                    for c in range(len(CHUNKS)):
                        finish(c)
                with pe.Else():
                    for part, sem, done in ((0, "high_part", pass_done(n)), (1, "middle_part", n + 1)):
                        pe.wait_ge(S(sem), done)
                        for k in range(BUCKETS):
                            for a, b in CHUNKS:
                                product(part, k, a, b)
                    pe.wait_ge(S("low_part"), n + 1)
                    for c, (a, b) in enumerate(CHUNKS):
                        for k in range(BUCKETS):
                            product(2, k, a, b)
                        finish(c)

            pe.sem_inc(S("item_done"), RING)
            pe.sem_inc(S("alt_item_done"), RING)
            pe.sem_inc(S("count_done"), CRING)
            pe.wait_ge(S("loads"), 16 * LOADS)
            pe.wait_ge(S("keep_last"), 1)
            pe.transpose(side[0:8, 0:P], small[:, 32:40], ident).then_inc(S("keepT_ps"), 1)
            pe.wait_ge(S("item_f32"), 1)
            for k in range(2):
                for c in range(IBLK):
                    last = pe.transpose(ps[:, k * 1024 + c * P:k * 1024 + (c + 1) * P],
                                        G[3 + k][:, c * P:(c + 1) * P], ident)
            last.then_inc(S("itemsT"), 1)
            pe.wait_ge(S("itemsT_used"), 1)
            pe.wait_ge(S("item_in"), 32)
            count_edges()
            pe.wait_ge(S("over"), 1)
            pe.matmul(side[:, 0:1], ones[:, 0:P], over[:, BUCKETS:BUCKETS + 1], start=True, stop=True).then_inc(S("over_ps"), 1)
            alt = alt_flag(pe)
            pe.wait_ge(S("x_in"), 16)
            for n in range(2):
                turn(G[3] if n else xT, "y_ps")
                sum_rows(n, alt, lambda c: None)
                pe.matmul(ps[:, 0:8], zeros[:], zeros[:, 0:8], start=False, stop=True,
                          skip_group_check=True).then_inc(S("agg_ps"), 1)
                pe.wait_ge(S("agg"), n + 1)
                dense([(w[f"wn{n + 1}"], G[2]), (w[f"ws{n + 1}"], G[3] if n else xT)], "lin")
                if n == 0:
                    pe.wait_ge(S("hid"), 1)
            pe.wait_ge(S("norm_in"), 1)
            norm([(xT, G[2])], 1)
            def conv_rows(k, c):
                pe.wait_ge(S("conv_in"), conv_chunk(k, c))
                a, b = CHUNKS[c]
                for n in range(a, b, P):
                    last = pe.matmul(ps[:, n:n + P], (G[3] if k else xT)[:, n:n + P], w[f"gcn{k}"], start=True, stop=True,
                                     skip_group_check=True)
                last.then_inc(S("y_ps"), 1)

            def own_loop(k, c):
                a, b = CHUNKS[c]
                for n in range(a, b, P):
                    last = pe.matmul(ps[:, n:n + P], G[2][:, n:n + P], ident, start=False, stop=(n + P == b),
                                     skip_group_check=True)
                last.then_inc(S("agg_ps"), 1)
                if k < 3 and c:
                    conv_rows(k + 1, c - 1)

            for c in range(len(CHUNKS)):
                conv_rows(0, c)
            for k in range(4):
                sum_rows(2 + k, alt, lambda c: own_loop(k, c))
                if k < 3:
                    conv_rows(k + 1, len(CHUNKS) - 1)
            pe.wait_ge(S("norm_in"), 2)
            norm([(xT, G[2])], 2)
            pe.wait_ge(S("conv_in"), 4 * len(CHUNKS) + 1)
            dense([(w["wsc"], xT)], "lin")
            pe.wait_ge(S("scaled"), 1)
            dense([(w["wy"], xT)], "lin")
            pe.wait_ge(S("scaled"), 2)
            turn(G[2], "rowsT")
            pe.wait_ge(S("table_rows"), 1)
            pe.wait_ge(S("sh_rows"), 16 * IBLK)
            item_turn(sh_rows, "shT_ps")
            pe.wait_ge(S("shT"), 1)

            def hidden(i, k, g):
                pe.wait_ge(S(f"ea_in{g}"), i * (16 * GROUP) + 16 * GROUP)
                pe.wait_ge(S("silu"), k + 1)
                pe.matmul(ps[0:100, (g % 2) * 512:(g % 2 + 1) * 512], wfc1[:],
                          ea_ring[:, g * GROUP * P:(g + 1) * GROUP * P], start=True, stop=True).then_inc(S("hid_ps"), 1)

            def edge_w(i, k, g):
                pe.wait_ge(S("silu"), k + 3)
                pe.wait_ge(S("w_copied"), k + 1)
                for j in range(GROUP):
                    last = pe.matmul(ps[:, (2 + g % 2) * 512 + j * P:(2 + g % 2) * 512 + (j + 1) * P],
                                     hid_ring[:, ((g % 2) * GROUP + j) * P:((g % 2) * GROUP + j + 1) * P],
                                     w["wfc2"][0:100, :], start=True, stop=True, skip_group_check=True)
                last.then_inc(S("w_ps"), 1)

            def by_dest(i, k, g):
                one_bucket = pe.value_load(quad_row[0:1, bass.ds(k, 1)], min_val=0, max_val=BUCKETS)
                pe.wait_ge(S("msg"), k + 3)
                pe.wait_ge(S("summed"), k * GROUP + GROUP)

                def products(together):
                    for j in range(GROUP):
                        o, u = sums_at(g, 0 if together else j), g * GROUP + j
                        m = ((g % 2) * GROUP + j) * 256
                        last = pe.matmul(ps[:, o:o + 256], hot[:, u * P:(u + 1) * P], msg_ring[:, m:m + 256],
                                         start=(j == 0 or not together), stop=(j == GROUP - 1 or not together),
                                         skip_group_check=True)
                    last.then_inc(S("sums_ps"), 1)

                with pe.If(one_bucket > 0):
                    products(True)
                with pe.Else():
                    products(False)

            pe.sem_inc(S("hid_ps"), QUADS)
            pe.sem_inc(S("w_ps"), 2)
            pe.sem_inc(S("sums_ps"), 2)
            parts = [(hidden, 0), (edge_w, 1), (by_dest, 3)]
            for g in range(QUADS):
                group_step(0, g, parts, first=True)
            with pe.Fori(1, TURNS) as i:
                for g in range(QUADS):
                    group_step(i, g, parts)
            for g in range(3):
                group_step(TURNS, g, [x for x in parts if x[1] > g])
            for half in range(2):
                pe.wait_ge(S("sums"), half + 1)
                for b in range(BUCKETS):
                    last = pe.transpose(ps[:, b * P:(b + 1) * P], sums[:, (2 * b + half) * P:(2 * b + half + 1) * P], ident)
                last.then_inc(S("sumsT"), 1)
            pe.wait_ge(S("agg"), 3)
            dense([(w["walpha"], G[2])], "lin")
            pe.wait_ge(S("scaled"), 3)
            dense([(w["wl2a"], G[2]), (w["wl2b"], G[3])], "lin")
            pe.wait_ge(S("norm_in"), 3)
            norm([(G[5], G[2])], 3)
            pe.wait_ge(S("layer_done"), 3)
            pe.matmul(side[:, 0:2], ones[:, 0:P], small[:, 16:18], start=True, stop=True).then_inc(S("tw_prep_ps"), 1)
            pe.wait_ge(S("tw_prep"), 1)
            pe.matmul(side[:, 8:11], ones[:, 0:P], small[:, 22:25], start=True, stop=True).then_inc(S("tw_prep_ps"), 1)
            pe.wait_ge(S("tw_prep"), 2)
            pe.transpose(side[0:3, 128:256], small[:, 29:32], ident).then_inc(S("tw_prep_ps"), 1)
            pe.wait_ge(S("tw_prep"), 3)

            def tw_first(i, s, q):
                if q == 0:
                    pe.wait_ge(S(f"tw_in{s}"), i * 16 + 16)
                pe.wait_ge(S("tw_relu"), i * (2 * TW_STEPS) + (s * TW_STEPS + q + 1))
                a = s * ZR * P + q * TW_COLS
                pe.matmul(ps[:, (q % 2) * 512:(q % 2) * 512 + TW_COLS], taln, tw_ring[:, a:a + TW_COLS],
                          start=True, stop=True).then_inc(S("tw1"), 1)

            def tw_second(i, s, q):
                pe.wait_ge(S("tw_relu"), i * (2 * TW_STEPS) + (s * TW_STEPS + q + 3))
                pe.wait_ge(S("tw_tanh"), i * (2 * TW_STEPS) + (s * TW_STEPS + q + 1))
                pe.matmul(ps[:, (2 + q % 2) * 512:(2 + q % 2) * 512 + TW_COLS], w["taw2"],
                          tw_act[:, q * TW_COLS:(q + 1) * TW_COLS], start=True, stop=True).then_inc(S("tw2"), 1)

            def tw_third(i, s):
                pe.wait_ge(S("tw_tanh"), i * (2 * TW_STEPS) + (s * TW_STEPS + TW_STEPS + 2))
                pe.wait_ge(S("tw_copied"), i * 2 + (s + 1))
                for c in range(ZR):
                    last = pe.matmul(ps[:, (4 + s) * 512 + c * 8:(4 + s) * 512 + c * 8 + 8],
                                     tw_th[:, c * P:(c + 1) * P], attw[:], start=True, stop=True, skip_group_check=True)
                last.then_inc(S("tw3"), 1)

            def tw_turns(i, first):
                for s in range(2):
                    tw_first(i, s, 0)
                    tw_first(i, s, 1)
                    if s == 1:
                        tw_third(i, 0)
                    elif not first:
                        tw_third(i - 1, 1)
                    tw_second(i, s, 0)
                    tw_first(i, s, 2)
                    tw_second(i, s, 1)
                    tw_first(i, s, 3)
                    tw_second(i, s, 2)
                    tw_second(i, s, 3)

            def z_transposes(i, k, s):
                pe.wait_ge(S("zhot"), k + 1)
                pe.wait_ge(S("zhotT"), k + 1)
                for j in range(ZR):
                    last = pe.transpose(zhot_ps[s][:, j * P:(j + 1) * P], zhot[:, (s * ZR + j) * P:(s * ZR + j + 1) * P],
                                        ident16)
                last.then_inc(S("zhot_ps"), 1)

            def z_products(i, k, s):
                pe.wait_ge(S("zhotT"), k + 3)
                pe.wait_ge(S("z_masked"), k + 1)
                for j in range(ZR):
                    for part in range(3):
                        last = pe.matmul(z_candidates(j, j + 1), zhotT[:, (s * ZR + j) * P:(s * ZR + j + 1) * P],
                                         ztab[:, part * 100:(part + 1) * 100], start=(part == 0), stop=(part == 2),
                                         skip_group_check=True)
                last.then_inc(S("z_ps"), 1)

            def find_sources():
                pe.sem_inc(S("zhot_ps"), 2)
                pe.sem_inc(S("z_ps"), 2)
                z_steps(pe, [(z_transposes, 0), (z_products, 1)], 1)

            dense([(w["ipw1a"], G[5])], "lin")
            pe.wait_ge(S("ip_hid"), 1)
            dense([(w["ipw1b"], G[5])], "lin")
            pe.wait_ge(S("ip_hid"), 2)
            norm([(G[0], G[2]), (G[1], G[3])], 4)
            pe.wait_ge(S("ip_norm"), 1)
            dense([(w["ipw2a"], G[0]), (w["ipw2b"], G[1])], "lin")
            pe.wait_ge(S("norm_in"), 4)
            norm([(G[0], G[2])], 5)
            for g in range(2):
                pe.wait_ge(S("gat_in"), g + 1)
                dense([(w[f"gw{g}"], G[0])], "lin")
                pe.wait_ge(S("gat_hT"), g + 1)
                for b in range(BUCKETS):
                    last = pe.matmul(side[:, b * 8:(b + 1) * 8], G[1][:, b * P:(b + 1) * P], att[:, 8 * g:8 * g + 8],
                                     start=True, stop=True, skip_group_check=True)
                last.then_inc(S("a8_ps"), 1)
                turn(G[1], "rowsT")
                pe.wait_ge(S("a8"), g + 1)
                if g == 0:
                    pe.wait_ge(S("table_rows"), 2)
                    pe.sem_inc(S("tw1"), 2 * TW_STEPS)
                    pe.sem_inc(S("tw2"), TW_STEPS)
                    pe.sem_inc(S("tw3"), 1)
                    tw_turns(0, True)
                    with pe.Fori(1, ZTURNS // 2) as i:
                        tw_turns(i, False)
                    tw_third(ZTURNS // 2 - 1, 1)
                    small_turn(1, 8)
                else:
                    pe.wait_ge(S("table_rows"), 3)
                    find_sources()
                small_turn(2 + 3 * g, 4)
                small_turn(3 + 3 * g, 8)
                small_turn(4 + 3 * g, 4)
                pe.wait_ge(S("prob_rows"), 16 * IBLK * (g + 1))
                pe.wait_ge(S("table_rows"), 2 + g)
                item_turn(prob_rows, "pT_ps")
                pe.wait_ge(S("pT"), g + 1)
                weighted_pass(g)
                pe.wait_ge(S("gat_rows"), g + 1)
                turn(G[2], "gatT")
                pe.wait_ge(S("norm_in"), 5 + g)
                norm([(G[0], G[2])], 6 + g)
            pe.wait_ge(S("norm_in"), 7)
            norm([(G[0], G[2])], 8)
            for c, (a, b) in enumerate(CHUNKS):
                pe.wait_ge(S("layer_done"), 3 + c + 1)
                for k in range(a, b, P):
                    last = pe.transpose(ps[:, k:k + P], G[0][:, k:k + P], ident)
                last.then_inc(S("outT"), 1)

        @block.scalar
        def _(act):
            def norm(xs, n):
                for c, (a, b) in enumerate(CHUNKS):
                    act.wait_ge(S("norm_cent"), norm_chunk(n, c))
                    for x, q in xs:
                        last = nc.scalar.activation(q[:, a:b], x[:, a:b], ACT.Square)
                    last.then_inc(S("norm_sq"), 1)
                for c, (a, b) in enumerate(CHUNKS):
                    act.wait_ge(S("norm_var"), norm_chunk(n, c))
                    nc.scalar.activation(xs[0][1][:, a:b], ps[:, a:b], ACT.Sqrt, bias=eps[:]).then_inc(S("norm_std"), 1)

            def rows_out(n):
                act.wait_ge(S("rowsT"), n)
                if n > 1:
                    act.wait_ge(S("table_out"), 16 * (n - 1))
                nc.scalar.copy(G[4], acc).then_inc(S("table_rows"), 1)

            act.wait_ge(S("deg"), 1)
            nc.scalar.activation(dinv, deg, ACT.Sqrt, bias=1.0).then_inc(S("sqrt_deg"), 1)
            act.sem_inc(S("count_zeroed"), 1)
            act.wait_ge(S("items_ready"), 1)
            for b in range(BUCKETS):
                if b < BUCKETS - 1:
                    last_item = act.value_load(thresh_i[0:1, b:b + 1], min_val=0, max_val=ITEMS)
                    hold(act, S("count_done"), last_item + (CRING + 1))
                else:
                    act.wait_ge(S("count_done"), ITEMS_RUN + CRING)
                column = counts[:, :, b * P:(b + 1) * P]
                nc.scalar.activation(column, acc.rearrange("p (s d) -> p s d", d=P), ACT.Copy,
                                     saturate=True).then_inc(S("count_copied"), 1)
                act.wait_ge(S("count_copied"), b + 1)
                nc.scalar.activation(acc, acc, ACT.Copy, scale=0.0).then_inc(S("count_zeroed"), 1)
                if b:
                    act.wait_ge(S("over_seen"), b)
                nc.scalar.activation(over_junk.rearrange("p (s d) -> p s d", d=P), column, ACT.Relu, bias=small[:, 1:2],
                                     accum_out=over[:, b:b + 1]).then_inc(S("over_seen"), 1)
            alt = alt_flag(act)

            def high(n, a, b, done):
                act.wait_ge(S("y"), done)
                nc.scalar.copy(parts16[0][:, a:b], G[2][:, a:b]).then_inc(S("high_part"), 1)

            def middle(n):
                with act.If(alt > 0):
                    act.sem_inc(S("holds"), 1)
                with act.Else():
                    act.wait_ge(S("rest"), n + 1)
                    nc.scalar.copy(parts16[1], rest).then_inc(S("middle_part"), 1)

            act.wait_ge(S("bias"), 1)
            for n in range(2):
                act.wait_ge(S("y_ps"), n + 1)
                nc.scalar.copy(G[2], acc).then_inc(S("y"), 1)
                high(n, 0, NP, n + 1)
                middle(n)
                if n == 0:
                    act.wait_ge(S("lin"), 1)
                    nc.scalar.activation(G[3], acc, ACT.Relu, bias=v["bn1"]).then_inc(S("hid"), 1)
            norm([(xT, G[2])], 1)
            def high_chunk(k, c):
                high(2 + k, *CHUNKS[c], pass_done(1 + k) + c + 1)

            for c in range(len(CHUNKS)):
                high_chunk(0, c)
            for k in range(4):
                middle(2 + k)
                if k < 3:
                    for c, (a, b) in enumerate(CHUNKS):
                        act.wait_ge(S("agg_conv"), conv_chunk(k, c))
                        nc.scalar.activation(G[3][:, a:b], G[2][:, a:b], ACT.Identity if k == 1 else ACT.Relu,
                                             bias=v[f"gb{k}"]).then_inc(S("conv_in"), 1)
                        if c > 1:
                            high_chunk(k + 1, c - 2)
                    for c in range(len(CHUNKS) - 2, len(CHUNKS)):
                        high_chunk(k + 1, c)
            norm([(xT, G[2])], 2)
            rows_out(1)
            act.sem_inc(S("silu"), 2)

            def silu(i, k, g):
                act.wait_ge(S("hid_ps"), k + QUADS + 1)
                act.wait_ge(S("w_ps"), k + 1)
                nc.scalar.activation(hid_ring[:, (g % 2) * GROUP * P:(g % 2 + 1) * GROUP * P],
                                     ps[0:100, (g % 2) * 512:(g % 2 + 1) * 512], ACT.Silu,
                                     scale=float(1 / np.sqrt(10.0))).then_inc(S("silu"), 1)

            def copy_w(i, k, g):
                hold(act, S("w_ps"), k + 3)
                hold(act, S("msg"), k + 1)
                for j in range(GROUP):
                    src = ps[:, (2 + g % 2) * 512 + j * P:(2 + g % 2) * 512 + (j + 1) * P]
                    dst = w_ring[:, ((g % 2) * GROUP + j) * P:((g % 2) * GROUP + j + 1) * P]
                    nc.scalar.activation(dst[:, 0:2 * MUL], src[:, 0:2 * MUL], ACT.Copy,
                                         scale=shT[:, bass.ds(k * (4 * GROUP) + 4 * j, 1)])
                a, b = (cut(t, P)[:, :, 2 * MUL:P] for t in (w_ring[:, (g % 2) * 512:(g % 2 + 1) * 512],
                                                            ps[:, (2 + g % 2) * 512:(3 + g % 2) * 512]))
                nc.scalar.copy(a, b).then_inc(S("w_copied"), 1)

            act.sem_inc(S("w_copied"), 2)
            parts = [(silu, 0), (copy_w, 1)]
            for g in range(QUADS):
                group_step(0, g, parts, first=True)
            with act.Fori(1, TURNS) as i:
                for g in range(QUADS):
                    group_step(i, g, parts)
            group_step(TURNS, 0, parts[1:])
            norm([(G[5], G[2])], 3)
            act.wait_ge(S("tw_prep"), 4)
            nc.scalar.activation(t_std, t_var, ACT.Sqrt, bias=eps[:]).then_inc(S("tw_std"), 1)
            act.wait_ge(S("lin"), 7)
            nc.scalar.activation(G[0], acc, ACT.Relu, bias=v["ipb1a"]).then_inc(S("ip_hid"), 1)
            act.wait_ge(S("lin"), 8)
            nc.scalar.activation(G[1], acc, ACT.Relu, bias=v["ipb1b"]).then_inc(S("ip_hid"), 1)
            norm([(G[0], G[2]), (G[1], G[3])], 4)
            norm([(G[0], G[2])], 5)
            for g in range(2):
                act.wait_ge(S("lin"), 10 + g)
                nc.scalar.copy(G[1], acc).then_inc(S("gat_hT"), 1)
                rows_out(2 + g)
                if g == 0:
                    act.sem_inc(S("tw_tanh"), 2)
                    with act.Fori(0, ZTURNS) as i:
                        for q in range(TW_STEPS):
                            act.wait_ge(S("tw2"), i * TW_STEPS + (q + TW_STEPS + 1))
                            act.wait_ge(S("tw3"), i + 1)
                            nc.scalar.activation(tw_th[:, q * TW_COLS:(q + 1) * TW_COLS],
                                                 ps[:, (2 + q % 2) * 512:(2 + q % 2) * 512 + TW_COLS],
                                                 ACT.Tanh, bias=v["tab2"]).then_inc(S("tw_tanh"), 1)
                else:
                    def copy_hot(i, k, s):
                        act.wait_ge(S("zhot_ps"), k + 3)
                        act.wait_ge(S("z_ps"), k + 1)
                        nc.scalar.copy(zhotT[:, s * ZR * P:(s + 1) * ZR * P], zhot_ps[s]).then_inc(S("zhotT"), 1)

                    act.sem_inc(S("zhotT"), 2)
                    z_steps(act, [(copy_hot, 0)], 0)
                act.wait_ge(S("lp"), g + 1)
                nc.scalar.activation(ploop, ploop, ACT.Exp).then_inc(S("ploop"), 1)
                act.wait_ge(S("alpha"), g + 1)
                nc.scalar.activation(z, z, ACT.Exp).then_inc(S("prob"), 1)
                norm([(G[0], G[2])], 6 + g)
                act.wait_ge(S("elu_min"), g + 1)
                nc.scalar.activation(G[2], G[2], ACT.Exp).then_inc(S("elu_exp"), 1)
            norm([(G[0], G[2])], 8)
            act.wait_ge(S("table_out"), 16 * 3)
            for c, (a, b) in enumerate(CHUNKS):
                act.wait_ge(S("outT"), c + 1)
                nc.scalar.copy(G[4][:, a:b], ps[:, a:b]).then_inc(S("out_rows"), 1)

        @block.vector
        def _(dve):
            vec = nc.vector
            count = [0]

            def link(ins):
                count[0] += 1
                ins.then_inc(S("dve_link"), 1)
                dve.wait_ge(S("dve_link"), count[0])

            def wide(a, k):
                return a.unsqueeze(2).to_broadcast([P, a.shape[1], k])

            vec.memset(zeros[:], 0.0)
            vec.memset(small[:, 1:2], -float(MOST))
            vec.memset(ones[:, 0:P], 1.0 / P)
            vec.memset(ones[:, P:2 * P], 0.5 / P)
            vec.memset(eps[:], LN_EPS)
            link(vec.memset(small[:, 0:1], float(E)))
            dve.wait_ge(S("scan_loads"), 48)
            link(vec.tensor_copy(big[:, SLOT:SLOT + 3 * RUN], big[:, 0:3 * RUN].bitcast(I32)))
            prev, cur, first = (big[:, SLOT + i * RUN:SLOT + (i + 1) * RUN] for i in range(3))
            link(vec.tensor_tensor(keep[:], prev, cur, ALU.is_equal))
            link(vec.tensor_tensor_scan(still[:], keep[:], keep[:], 1.0, ALU.mult, ALU.mult))
            vec.tensor_copy(small[:, 32:40], still[:, RUN - 1:RUN].to_broadcast([P, 8])).then_inc(S("keep_last"), 1)
            dve.wait_ge(S("keepT_ps"), 1)
            link(vec.tensor_copy(keepT[:, 0:P], side[0:8, 0:P]))
            link(vec.tensor_scalar(keepT[:, P:2 * P], keepT[:, 0:P], 1.0, BIG, ALU.subtract, ALU.mult))
            dve.wait_ge(S("iotas"), 3)
            for b in range(BUCKETS):
                link(vec.tensor_scalar(hot[:, 0:RUN], first, nodeid[:, b:b + 1], None, ALU.is_lt, ALU.add,
                                       accum_out=cnt[:, b:b + 1]))
            link(vec.tensor_scalar(cnt, cnt, 1.0, 0.0, ALU.subtract, ALU.max))
            vec.tensor_copy(rowsel, cnt).then_inc(S("rowsel_ready"), 1)
            dve.wait_ge(S("ptr_rows"), 16 * BUCKETS)
            link(vec.tensor_copy(G[3], G[2].bitcast(I32)))
            link(vec.tensor_tensor(cut(G[3], P), cut(G[3], P), wide(nodeid, P), ALU.is_lt))
            link(vec.tensor_reduce(deg, cut(G[3], P), AX, ALU.add))
            vec.scalar_tensor_tensor(rowptr, cnt, float(P), deg, ALU.mult, ALU.add).then_inc(S("rowptr_ready"), 1)
            dve.wait_ge(S("rowptr_ready"), 1)
            dve.wait_ge(S("rp_in"), 32)
            vec.tensor_tensor(deg, nextptr, rowptr, ALU.subtract).then_inc(S("deg"), 1)
            dve.wait_ge(S("deg"), 1)
            link(vec.tensor_scalar(invdeg, deg, 1.0, None, ALU.max))
            link(vec.reciprocal(invdeg, invdeg))
            link(vec.tensor_scalar(has, deg, 1.0, None, ALU.min))
            link(vec.tensor_scalar(cnt, nextptr, 1.0, 0.0, ALU.subtract, ALU.max))
            link(vec.tensor_copy(end_i, cnt))
            link(vec.tensor_scalar(cnt, has, 1.0, -FAR, ALU.subtract, ALU.mult))
            link(vec.tensor_tensor(cnt, cnt, rowptr, ALU.add))
            link(vec.tensor_copy(start_i, cnt))
            dve.wait_ge(S("sqrt_deg"), 1)
            vec.reciprocal(dinv, dinv).then_inc(S("nodevec_ready"), 1)
            th = thresh[:, 0:BUCKETS - 1]
            link(vec.tensor_copy(thresh_i[:], th))
            link(vec.tensor_scalar(thresh_i[:], thresh_i[:], 7, None, ALU.arith_shift_right))
            link(vec.tensor_copy(th, thresh_i[:]))
            link(vec.tensor_tensor(th, th, iota[:, 0:BUCKETS - 1], ALU.add))
            link(vec.tensor_copy(thresh_i[:], th))
            item_n, item_b, item_t, item_off = (item_f[:, i * IBLK:(i + 1) * IBLK] for i in range(4))
            past = cut(hot[:, 0:IBLK * (BUCKETS - 1)], BUCKETS - 1)
            link(vec.tensor_tensor(past, th.unsqueeze(1).to_broadcast([P, IBLK, BUCKETS - 1]),
                                   wide(item_n, BUCKETS - 1), ALU.is_lt))
            link(vec.tensor_reduce(item_b, past, AX, ALU.add))
            link(vec.tensor_tensor(item_t, item_n, item_b, ALU.subtract))
            link(vec.tensor_scalar(item_t, item_t, float(TILES - 1), None, ALU.min))
            link(vec.tensor_copy(item_i[:, 0:IBLK], item_b))
            vec.tensor_copy(item_i[:, IBLK:2 * IBLK], item_t).then_inc(S("items_ready"), 1)
            link(vec.tensor_scalar(item_off, item_n, float(ITEMS - 1), FAR, ALU.is_gt, ALU.mult))
            link(vec.scalar_tensor_tensor(item_off, item_b, float(P), item_off, ALU.mult, ALU.add))
            dve.wait_ge(S("item_rows"), 16 * 2 * IBLK)
            link(vec.tensor_copy(G[3][:, 0:IPAD], G[3][:, 0:IPAD].bitcast(I32)))
            link(vec.tensor_copy(G[4][:, 0:IPAD], G[4][:, 0:IPAD].bitcast(I32)))
            vec.tensor_tensor(cut(G[3][:, 0:IPAD], P), cut(G[3][:, 0:IPAD], P), wide(item_off, P),
                              ALU.subtract).then_inc(S("item_f32"), 1)
            dve.wait_ge(S("item_f32"), 1)
            dve.sem_inc(S("slots_free"), 1)
            dve.wait_ge(S("itemsT"), 1)
            vec.tensor_copy(dloc[:], ps[:, 0:IPAD])
            vec.tensor_scalar(src_f, ps[:, 1024:1024 + IPAD], float(MID), None, ALU.subtract)
            vec.tensor_copy(srcI[:], ps[:, 1024:1024 + IPAD]).then_inc(S("itemsT_used"), 1)
            dve.wait_ge(S("itemsT_used"), 1)
            dve.wait_ge(S("node_iota"), 1)
            link(vec.tensor_copy(node_iota16, node_iota))
            with dve.Fori(0, TURNS) as i:
                for u in range(RING):
                    c = u % CRING
                    dve.wait_ge(S("count_done"), i * RING + (u + 1))
                    vec.tensor_scalar(src_hot[:, c * NP:(c + 1) * NP], node_iota16,
                                      src_f[:, bass.ds(i * RING + u, 1)], None, ALU.is_equal)
                    vec.tensor_scalar(dst_hot[:, c * P:(c + 1) * P], iota[:], dloc[:, bass.ds(i * RING + u, 1)], None,
                                      ALU.is_equal).then_inc(S("count_ready"), 1)
            dve.wait_ge(S("over_seen"), BUCKETS)
            vec.tensor_reduce(over[:, BUCKETS:BUCKETS + 1], over[:, 0:BUCKETS], AX, ALU.add).then_inc(S("over"), 1)
            dve.wait_ge(S("over_ps"), 1)
            vec.tensor_scalar(flag[:], side[0:1, 0:1], 0.0, None, ALU.is_gt).then_inc(S("flag"), 1)
            alt = alt_flag(dve)

            def item_columns(dst, sem, n):
                vec.tensor_copy(dst.rearrange("p (c k h) -> p c h k", c=IBLK, h=4),
                                ps[:, 0:4 * IPAD].rearrange("p (c h k) -> p c h k", c=IBLK, h=4)).then_inc(S(sem), 1)
                dve.wait_ge(S(sem), n)

            dve.wait_ge(S("item_in"), 32)
            buckets_f, same = rows[0:1, 0:ITEMS_RUN], hot[0:1, 0:ITEMS_RUN // GROUP]
            first_b, last_b = (cut(buckets_f, GROUP)[:, :, j] for j in (0, GROUP - 1))
            link(vec.tensor_copy(buckets_f, bk_row[:]))
            link(vec.tensor_tensor(same, first_b, last_b, ALU.is_equal))
            link(vec.scalar_tensor_tensor(first_b, first_b, 1.0, same, ALU.add, ALU.mult))
            link(vec.tensor_copy(quad_row[:], first_b))
            link(vec.tensor_copy(buckets_f, first_tiles))
            link(vec.scalar_tensor_tensor(first_b, first_b, 1.0, same, ALU.add, ALU.mult))
            link(vec.tensor_copy(quad_tile, first_b))
            dve.wait_ge(S("loads"), 16 * LOADS)
            link(vec.tensor_scalar(w["wfc2"], w["wfc2"], 0.1, None, ALU.mult))
            link(vec.tensor_scalar(w["wfc2"][:, 2 * MUL:3 * MUL], w["wfc2"][:, 2 * MUL:3 * MUL], float(1 / np.sqrt(3.0)),
                                   None, ALU.mult))
            link(vec.tensor_tensor(v["bn2"], v["bn2"], v["bs2"], ALU.add))
            vec.tensor_tensor(v["bn1"], v["bn1"], v["bs1"], ALU.add).then_inc(S("bias"), 1)

            def indices(i, u, pre=""):
                vec.tensor_copy(idx_ring[:, u:u + HALF],
                                srcI[:, bass.ds(i * RING + u, HALF)]).then_inc(S(pre + "idx_ready"), 1)

            def one_hot(i, u):
                return vec.tensor_scalar(hot[:, u * P:(u + 1) * P], iota[:], dloc[:, bass.ds(i * RING + u, 1)], None,
                                         ALU.is_equal)

            def passed(m):
                dve.wait_ge(S("item_done"), RING + (m + 1) * ITEMS_RUN)

            def sum_rows(n):
                with dve.If(alt > 0):
                    dve.wait_ge(S("high_part"), pass_done(n))
                    with dve.Fori(0, TURNS) as i:
                        for u in range(RING):
                            if u % HALF == 0:
                                hold(dve, S("alt_item_done"), i * RING + (n * ITEMS_RUN + u + HALF))
                                indices(i, u, "alt_")
                            one_hot(i, u).then_inc(S("alt_item_ready"), 1)
                with dve.Else():
                    dve.wait_ge(S("high_part"), pass_done(n))
                    vec.tensor_tensor(rest, G[2], parts16[0], ALU.subtract).then_inc(S("rest"), 1)
                    dve.wait_ge(S("middle_part"), n + 1)
                    vec.tensor_tensor(parts16[2], rest, parts16[1], ALU.subtract).then_inc(S("low_part"), 1)

            def group_heads(k, g):
                return vec.tensor_tensor(cut(hot[:, g * GROUP * P:(g + 1) * GROUP * P], P),
                                         iota[:].unsqueeze(1).to_broadcast([P, GROUP, P]),
                                         wide(dloc[:, bass.ds(k * GROUP, GROUP)], P), ALU.is_equal)

            def weighted_pass(n, m):
                def heads(i, k, g):
                    if g % 2 == 0:
                        hold(dve, S("item_done"), i * RING + (m * ITEMS_RUN + g * GROUP + HALF))
                        indices(i, g * GROUP)
                    group_heads(k, g)

                def weigh(i, k, g):
                    group = rows[:, g * GROUP * P:(g + 1) * GROUP * P]
                    dve.wait_ge(S(f"row_in{g}"), i * (16 * GROUP) + 16 * GROUP * (n * TURNS + 1))
                    vec.tensor_tensor(cut(group, C), cut(group, C), wide(pT[:, bass.ds(k * (4 * GROUP), 4 * GROUP)], C),
                                      ALU.mult).then_inc(S("item_ready"), 1)

                parts = [(heads, 0), (weigh, 2)]
                for g in range(QUADS):
                    group_step(0, g, parts, first=True)
                with dve.Fori(1, TURNS) as i:
                    for g in range(QUADS):
                        group_step(i, g, parts)
                for g in range(2):
                    group_step(TURNS, g, parts[1:])
                passed(m)

            def norm(xs, n, ready=None):
                for c, (a, b) in enumerate(CHUNKS):
                    dve.wait_ge(S("norm_mean"), norm_chunk(n, c))
                    for x, q in xs:
                        last = vec.tensor_tensor(x[:, a:b], x[:, a:b], ps[:, a:b], ALU.subtract)
                    last.then_inc(S("norm_cent"), 1)
                rstd = xs[0][1]
                for c, (a, b) in enumerate(CHUNKS):
                    dve.wait_ge(S("norm_std"), norm_chunk(n, c))
                    link(vec.reciprocal(rstd[:, a:b], rstd[:, a:b]))
                    for x, q in xs:
                        last = vec.tensor_tensor(x[:, a:b], x[:, a:b], rstd[:, a:b], ALU.mult)
                    if ready:
                        last.then_inc(S(ready), 1)
                if not ready:
                    link(last)

            dve.wait_ge(S("nodevec_in"), 16)
            for n in range(2):
                sum_rows(n)
                dve.wait_ge(S("agg_ps"), n + 1)
                vec.tensor_tensor(G[2], acc, deg_bc, ALU.mult).then_inc(S("agg"), 1)
            dve.wait_ge(S("lin"), 2)
            vec.scalar_tensor_tensor(xT, acc, v["bn2"], xT, ALU.add, ALU.add).then_inc(S("norm_in"), 1)
            norm([(xT, G[2])], 1)
            dve.sem_inc(S("layer_done"), 1)
            dve.sem_inc(S("conv_in"), len(CHUNKS))
            dve.wait_ge(S("nodevec_in"), 32)

            def conv_rows(k, c):
                a, b = CHUNKS[c]
                dve.wait_ge(S("y_ps"), pass_done(1 + k) + c + 1)
                vec.tensor_tensor(cut(G[2][:, a:b], P), cut(ps[:, a:b], P), wide(dinv[:, a // P:b // P], P),
                                  ALU.mult).then_inc(S("y"), 1)

            for c in range(len(CHUNKS)):
                conv_rows(0, c)
            for k in range(4):
                sum_rows(2 + k)
                for c, (a, b) in enumerate(CHUNKS):
                    dve.wait_ge(S("agg_ps"), pass_done(1 + k) + c + 1)
                    vec.tensor_tensor(G[2][:, a:b], ps[:, a:b], deg_bc[:, a:b], ALU.mult).then_inc(S("agg_conv"), 1)
                    if k < 3 and c:
                        conv_rows(k + 1, c - 1)
                if k < 3:
                    conv_rows(k + 1, len(CHUNKS) - 1)
            dve.wait_ge(S("agg_conv"), 4 * len(CHUNKS))
            vec.scalar_tensor_tensor(xT, G[2], v["gb3"], xT, ALU.add, ALU.add).then_inc(S("norm_in"), 1)
            norm([(xT, G[2])], 2)
            dve.sem_inc(S("layer_done"), 1)
            dve.sem_inc(S("conv_in"), 1)
            dve.wait_ge(S("nodevec_in"), 48)
            dve.wait_ge(S("attr_in"), 16)
            vec.memset(ea_ring, 0.0)
            dve.wait_ge(S("lin"), 3)
            vec.scalar_tensor_tensor(scT, acc, INV, attr_bc, ALU.mult, ALU.mult).then_inc(S("scaled"), 1)
            dve.wait_ge(S("lin"), 4)
            vec.scalar_tensor_tensor(G[2], acc, INV, attr_bc, ALU.mult, ALU.mult).then_inc(S("scaled"), 1)
            dve.wait_ge(S("shT_ps"), 1)
            item_columns(shT, "shT", 1)
            link(vec.memset(sums, 0.0))

            def messages(i, k, g):
                row = cut(rows[:, g * GROUP * P:(g + 1) * GROUP * P], P)
                y0, y1 = row[:, :, 0:MUL], row[:, :, MUL:P].rearrange("p j (c u) -> p j c u", u=MUL)
                wt = cut(w_ring[:, (g % 2) * 512:(g % 2 + 1) * 512], P)
                w00, w10, w11, w01 = (wt[:, :, a * MUL:(a + 1) * MUL] for a in range(4))
                msg = cut(msg_ring[:, (g % 2) * GROUP * 256:(g % 2 + 1) * GROUP * 256], 256)
                m00, m11 = msg[:, :, 0:MUL], msg[:, :, MUL:2 * MUL]
                m01, m10 = (msg[:, :, a:a + 3 * MUL].rearrange("p j (c u) -> p j c u", u=MUL) for a in (64, 160))
                t01 = cut(mul_tmp[:, 0:GROUP * MUL], MUL)
                dot = mul_tmp[:, GROUP * MUL:GROUP * 4 * MUL]
                d = cut(dot_sum, MUL)
                sh = cut(shT[:, bass.ds(k * (4 * GROUP), 4 * GROUP)], 4)
                sh1 = sh[:, :, 1:4].unsqueeze(3).to_broadcast([P, GROUP, 3, MUL])

                def vectors(a):
                    return a.unsqueeze(2).to_broadcast([P, GROUP, 3, MUL])

                dve.wait_ge(S(f"row_in{g}"), i * (16 * GROUP) + 16 * GROUP)
                vec.tensor_tensor(dot.rearrange("p (j c u) -> p j c u", c=3, u=MUL), y1, sh1,
                                  ALU.mult).then_inc(S("prod"), 1)
                dve.wait_ge(S("w_copied"), k + 3)
                dve.wait_ge(S("msg"), k + 2)
                vec.tensor_tensor(t01, w01, y0, ALU.mult).then_inc(S("prod"), 1)
                dve.wait_ge(S("sums_ps"), k + 1)
                vec.tensor_tensor(m00, y0, w00, ALU.mult)
                dve.wait_ge(S("prod"), k * 3 + 1)
                vec.tensor_reduce(d, dot.rearrange("p (j c u) -> p j u c", c=3, u=MUL), AX,
                                  ALU.add).then_inc(S("prod"), 1)
                vec.tensor_tensor(m10, y1, vectors(w10), ALU.mult)
                dve.wait_ge(S("prod"), k * 3 + 2)
                vec.tensor_tensor(m01, vectors(t01), sh1, ALU.mult)
                dve.wait_ge(S("prod"), k * 3 + 3)
                vec.tensor_tensor(m11, d, w11, ALU.mult).then_inc(S("msg"), 1)

            def add_up(i, k, g):
                one_bucket = dve.value_load(quad_row[0:1, bass.ds(k, 1)], min_val=0, max_val=BUCKETS)
                with dve.If(one_bucket > 0):
                    dve.wait_ge(S("sums_ps"), k + 3)
                    dve.wait_ge(S("summed"), k * GROUP + 2 * GROUP)
                    dst, o = sums_from_1[:, bass.ds(one_bucket * 256, 256)], sums_at(g, 0)
                    vec.tensor_tensor(dst, dst, ps[:, o:o + 256], ALU.add).then_inc(S("summed"), GROUP)
                with dve.Else():
                    dve.wait_ge(S("sums_ps"), k + 3)
                    for j in range(GROUP):
                        b = dve.value_load(bk_row[0:1, bass.ds(k * GROUP + j, 1)], min_val=0, max_val=BUCKETS - 1)
                        dst, o = sums[:, bass.ds(b * 256, 256)], sums_at(g, j)
                        dve.wait_ge(S("summed"), k * GROUP + (j + 2 * GROUP))
                        vec.tensor_tensor(dst, dst, ps[:, o:o + 256], ALU.add).then_inc(S("summed"), 1)

            def heads(i, k, g):
                if g % 2 == 0:
                    indices(i, g * GROUP)
                group_heads(k, g)

            dve.sem_inc(S("msg"), 2)
            dve.sem_inc(S("summed"), 2 * GROUP)
            parts = [(messages, 2), (add_up, 4), (heads, 0)]
            for g in range(QUADS):
                group_step(0, g, parts, first=True)
            with dve.Fori(1, TURNS) as i:
                for g in range(QUADS):
                    group_step(i, g, parts)
            for g in range(4):
                group_step(TURNS, g, [x for x in parts if x[1] > g])
            dve.wait_ge(S("summed"), ITEMS_RUN + 2 * GROUP)
            dve.sem_inc(S("sums"), 1)
            dve.wait_ge(S("sumsT"), 1)
            vec.tensor_tensor(G[2], acc, deg_bc, ALU.mult).then_inc(S("sums"), 1)
            dve.wait_ge(S("sumsT"), 2)
            vec.tensor_tensor(G[3], acc, deg_bc, ALU.mult).then_inc(S("agg"), 1)
            dve.wait_ge(S("lin"), 5)
            vec.scalar_tensor_tensor(alphaT, acc, INV2, attr_bc, ALU.mult, ALU.mult).then_inc(S("scaled"), 1)
            dve.wait_ge(S("lin"), 6)
            link(vec.scalar_tensor_tensor(convT, acc, INV2, attr_bc, ALU.mult, ALU.mult))
            link(vec.tensor_tensor(convT, convT, alphaT, ALU.mult))
            link(vec.tensor_tensor(G[3], convT, scT, ALU.add))
            vec.tensor_tensor(G[5], xT, G[3], ALU.add).then_inc(S("norm_in"), 1)
            norm([(G[5], G[2])], 3)
            dve.sem_inc(S("layer_done"), 1)
            dve.wait_ge(S("tw_prep_ps"), 1)
            w1b1, lnw = small[:, 20:22], small[:, 18:19]
            link(vec.tensor_tensor(w1b1, small[:, 16:18], side[:, 0:2], ALU.subtract))
            vec.tensor_tensor(small[:, 22:24], w1b1, w1b1[:, 0:1].to_broadcast([P, 2]), ALU.mult)
            vec.tensor_tensor(small[:, 24:25], w1b1[:, 1:2], w1b1[:, 1:2], ALU.mult).then_inc(S("tw_prep"), 1)
            dve.wait_ge(S("tw_prep_ps"), 2)
            link(vec.tensor_copy(small[:, 25:28], side[:, 8:11]))
            link(vec.tensor_scalar(small[:, 28:29], small[:, 26:27], 2.0, None, ALU.mult))
            vec.tensor_tensor(small[:, 29:31], w1b1, lnw.to_broadcast([P, 2]), ALU.mult)
            vec.tensor_copy(small[:, 31:32], small[:, 19:20]).then_inc(S("tw_prep"), 1)
            dve.wait_ge(S("tw_prep_ps"), 3)
            link(vec.memset(taln, 0.0))
            link(vec.tensor_copy(taln[0:3, :], side[0:3, 128:256]))
            dve.wait_ge(S("ew_in"), 48)
            link(vec.tensor_tensor(edgew[:, 0:2 * D], edgew[:, 0:2 * D], edgew[:, 2 * D:4 * D], ALU.mult))
            vec.tensor_reduce(attw[:], cut(edgew[:, 0:2 * D], C), AX, ALU.add).then_inc(S("tw_prep"), 1)
            link(vec.tensor_scalar(t_var, t_time, small[:, 25:26], small[:, 28:29], ALU.mult, ALU.add))
            link(vec.tensor_tensor(t_var, t_var, t_time, ALU.mult))
            vec.tensor_scalar(t_var, t_var, small[:, 27:28], 0.0, ALU.add, ALU.max).then_inc(S("tw_prep"), 1)
            dve.wait_ge(S("tw_std"), 1)
            vec.memset(t_one, 1.0)
            link(vec.reciprocal(t_r, t_std))
            vec.tensor_tensor(t_tr, t_time, t_r, ALU.mult).then_inc(S("tw_prep"), 1)

            def tw_relu(i, s, q):
                n = i * (2 * TW_STEPS) + (s * TW_STEPS + q)
                dve.wait_ge(S("tw1"), n + (2 * TW_STEPS + 1))
                dve.wait_ge(S("tw2"), n + 1)
                vec.tensor_scalar(tw_act[:, q * TW_COLS:(q + 1) * TW_COLS],
                                  ps[:, (q % 2) * 512:(q % 2) * 512 + TW_COLS], 0.0, None, ALU.max).then_inc(S("tw_relu"), 1)

            def tw_copy(i, s):
                hold(dve, S("tw3"), i * 2 + (s + 2))
                vec.tensor_copy(ae[:, bass.ds((i * 2 + s) * (ZR * 8), ZR * 8)],
                                ps[:, (4 + s) * 512:(4 + s) * 512 + ZR * 8]).then_inc(S("tw_copied"), 1)

            def tw_turns(i, first, z_turn):
                for s in range(2):
                    z_turn(i, s, first)
                    tw_relu(i, s, 0)
                    tw_relu(i, s, 1)
                    if s == 1:
                        tw_copy(i, 0)
                    elif not first:
                        tw_copy(i - 1, 1)
                    tw_relu(i, s, 2)
                    tw_relu(i, s, 3)

            scans = [0]

            def across(dst, k, penal, op0, op1, init):
                scans[0] += 1
                n = scans[0]
                link(vec.memset(carry[:, 0:1], init))
                vec.tensor_copy(small[:, 32:32 + k], dst[:, RUN - 1, 0:k]).then_inc(S("scan_last"), 1)
                dve.wait_ge(S("scan_lastT"), n)
                vec.tensor_tensor_scan(carry[0:k, 1:P + 1], keepT[0:k, (P if penal else 0):(2 * P if penal else P)],
                                       side[0:k, 0:P], init, op0, op1).then_inc(S("scan_carry"), 1)
                dve.wait_ge(S("scan_carryT"), n)
                link(vec.tensor_copy(carry_in[:, 0:k], side[:, 256:256 + k]))
                for h in range(k):
                    last = vec.scalar_tensor_tensor(dst[:, :, h], pen_still if penal else still[:],
                                                    carry_in[:, h:h + 1], dst[:, :, h], op0, op1)
                return last

            def run_ae():
                vec.memset(fillw, 0.0).then_inc(S("fill_zero"), 1)
                dve.wait_ge(S("seg_zeroed"), 16)
                for h in range(8):
                    last = vec.tensor_tensor_scan(fill_v[:, :, h], keep[:], ae_v[:, :, h], 0.0, ALU.mult, ALU.add)
                link(last)
                across(fill_v, 8, False, ALU.mult, ALU.add, 0.0).then_inc(S("run8"), 1)

            def zhots(i, k, s):
                dve.wait_ge(S("zhot_ps"), k + 1)
                for j in range(ZR):
                    last = vec.tensor_scalar(zhot[:, (s * ZR + j) * P:(s * ZR + j + 1) * P], iota16,
                                             src_low[:, bass.ds(k * ZR + j, 1)], None, ALU.is_equal)
                last.then_inc(S("zhot"), 1)

            def select(i, k, s):
                vec.tensor_tensor(cut(zmask, BUCKETS), iota[:, 0:BUCKETS].unsqueeze(1).to_broadcast([P, ZR, BUCKETS]),
                                  wide(src_high[:, bass.ds(k * ZR, ZR)], BUCKETS), ALU.is_equal).then_inc(S("zmask"), 1)
                dve.wait_ge(S("z_ps"), k + 3)
                dve.wait_ge(S("zmask"), k + 1)
                for a in range(0, ZR, 5):
                    b = min(a + 5, ZR)
                    last = vec.tensor_tensor(cut(zprod[:, a * 100:b * 100], 4), cut(z_candidates(a, b), 4),
                                             wide(zmask[:, a * BUCKETS:b * BUCKETS], 4), ALU.mult)
                last.then_inc(S("z_masked"), 1)
                dve.wait_ge(S("z_masked"), k + 2)
                dve.wait_ge(S("z_taken"), k + ZTURNS)
                vec.tensor_reduce(cut(zsum, 4), zprod.rearrange("p (j s h) -> p j h s", j=ZR, h=4), AX,
                                  ALU.add).then_inc(S("z_sum"), 1)
                hold(dve, S("z_sum"), k + 1)
                vec.tensor_copy(z[:, bass.ds(k * (ZR * 4), ZR * 4)], zsum).then_inc(S("z_taken"), 1)

            def find_sources(asrc):
                dve.wait_ge(S("table_rows"), 3)
                link(vec.tensor_scalar(src_low.bitcast(I32), src_scan[:], 7, None, ALU.arith_shift_right))
                link(vec.tensor_copy(src_high, src_low.bitcast(I32)))
                link(vec.tensor_copy(src_low, src_scan[:]))
                link(vec.scalar_tensor_tensor(src_low, src_high, -float(P), src_low, ALU.mult, ALU.add))
                rest_v = cut(zrest, 4)
                parts = [ztab[:, i * 100:(i + 1) * 100] for i in range(3)]
                link(vec.tensor_copy(cut(parts[0], 4), asrc))
                link(vec.tensor_tensor(rest_v, asrc, cut(parts[0], 4), ALU.subtract))
                link(vec.tensor_copy(parts[1], zrest))
                link(vec.tensor_tensor(parts[2], zrest, parts[1], ALU.subtract))
                link(vec.tensor_copy(ident16, ident))
                link(vec.tensor_copy(iota16, iota[:]))
                dve.sem_inc(S("z_masked"), 1)

                def gathered(i, s, take, give):
                    a, b = ZHALF[s]
                    if take:
                        hold(dve, S(f"z_in{s}"), i * (16 * (b - a)) + 16 * ZR * (ZTURNS // 2))
                        vec.tensor_copy(z[:, bass.ds(i * (ZR * 4) + ((ZLOOK - 1) * ZR + a) * 4, (b - a) * 4)],
                                        zring[:, a * 4:b * 4]).then_inc(S("z_gathered"), 1)
                    if give:
                        vec.tensor_copy(idx_ring[:, a:b],
                                        src_scan[:, bass.ds(i * ZR + (ZLOOK * ZR + a), b - a)]).then_inc(S("zidx_ready"), 1)

                z_steps(dve, [(zhots, 0), (select, 2)], 2, gathered)
                dve.wait_ge(S("z_gathered"), 2 * (ZTURNS - ZLOOK))

            norm([(G[0], G[2]), (G[1], G[3])], 4)
            vec.tensor_scalar(G[0], G[0], v["lnwa"], v["lnba"], ALU.mult, ALU.add)
            vec.tensor_scalar(G[1], G[1], v["lnwb"], v["lnbb"], ALU.mult, ALU.add).then_inc(S("ip_norm"), 1)
            dve.wait_ge(S("lin"), 9)
            vec.tensor_scalar(G[0], acc, v["ipb2"], None, ALU.add).then_inc(S("norm_in"), 1)
            norm([(G[0], G[2])], 5)
            link(vec.tensor_scalar(G[0], G[0], v["pnw"], v["pnb"], ALU.mult, ALU.add))
            link(vec.tensor_copy(G[3], G[5]))
            vec.tensor_scalar(G[0], G[0], 0.0, 10.0, ALU.max, ALU.min).then_inc(S("gat_in"), 1)
            for g in range(2):
                a8v, loop8 = cut(a8, 8), cut(aeloop8, 8)
                asrc, adst, aloop = a8v[:, :, 0:4], a8v[:, :, 4:8], loop8[:, :, 4 * g:4 * g + 4]
                dve.wait_ge(S("a8_ps"), g + 1)
                vec.tensor_copy(a8, side[:, 0:8 * BUCKETS]).then_inc(S("a8"), 1)
                dve.wait_ge(S("a8"), g + 1)

                def z_take(i, s):
                    hold(dve, S(f"z_in{s}"), i * (16 * ZR) + 16 * ZR * (g * (ZTURNS // 2) + 1))
                    vec.tensor_copy(z[:, bass.ds((i * 2 + s) * (ZR * 4), ZR * 4)],
                                    zring[:, s * ZR * 4:(s + 1) * ZR * 4]).then_inc(S("z_taken"), 1)

                def z_index(i, s):
                    vec.tensor_copy(idx_ring[:, s * ZR:(s + 1) * ZR],
                                    src_scan[:, bass.ds((i * 2 + s) * ZR, ZR)]).then_inc(S("zidx_ready"), 1)

                def z_turn(i, s, first=False):
                    if not first:
                        z_take(i - 1, s)
                    z_index(i, s)

                if g == 0:
                    dve.wait_ge(S("table_rows"), 2)
                    vec.memset(tw_ring, 0.0)
                    dve.sem_inc(S("tw_relu"), 2)
                    dve.sem_inc(S("tw_copied"), 2)
                    tw_turns(0, True, z_turn)
                    with dve.Fori(1, ZTURNS // 2) as i:
                        tw_turns(i, False, z_turn)
                    tw_copy(ZTURNS // 2 - 1, 1)
                    dve.wait_ge(S("tw_copied"), ZTURNS + 2)
                    for s in range(2):
                        z_take(ZTURNS // 2 - 1, s)
                else:
                    find_sources(asrc)
                dve.wait_ge(S("z_taken"), ZTURNS + g * ZLOOK)
                if g == 0:
                    run_ae()
                link(vec.tensor_tensor(z_v, z_v, ae_v[:, :, 4 * g:4 * g + 4], ALU.add))
                link(vec.tensor_scalar(pen_keep, keep[:], 1.0, BIG, ALU.subtract, ALU.mult))
                link(vec.tensor_scalar(pen_still, still[:], 1.0, BIG, ALU.subtract, ALU.mult))
                for h in range(4):
                    last = vec.tensor_tensor_scan(run_v[:, :, h], pen_keep, z_v[:, :, h], -BIG, ALU.add, ALU.max)
                link(last)
                across(run_v, 4, True, ALU.add, ALU.max, -BIG).then_inc(S("runmax"), 1)
                zm, pl, sg, amv = cut(zmax, 4), cut(ploop, 4), cut(sseg, 4), cut(am, 8)
                link(vec.tensor_scalar(cnt, has, 1.0, BIG, ALU.subtract, ALU.mult))
                if g == 0:
                    dve.wait_ge(S("aeloop_rows"), 16 * BUCKETS)
                    link(vec.tensor_tensor(cut(aeloop8, 8), cut(aeloop8, 8), wide(invdeg, 8), ALU.mult))
                    link(vec.tensor_tensor(cut(aeloop8, 8), cut(aeloop8, 8), wide(has, 8), ALU.mult))
                dve.wait_ge(S("zmax_rows"), 16 * BUCKETS * (g + 1))
                link(vec.tensor_tensor(zm, zm, wide(has, 4), ALU.mult))
                link(vec.tensor_tensor(zm, zm, wide(cnt, 4), ALU.add))
                link(vec.tensor_tensor(pl, asrc, aloop, ALU.add))
                link(vec.tensor_tensor(zm, zm, pl, ALU.max))
                link(vec.tensor_tensor(zm, zm, adst, ALU.add))
                link(vec.tensor_tensor(pl, pl, adst, ALU.add))
                link(vec.tensor_copy(amv[:, :, 0:4], adst))
                vec.scalar_tensor_tensor(amv[:, :, 4:8], zm, 0.2, zm, ALU.mult, ALU.max).then_inc(S("am"), 1)
                dve.wait_ge(S("am"), g + 1)
                link(vec.scalar_tensor_tensor(pl, pl, 0.2, pl, ALU.mult, ALU.max))
                vec.tensor_tensor(pl, pl, amv[:, :, 4:8], ALU.subtract).then_inc(S("lp"), 1)
                dve.wait_ge(S("seg_in"), 16 * (g + 1))
                for h in range(8):
                    last = vec.tensor_tensor_scan(fill_v[:, :, h], keep[:], fill_v[:, :, h], 0.0, ALU.mult, ALU.add)
                link(last)
                link(across(fill_v, 8, False, ALU.mult, ALU.add, 0.0))
                link(vec.tensor_tensor(z_v, z_v, fill_v[:, :, 0:4], ALU.add))
                link(vec.scalar_tensor_tensor(z, z, 0.2, z, ALU.mult, ALU.max))
                link(vec.tensor_tensor(z_v, z_v, fill_v[:, :, 4:8], ALU.subtract))
                vec.tensor_scalar(z, z, 0.0, None, ALU.min).then_inc(S("alpha"), 1)
                dve.wait_ge(S("prob"), g + 1)
                dve.wait_ge(S("runmax_out"), 16 * (g + 1))
                for h in range(4):
                    last = vec.tensor_tensor_scan(run_v[:, :, h], keep[:], z_v[:, :, h], 0.0, ALU.mult, ALU.add)
                link(last)
                across(run_v, 4, False, ALU.mult, ALU.add, 0.0).then_inc(S("runsum"), 1)
                dve.wait_ge(S("pT_ps"), g + 1)
                item_columns(pT, "pT", g + 1)
                weighted_pass(1 + g, g)
                dve.wait_ge(S("sseg_rows"), 16 * BUCKETS * (g + 1))
                dve.wait_ge(S("ploop"), g + 1)
                link(vec.tensor_tensor(sg, sg, wide(has, 4), ALU.mult))
                link(vec.tensor_tensor(sg, sg, pl, ALU.add))
                link(vec.tensor_scalar(sseg, sseg, 1e-16, None, ALU.add))
                link(vec.reciprocal(rs, sseg))
                link(vec.tensor_tensor(cut(G[2], C), cut(G[4], C), wide(ploop, C), ALU.mult))
                link(vec.tensor_tensor(G[2], G[2], acc1, ALU.add))
                vec.tensor_tensor(cut(G[2], C), cut(G[2], C), wide(rs, C), ALU.mult).then_inc(S("gat_rows"), 1)
                dve.wait_ge(S("gatT"), g + 1)
                link(vec.scalar_tensor_tensor(G[0], acc, v[f"g{g + 1}b"], G[0], ALU.add, ALU.add))
                vec.tensor_scalar(G[0], G[0], 10.0, -10.0, ALU.min, ALU.max).then_inc(S("norm_in"), 1)
                norm([(G[0], G[2])], 6 + g)
                link(vec.tensor_scalar(G[0], G[0], v[f"n{g + 1}w"], v[f"n{g + 1}b"], ALU.mult, ALU.add))
                vec.tensor_scalar(G[2], G[0], 0.0, None, ALU.min).then_inc(S("elu_min"), 1)
                dve.wait_ge(S("elu_exp"), g + 1)
                link(vec.scalar_tensor_tensor(G[0], G[0], 0.0, G[2], ALU.max, ALU.add))
                if g == 0:
                    vec.tensor_scalar(G[0], G[0], 1.0, None, ALU.subtract).then_inc(S("gat_in"), 1)
                    dve.wait_ge(S("gat_in"), 2)
            vec.scalar_tensor_tensor(G[0], G[0], 1.0, G[3], ALU.subtract, ALU.add).then_inc(S("norm_in"), 1)
            norm([(G[0], G[2])], 8, "layer_done")


def layouts(x):
    def pad(a, *shape):
        out = np.zeros(shape, a.dtype)
        out[tuple(slice(0, n) for n in a.shape)] = a
        return out

    dst = np.full(EP + 1, NP, np.int32)
    dst[0] = -1
    dst[1:E + 1] = x["dst"]
    src = pad(x["src"], EP)
    w2 = "L2_gnn_W_"

    def blocks(w0, w1, rows0, rows1, cols0, cols1):
        out = np.zeros((P, P), np.float32)
        out[np.ix_(rows0, cols0)] = w0
        for c in range(3):
            out[np.ix_(rows1[c], cols1[c])] = w1
        return out

    u = np.arange(MUL)
    mixed = [MUL + 3 * u + c for c in range(3)]
    split = [MUL + MUL * c + u for c in range(3)]
    wl1 = x[w2 + "l2_1"]
    wl2a, wl2b = np.zeros((P, P), np.float32), np.zeros((P, P), np.float32)
    wl2a[np.ix_(np.arange(2 * MUL), u)] = x[w2 + "l2_0"]
    for c in range(3):
        at, to = (wl2a, 2 * MUL + MUL * c) if c < 2 else (wl2b, 0)
        at[np.ix_(to + u, mixed[c])] = wl1[:MUL]
        wl2b[np.ix_(MUL + MUL * c + u, mixed[c])] = wl1[MUL:]
    walpha = np.zeros((P, P), np.float32)
    walpha[:2 * MUL, :] = x[w2 + "alpha"]
    mats = {
        "wn1": x["L0_gnn_W_neigh1"].T, "ws1": x["L0_gnn_W_self1"].T,
        "wn2": x["L0_gnn_W_neigh2"].T, "ws2": x["L0_gnn_W_self2"].T,
        "wy": blocks(x[w2 + "l1_0"], x[w2 + "l1_1"], u, mixed, u, split),
        "wsc": blocks(x[w2 + "sc0"], x[w2 + "sc1"], u, mixed, u, mixed),
        "wl2a": wl2a, "wl2b": wl2b, "walpha": walpha, "wfc2": pad(x[w2 + "fc2"].reshape(100, 4, MUL)[:, [0, 3, 1, 2]].reshape(100, P), P, P),
        "ipw1a": x["L3_gnn_ip_w1"][:, :P], "ipw1b": x["L3_gnn_ip_w1"][:, P:],
        "ipw2a": x["L3_gnn_ip_w2"][:P], "ipw2b": x["L3_gnn_ip_w2"][P:],
        "taw2": x["L3_gnn_ta_w2"], "gw0": x["L3_gnn_g1_w"], "gw1": x["L3_gnn_g2_w"], "ident": np.eye(P, dtype=np.float32),
    }
    for k in range(4):
        mats[f"gcn{k}"] = pad(x[f"L1_gnn_W{k + 1}"], P, P)
    vecs = {
        "bn1": x["L0_gnn_b_neigh1"], "bs1": x["L0_gnn_b_self1"], "bn2": x["L0_gnn_b_neigh2"], "bs2": x["L0_gnn_b_self2"],
        "ipb1a": x["L3_gnn_ip_b1"][:P], "ipb1b": x["L3_gnn_ip_b1"][P:], "lnwa": x["L3_gnn_ip_ln_w"][:P],
        "lnwb": x["L3_gnn_ip_ln_w"][P:], "lnba": x["L3_gnn_ip_ln_b"][:P], "lnbb": x["L3_gnn_ip_ln_b"][P:],
        "ipb2": x["L3_gnn_ip_b2"], "pnw": x["L3_gnn_pn_w"], "pnb": x["L3_gnn_pn_b"], "tab2": x["L3_gnn_ta_b2"],
        "g1b": x["L3_gnn_g1_b"], "g2b": x["L3_gnn_g2_b"], "n1w": x["L3_gnn_n1_w"], "n1b": x["L3_gnn_n1_b"],
        "n2w": x["L3_gnn_n2_w"], "n2b": x["L3_gnn_n2_b"],
    }
    for k in range(4):
        vecs[f"gb{k}"] = pad(x[f"L1_gnn_b{k + 1}"], P)
    att = np.zeros((P, 16), np.float32)
    for g in range(2):
        for j, name in enumerate(("src", "dst")):
            for h in range(HEADS):
                att[h * C:(h + 1) * C, 8 * g + 4 * j + h] = x[f"L3_gnn_g{g + 1}_att_{name}"][h]
    return {
        "xT": pad(x["x"], NP, D).T,
        "dst_ext": dst, "dst_rows": dst[1:].reshape(TILES, P), "dst_first": dst[1::P],
        "src_rows": src.reshape(TILES, P),
        "ea4_rows": pad(x["edge_attr_4"], EP, 4).reshape(TILES, 4 * P),
        "ea10T": np.concatenate([np.zeros((10, P), np.float32), pad(x["edge_attr_10"], EP + GROUP * P, 10).T], axis=1),
        "ew_jp": pad(x["edge_weight"], EP).reshape(P, RUN).T.reshape(-1),
        "attr": pad(x["node_vec1"], NP, 1).T,
        "weights": np.concatenate([mats[n] for n in WEIGHTS], axis=1),
        "vectors": np.stack([vecs[n] for n in VECS], axis=1),
        "wfc1": pad(x[w2 + "fc1"], P, 100), "att": att,
        "edgew": np.concatenate([x["L3_gnn_g1_ew"], x["L3_gnn_g2_ew"]], axis=1),
        "att_edge": np.concatenate([x["L3_gnn_g1_att_edge"].reshape(1, D), x["L3_gnn_g2_att_edge"].reshape(1, D)], axis=1),
        "ta_cols": np.stack([x["L3_gnn_ta_w1"][0], x["L3_gnn_ta_b1"], x["L3_gnn_ta_ln_w"], x["L3_gnn_ta_ln_b"]], axis=1),
    }


def kernel(**inputs):
    import concourse.bacc as bacc
    from concourse.bass_utils import run_bass_kernel_spmd

    arrays = {k: np.ascontiguousarray(a) for k, a in layouts({k: np.asarray(a) for k, a in inputs.items()}).items()}
    nc = bacc.Bacc("TRN2", target_bir_lowering=False, num_devices=1)
    io = {k: nc.dram_tensor(f"in_{k}", a.shape, mybir.dt.from_np(a.dtype), kind="ExternalInput").ap()
          for k, a in arrays.items()}
    out = nc.dram_tensor("out", [NP, D], F32, kind="ExternalOutput").ap()
    gnn_kernel(nc, io, out)
    r = run_bass_kernel_spmd(nc, [{f"in_{k}": a for k, a in arrays.items()}], core_ids=[0])
    return r.results[0]["out"][:N]
```
